# Optimizing a Trainium2 kernel written in Bass

```python
import numpy as np
import jax
import jax.numpy as jnp

def _softmax(x, axis=-1):
    return jax.nn.softmax(x, axis=axis)

def _gelu(x):
    return jax.nn.gelu(x, approximate=True)

def _silu(x):
    return jax.nn.silu(x)

def _sigmoid(x):
    return jax.nn.sigmoid(x)

def _layernorm(x, axis=-1, eps=1e-05):
    m = jnp.mean(x, axis=axis, keepdims=True)
    v = jnp.var(x, axis=axis, keepdims=True)
    return (x - m) / jnp.sqrt(v + eps)

def _scatter_add(tgt, idx, src, axis=0):
    return tgt.at[idx].add(src)

def _segment_sum(src, seg, n):
    return jax.ops.segment_sum(src, seg, n)
kernel_name = 'mk_decoder_preln_d1_seqx_r4_e53241'

def setup_inputs(seed: int=0):
    np.random.seed(seed)
    _w = jnp.asarray

    def _rec_inputs():
        import jax
        import jax.numpy as jnp
        _rk = jax.random.key(seed)
        x = -0.0002928 + 1 * jax.random.normal(jax.random.fold_in(_rk, 1), (8, 512, 256), jnp.float32)
        _lenS = 512 - jax.random.randint(jax.random.fold_in(_rk, 7), (8,), 0, max(1, 512 // 4) + 1, jnp.int32)
        _lenS2 = 1601 - jax.random.randint(jax.random.fold_in(_rk, 8), (8,), 0, max(1, 1601 // 4) + 1, jnp.int32)
        _ctx_1024P = jax.random.normal(jax.random.fold_in(_rk, 11), (8, 16, 256), jnp.float32)
        _ctx_1024c = jax.random.dirichlet(jax.random.fold_in(_rk, 511), 0.3 * jnp.ones((16,), jnp.float32), (8, 1601))
        _ctx_1024t = jnp.einsum('bsk,bkd->bsd', _ctx_1024c, _ctx_1024P)
        _ctx_1024t = _ctx_1024t * jax.lax.rsqrt(jnp.mean(jnp.square(_ctx_1024t)) + 1e-12) * 0.953939
        ctx_1024 = -0.000191848 + 0.999787 * (_ctx_1024t + 0.3 * jax.random.normal(jax.random.fold_in(_rk, 611), (8, 1601, 256), jnp.float32))
        return (x, ctx_1024)
    x, ctx_1024 = _rec_inputs()

    def _L0_attn_setup():
        import jax, jax.numpy as jnp
        import numpy as np
        B, T, C, NH = (8, 256, 256, 16)
        HD = C // NH
        EPS = 1e-05

        def _decay_mask(nh, t, dtype):
            gamma = 1.0 - 2.0 ** (-5.0 - jnp.arange(nh, dtype=jnp.float32))
            idx = jnp.arange(t)
            diff = idx[:, None] - idx[None, :]
            mask = diff >= 0
            pow_ = gamma[:, None, None] ** jnp.where(mask, diff, 0).astype(jnp.float32)
            return (jnp.where(mask[None], pow_, 0.0).astype(dtype), gamma.astype(dtype))

        def _reference_tuple_inner(x, past_kv, W_qkv, gn_weight, gn_bias):
            b, t, c = x.shape
            nh = gn_weight.shape[0]
            hd = c // nh
            qkv = x @ W_qkv
            q, k, v = jnp.split(qkv, 3, axis=2)
            split_heads = lambda u: u.reshape(b, t, nh, hd).transpose(0, 2, 1, 3)
            q, k, v = (split_heads(q), split_heads(k), split_heads(v))
            decay, gamma = _decay_mask(nh, t, x.dtype)
            ret = jnp.einsum('bhtd,bhsd->bhts', q, k) * decay
            inner = jnp.einsum('bhts,bhsd->bhtd', ret, v)
            inner_decay = float(nh * hd)
            cross = jnp.einsum('bhtd,hde->bhte', q, past_kv) * inner_decay
            r = inner + cross
            current_kv = gamma[:, None, None] * past_kv + jnp.einsum('bhtd,bhte->bhde', k, v)
            current_kv = current_kv.mean(axis=0)
            y = r.transpose(0, 1, 3, 2)
            mu = y.mean(axis=(1, 2, 3), keepdims=True)
            var = y.var(axis=(1, 2, 3), keepdims=True)
            yn = (y - mu) * jax.lax.rsqrt(var + EPS)
            yn = yn * gn_weight[None, :, None, None] + gn_bias[None, :, None, None]
            out = yn.transpose(0, 3, 1, 2).reshape(b, t, c)
            return (out, current_kv)
        key = jax.random.key(seed)
        k1, k2, k3 = jax.random.split(key, 3)
        x = jax.random.normal(k1, (B, T, C), dtype=jnp.float32)
        past_kv = jax.random.normal(k2, (NH, HD, HD), dtype=jnp.float32) * 0.1
        W_qkv = jax.random.normal(k3, (C, 3 * C), dtype=jnp.float32) * 0.02
        gn_weight = jnp.ones((NH,), dtype=jnp.float32)
        gn_bias = jnp.zeros((NH,), dtype=jnp.float32)
        return {'x': x, 'past_kv': past_kv, 'W_qkv': W_qkv, 'gn_weight': gn_weight, 'gn_bias': gn_bias}
    _L0_attn_all = _L0_attn_setup()
    _L0_attn_in = {k: v for k, v in _L0_attn_all.items() if k in ('past_kv', 'W_qkv', 'gn_weight', 'gn_bias')}
    del _L0_attn_all

    def _L0_xattn_setup():
        import jax, jax.numpy as jnp
        import numpy as np
        D_MODEL = 256
        NUM_HEADS = 16
        DEPTH = D_MODEL // NUM_HEADS
        key = jax.random.key(seed)
        ks = jax.random.split(key, 10)
        B, T, C = (2, 512, 768)
        s = 1.0 / np.sqrt(D_MODEL)
        inp = {'x': jax.random.normal(ks[0], (B, T, D_MODEL), dtype=jnp.float32), 'context': jax.random.normal(ks[1], (B, C, D_MODEL), dtype=jnp.float32), 'Wq': jax.random.normal(ks[2], (D_MODEL, D_MODEL), dtype=jnp.float32) * s, 'bq': jnp.zeros((D_MODEL,), dtype=jnp.float32), 'Wk': jax.random.normal(ks[3], (D_MODEL, D_MODEL), dtype=jnp.float32) * s, 'bk': jnp.zeros((D_MODEL,), dtype=jnp.float32), 'Wv': jax.random.normal(ks[4], (D_MODEL, D_MODEL), dtype=jnp.float32) * s, 'bv': jnp.zeros((D_MODEL,), dtype=jnp.float32), 'Wo': jax.random.normal(ks[5], (D_MODEL, D_MODEL), dtype=jnp.float32) * s, 'bo': jnp.zeros((D_MODEL,), dtype=jnp.float32)}
        return inp
    _L0_xattn_all = _L0_xattn_setup()
    _L0_xattn_in = {k: v for k, v in _L0_xattn_all.items() if k in ('Wq', 'bq', 'Wk', 'bk', 'Wv', 'bv', 'Wo', 'bo')}
    del _L0_xattn_all

    def _L0_ffn_setup():
        import jax, jax.numpy as jnp
        import numpy as np
        H = 256
        I = 128
        E = 8
        K = 2
        SI = I * 2
        B, S = (2, 256)

        def _mlp(x, gw, uw, dw):
            return jax.nn.silu(x @ gw.T) * (x @ uw.T) @ dw.T
        key = jax.random.key(seed)
        ks = jax.random.split(key, 9)
        s = 0.02
        return {'x': jax.random.normal(ks[0], (B, S, H), jnp.float32), 'gate_w': jax.random.normal(ks[1], (E, H), jnp.float32) * s, 'lb_bias': jnp.zeros((E,), jnp.float32), 'expert_gate_w': jax.random.normal(ks[2], (E, I, H), jnp.float32) * s, 'expert_up_w': jax.random.normal(ks[3], (E, I, H), jnp.float32) * s, 'expert_down_w': jax.random.normal(ks[4], (E, H, I), jnp.float32) * s, 'shared_gate_w': jax.random.normal(ks[5], (SI, H), jnp.float32) * s, 'shared_up_w': jax.random.normal(ks[6], (SI, H), jnp.float32) * s, 'shared_down_w': jax.random.normal(ks[7], (H, SI), jnp.float32) * s}
    _L0_ffn_all = _L0_ffn_setup()
    _L0_ffn_in = {k: v for k, v in _L0_ffn_all.items() if k in ('gate_w', 'lb_bias', 'expert_gate_w', 'expert_up_w', 'expert_down_w', 'shared_gate_w', 'shared_up_w', 'shared_down_w')}
    del _L0_ffn_all
    return {'x': x, 'ctx_1024': ctx_1024, 'L0_attn_past_kv': _L0_attn_in['past_kv'], 'L0_attn_W_qkv': _L0_attn_in['W_qkv'], 'L0_attn_gn_weight': _L0_attn_in['gn_weight'], 'L0_attn_gn_bias': _L0_attn_in['gn_bias'], 'L0_xattn_Wq': _L0_xattn_in['Wq'], 'L0_xattn_bq': _L0_xattn_in['bq'], 'L0_xattn_Wk': _L0_xattn_in['Wk'], 'L0_xattn_bk': _L0_xattn_in['bk'], 'L0_xattn_Wv': _L0_xattn_in['Wv'], 'L0_xattn_bv': _L0_xattn_in['bv'], 'L0_xattn_Wo': _L0_xattn_in['Wo'], 'L0_xattn_bo': _L0_xattn_in['bo'], 'L0_ffn_gate_w': _L0_ffn_in['gate_w'], 'L0_ffn_lb_bias': _L0_ffn_in['lb_bias'], 'L0_ffn_expert_gate_w': _L0_ffn_in['expert_gate_w'], 'L0_ffn_expert_up_w': _L0_ffn_in['expert_up_w'], 'L0_ffn_expert_down_w': _L0_ffn_in['expert_down_w'], 'L0_ffn_shared_gate_w': _L0_ffn_in['shared_gate_w'], 'L0_ffn_shared_up_w': _L0_ffn_in['shared_up_w'], 'L0_ffn_shared_down_w': _L0_ffn_in['shared_down_w']}

def reference(x, ctx_1024, L0_attn_past_kv, L0_attn_W_qkv, L0_attn_gn_weight, L0_attn_gn_bias, L0_xattn_Wq, L0_xattn_bq, L0_xattn_Wk, L0_xattn_bk, L0_xattn_Wv, L0_xattn_bv, L0_xattn_Wo, L0_xattn_bo, L0_ffn_gate_w, L0_ffn_lb_bias, L0_ffn_expert_gate_w, L0_ffn_expert_up_w, L0_ffn_expert_down_w, L0_ffn_shared_gate_w, L0_ffn_shared_up_w, L0_ffn_shared_down_w):
    import jax
    import jax.numpy as jnp

    def _L0_attn_ref(x, past_kv, W_qkv, gn_weight, gn_bias):
        import jax, jax.numpy as jnp
        import numpy as np
        B, T, C, NH = (8, 256, 256, 16)
        HD = C // NH
        EPS = 1e-05

        def _decay_mask(nh, t, dtype):
            gamma = 1.0 - 2.0 ** (-5.0 - jnp.arange(nh, dtype=jnp.float32))
            idx = jnp.arange(t)
            diff = idx[:, None] - idx[None, :]
            mask = diff >= 0
            pow_ = gamma[:, None, None] ** jnp.where(mask, diff, 0).astype(jnp.float32)
            return (jnp.where(mask[None], pow_, 0.0).astype(dtype), gamma.astype(dtype))

        def _reference_tuple_inner(x, past_kv, W_qkv, gn_weight, gn_bias):
            b, t, c = x.shape
            nh = gn_weight.shape[0]
            hd = c // nh
            qkv = x @ W_qkv
            q, k, v = jnp.split(qkv, 3, axis=2)
            split_heads = lambda u: u.reshape(b, t, nh, hd).transpose(0, 2, 1, 3)
            q, k, v = (split_heads(q), split_heads(k), split_heads(v))
            decay, gamma = _decay_mask(nh, t, x.dtype)
            ret = jnp.einsum('bhtd,bhsd->bhts', q, k) * decay
            inner = jnp.einsum('bhts,bhsd->bhtd', ret, v)
            inner_decay = float(nh * hd)
            cross = jnp.einsum('bhtd,hde->bhte', q, past_kv) * inner_decay
            r = inner + cross
            current_kv = gamma[:, None, None] * past_kv + jnp.einsum('bhtd,bhte->bhde', k, v)
            current_kv = current_kv.mean(axis=0)
            y = r.transpose(0, 1, 3, 2)
            mu = y.mean(axis=(1, 2, 3), keepdims=True)
            var = y.var(axis=(1, 2, 3), keepdims=True)
            yn = (y - mu) * jax.lax.rsqrt(var + EPS)
            yn = yn * gn_weight[None, :, None, None] + gn_bias[None, :, None, None]
            out = yn.transpose(0, 3, 1, 2).reshape(b, t, c)
            return (out, current_kv)
        return _reference_tuple_inner(x, past_kv, W_qkv, gn_weight, gn_bias)[0]

    def _L0_xattn_ref(x, context, Wq, bq, Wk, bk, Wv, bv, Wo, bo):
        import jax, jax.numpy as jnp
        import numpy as np
        D_MODEL = 256
        NUM_HEADS = 16
        DEPTH = D_MODEL // NUM_HEADS
        B, T, D = x.shape
        C = context.shape[1]
        H, d = (NUM_HEADS, DEPTH)
        q = x @ Wq.T + bq
        k = context @ Wk.T + bk
        v = context @ Wv.T + bv
        q = q.reshape(B, T, H, d).transpose(0, 2, 1, 3)
        k = k.reshape(B, C, H, d).transpose(0, 2, 1, 3)
        v = v.reshape(B, C, H, d).transpose(0, 2, 1, 3)
        scores = jnp.einsum('bhtd,bhcd->bhtc', q, k) / jnp.sqrt(jnp.asarray(d, x.dtype))
        attn = jax.nn.softmax(scores, axis=-1)
        out = jnp.einsum('bhtc,bhcd->bhtd', attn, v)
        out = out.transpose(0, 2, 1, 3).reshape(B, T, D)
        return out @ Wo.T + bo

    def _L0_ffn_ref(x, gate_w, lb_bias, expert_gate_w, expert_up_w, expert_down_w, shared_gate_w, shared_up_w, shared_down_w):
        import jax, jax.numpy as jnp
        import numpy as np
        H = 256
        I = 128
        E = 8
        K = 2
        SI = I * 2
        B, S = (2, 256)

        def _mlp(x, gw, uw, dw):
            return jax.nn.silu(x @ gw.T) * (x @ uw.T) @ dw.T
        b, s, h = x.shape
        xf = x.reshape(-1, h)
        logits = xf @ gate_w.T + lb_bias
        scores = jax.nn.sigmoid(logits.astype(jnp.float32))
        topw, topi = jax.lax.top_k(scores, K)
        topw = (topw / (topw.sum(-1, keepdims=True) + 1e-08)).astype(x.dtype)
        out = jnp.zeros_like(xf)
        for e in range(E):
            m = topi == e
            sel = m.any(axis=-1)
            cnt = m.sum()
            wmean = (topw * m).sum() / jnp.maximum(cnt, 1).astype(topw.dtype)
            y = _mlp(xf, expert_gate_w[e], expert_up_w[e], expert_down_w[e])
            out = out + jnp.where(sel[:, None], y * wmean, jnp.zeros((), x.dtype))
        out = out.reshape(b, s, h)
        out = out + _mlp(x, shared_gate_w, shared_up_w, shared_down_w)
        return out
    x = x + _L0_attn_ref(_layernorm(x, axis=-1), L0_attn_past_kv, L0_attn_W_qkv, L0_attn_gn_weight, L0_attn_gn_bias)
    x = x + _L0_xattn_ref(_layernorm(x, axis=-1), ctx_1024, L0_xattn_Wq, L0_xattn_bq, L0_xattn_Wk, L0_xattn_bk, L0_xattn_Wv, L0_xattn_bv, L0_xattn_Wo, L0_xattn_bo)
    x = x + _L0_ffn_ref(_layernorm(x, axis=-1), L0_ffn_gate_w, L0_ffn_lb_bias, L0_ffn_expert_gate_w, L0_ffn_expert_up_w, L0_ffn_expert_down_w, L0_ffn_shared_gate_w, L0_ffn_shared_up_w, L0_ffn_shared_down_w)
    return x

_drawn_inputs = setup_inputs


def setup_inputs(seed=0):
    import zlib

    import numpy as np

    out = dict(_drawn_inputs(seed))
    spreads = {'L0_attn_gn_weight': (1.0, 0.2),
     'L0_attn_gn_bias': (0.0, 0.1),
     'L0_xattn_bq': (0.0, 0.564),
     'L0_xattn_bk': (0.0, 0.8),
     'L0_xattn_bv': (0.0, 0.1),
     'L0_xattn_bo': (0.0, 0.1),
     'L0_ffn_lb_bias': (0.0, 0.8)}
    factors = {'L0_ffn_gate_w': 8.0,
     'L0_ffn_expert_gate_w': 8.0,
     'L0_ffn_expert_up_w': 8.0,
     'L0_ffn_expert_down_w': 8.0,
     'L0_ffn_shared_gate_w': 5.412,
     'L0_ffn_shared_up_w': 5.309,
     'L0_ffn_shared_down_w': 5.338}
    for name, (base, spread) in spreads.items():
        noise = np.random.default_rng([zlib.crc32(name.encode()), seed]).standard_normal(out[name].shape)
        drawn = base * np.exp(spread * noise) if base else spread * noise
        out[name] = jnp.asarray(drawn.astype(out[name].dtype))
    for name, factor in factors.items():
        out[name] = (out[name] * factor).astype(out[name].dtype)
    return out
```

```python
from contextlib import ExitStack

import numpy as np

import concourse.bass as bass
from concourse import mybir

F32 = mybir.dt.float32
BF16 = mybir.dt.bfloat16
ALU = mybir.AluOpType
ACT = mybir.ActivationFunctionType
AX = mybir.AxisListType

P = 128
B, T, D, H = 8, 512, 256, 16
HD = D // H
TT = T // P
KT = D // P
HT = P // HD
NT = B * TT
S = 1601
SC = -(-S // P)
EPS = 1e-5


def widths(total, step):
    return [min(step, total - i) for i in range(0, total, step)]



R_BANKS = 6
R_ITEMS = 36
R_LINKS = 17


def retention(nc, x_all, ln2, io):
    with ExitStack() as ctx:
        def sb(name, shape, dt=F32):
            return ctx.enter_context(nc.sbuf_tensor(name, shape, dt))

        def sem(name):
            return ctx.enter_context(nc.semaphore(name))

        ps = ctx.enter_context(nc.psum_tensor("r_ps", [P, 8, 512], F32))
        ident = sb("r_ident", [P, P])
        decay = sb("r_decay", [P, H, P])
        qdecay = sb("r_qdecay", [P, KT, P])
        kvscale = sb("r_kvscale", [P, 2 * D])
        headmask = sb("r_headmask", [P, HT])
        blockmask = sb("r_blockmask", [P, P])
        chunkdecay = sb("r_chunkdecay", [P, KT])
        meanw = sb("r_meanw", [P, P])
        wqkv = sb("r_wqkv", [P, KT, 3 * D])
        past = sb("r_past", [P, KT, HD])
        gw = sb("r_gw", [P, D])
        gb = sb("r_gb", [P, D])

        past_bd = sb("r_past_bd", [P, KT, P])
        xn = sb("r_xn", [P, TT, D])
        xnT = sb("r_xnT", [P, KT, T])
        qT = sb("r_qT", [P, KT, T])
        qwide = sb("r_qwide", [P, KT, HT, T])
        qg = sb("r_qg", [P, KT, T])
        kT = sb("r_kT", [P, KT, T])
        kv = sb("r_kv", [P, TT, 2 * D])
        probs = sb("r_probs", [P, 2, H, P])
        state = sb("r_state", [P, TT, KT, P])
        stmp = sb("r_stmp", [P, P])
        r = sb("r_r", [P, TT, D])
        bst = sb("r_bst", [P, TT, 6])
        lmv = sb("r_lmv", [P, TT, 2])
        rbst = sb("r_rbst", [P, TT, 6])
        rmv = sb("r_rmv", [P, 2])
        rs2 = sb("r_rs2", [P, 2])
        gs2 = sb("r_gs2", [P, 2])
        var = sb("r_var", [P, TT])
        carrier = sb("r_carrier", [P, 1])
        std = sb("r_std", [P, TT])
        rstd = sb("r_rstd", [P, TT])
        ga = sb("r_ga", [P, D])
        gbm = sb("r_gbm", [P, D])
        y = sb("r_y", [P, TT, D])

        x_loaded, consts = sem("x_loaded"), sem("r_consts")
        filled, drained = sem("r_filled"), sem("r_drained")
        var_ready, std_ready = sem("var_ready"), sem("std_ready")
        xn_ready, past_ready = sem("xn_ready"), sem("past_ready")
        q_wide, q_decayed = sem("q_wide"), sem("q_decayed")
        stats_ready, stats_filled = sem("stats_ready"), sem("stats_filled")
        affine_ready, x1_ready, y_step = sem("affine_ready"), sem("x1_ready"), sem("y_step")
        link_r = sem("r_link")

        NCONST = 12
        block = ctx.enter_context(nc.Block())

        @block.sync
        def _(sp):
            sp.dma_start(x_all[:, 0:TT, :], io["x"][0].rearrange("(n p) d -> p n d", p=P)).then_inc(x_loaded, 16)
            sp.dma_start(wqkv[:], io["wqkv"].rearrange("(k p) n -> p k n", p=P)).then_inc(consts, 16)
            for t, name in ((ident, "ident"), (kvscale, "kvscale"), (qdecay, "qdecay"), (headmask, "headmask"),
                            (blockmask, "blockmask"), (chunkdecay, "chunkdecay"), (meanw, "meanw"),
                            (decay, "decay"), (past, "past"), (gw, "gw"), (gb, "gb")):
                sp.dma_start(t[:], io[name]).then_inc(consts, 16)
            for b in range(1, B):
                sp.wait_ge(x_loaded, 16 * b)
                sp.dma_start(x_all[:, b * TT:(b + 1) * TT, :],
                             io["x"][b].rearrange("(n p) d -> p n d", p=P)).then_inc(x_loaded, 16)

        @block.tensor
        def _(pe):
            pe.wait_ge(consts, 16 * NCONST)
            pe.wait_ge(past_ready, 1)

            def batch(b):
                k = [0]
                start = b * R_ITEMS

                def bank():
                    if not (isinstance(b, int) and b == 0 and k[0] < R_BANKS):
                        pe.wait_ge(drained, start + (k[0] - R_BANKS + 1))
                    k[0] += 1
                    return (k[0] - 1) % R_BANKS

                pe.wait_ge(xn_ready, b + 1)
                for f in range(KT):
                    o = bank()
                    for t in range(TT):
                        m = pe.transpose(ps[:, o, t * P:(t + 1) * P], xn[:, t, f * P:(f + 1) * P], ident[:])
                    m.then_inc(filled, 1)
                pe.wait_ge(drained, start + KT)
                for part in range(2):
                    for f in range(KT):
                        o = bank()
                        for kk in range(KT):
                            m = pe.matmul(ps[:, o, :], wqkv[:, kk, part * D + f * P:part * D + (f + 1) * P],
                                          xnT[:, kk, :], start=kk == 0, stop=kk == KT - 1)
                        m.then_inc(filled, 1)
                for c in range(TT):
                    o = bank()
                    for kk in range(KT):
                        m = pe.matmul(ps[:, o, :], xnT[:, kk, c * P:(c + 1) * P], wqkv[:, kk, D:3 * D],
                                      start=kk == 0, stop=kk == KT - 1)
                    m.then_inc(filled, 1)
                pe.wait_ge(q_wide, (b + 1) * KT * HT)
                pe.wait_ge(q_decayed, b + 1)

                def scores(c):
                    for f in range(KT):
                        for half in range(2):
                            o = bank()
                            pe.matmul(ps[:, o, :], kT[:, f, c * P:(c + 1) * P],
                                      qwide[:, f, 4 * half:4 * half + 4, c * P:(c + 1) * P],
                                      start=True, stop=True).then_inc(filled, 1)

                def states(c):
                    for f in range(KT):
                        o = bank()
                        pe.matmul(ps[:, o, 0:P], kv[:, c, f * P:(f + 1) * P],
                                  kv[:, c, D + f * P:D + (f + 1) * P], start=True, stop=True).then_inc(filled, 1)

                def output(c):
                    pe.wait_ge(drained, start + probs_item[c])
                    o = bank()
                    for f in range(KT):
                        m = pe.matmul(ps[:, o, f * P:(f + 1) * P], qT[:, f, c * P:(c + 1) * P], past_bd[:, f, :],
                                      start=f == 0, stop=False, skip_group_check=True)
                        if c:
                            pe.matmul(ps[:, o, f * P:(f + 1) * P], qg[:, f, c * P:(c + 1) * P], state[:, c, f, :],
                                      start=False, stop=False, skip_group_check=True)
                    for h in range(H):
                        m = pe.matmul(ps[:, o, h * HD:(h + 1) * HD], probs[:, c % 2, h, :],
                                      kv[:, c, D + h * HD:D + (h + 1) * HD], start=False, stop=h == H - 1,
                                      skip_group_check=True)
                    m.then_inc(filled, 1)

                probs_item = [14, 20, 27, 34]
                pe.wait_ge(drained, start + 10)
                scores(0)
                for c in range(1, TT):
                    scores(c)
                    states(c - 1)
                    output(c - 1)
                output(TT - 1)
                assert k[0] == R_ITEMS
                pe.wait_ge(stats_ready, b + 1)
                pe.matmul(ps[:, R_BANKS, 0:2], meanw[:], rs2[:], start=True, stop=True).then_inc(stats_filled, 1)

            batch(0)
            with pe.Fori(1, B - 1) as b:
                batch(b)
            batch(B - 1)

        @block.scalar
        def _(act):
            def root(n):
                act.wait_ge(var_ready, n)
                nc.scalar.activation(std[:], var[:], ACT.Sqrt).then_inc(std_ready, 1)

            def widen(b):
                act.wait_ge(drained, b * R_ITEMS + 4)
                for f in range(KT):
                    for h in range(HT):
                        nc.scalar.activation(qwide[:, f, h, :], qT[:, f, :], ACT.Copy,
                                             scale=headmask[:, h:h + 1]).then_inc(q_wide, 1)

            root(1)
            act.wait_ge(consts, 16 * NCONST)
            widen(0)
            root(2)
            root(3)
            with act.Fori(1, B - 1) as b:
                widen(b)
                for n in range(3):
                    root(3 * b + n + 1)
            widen(B - 1)
            root(3 * B - 2)
            root(3 * B - 1)
            root(3 * B)

        @block.gpsimd
        def _(pool):
            pool.wait_ge(consts, 16 * NCONST)

            def batch(b):
                pool.wait_ge(drained, b * R_ITEMS + 4)
                qd = qdecay[:].unsqueeze(2).broadcast_to([P, KT, TT, P])
                nc.gpsimd.tensor_tensor(qg[:].rearrange("p k (c t) -> p k c t", c=TT),
                                        qT[:].rearrange("p k (c t) -> p k c t", c=TT), qd,
                                        ALU.mult).then_inc(q_decayed, 1)
                pool.wait_ge(affine_ready, b + 1)
                g3 = ga[:].unsqueeze(1).broadcast_to([P, TT, D])
                b3 = gbm[:].unsqueeze(1).broadcast_to([P, TT, D])
                xb = x_all[:, bass.ts(b, TT), :]
                nc.gpsimd.tensor_tensor(y[:], r[:], g3, ALU.mult).then_inc(y_step, 1)
                pool.wait_ge(y_step, b * 2 + 1)
                nc.gpsimd.tensor_tensor(y[:], y[:], b3, ALU.add).then_inc(y_step, 1)
                pool.wait_ge(y_step, b * 2 + 2)
                nc.gpsimd.tensor_tensor(xb, xb, y[:], ALU.add).then_inc(x1_ready, 1)

            with pool.Fori(0, B) as b:
                batch(b)

        @block.vector
        def _(dve):
            steps = [0]
            base = [0]

            def link(ins):
                steps[0] += 1
                ins.then_inc(link_r, 1)
                dve.wait_ge(link_r, base[0] + steps[0])

            def carry_wait():
                nc.vector.memset(carrier[:], 0.0)

            def row_moments(b, mv):
                for t in range(TT):
                    ins = nc.vector.bn_stats(bst[:, t, :], x_all[:, bass.ds(b * TT + t, 1), :].rearrange("p o d -> p (o d)"))
                link(ins)
                carry_wait()
                for t in range(TT):
                    ins = nc.vector.bn_aggr(mv[:, t, :], bst[:, t, :])
                link(ins)
                nc.vector.tensor_scalar(var[:], mv[:, :, 1], EPS, None, ALU.add).then_inc(var_ready, 1)

            def normalise(b, n):
                dve.wait_ge(x_loaded, b * 16 + 16)
                row_moments(b, lmv)
                dve.wait_ge(std_ready, n)
                link(nc.vector.reciprocal(rstd[:], std[:]))
                for t in range(TT):
                    ins = nc.vector.tensor_scalar(xn[:, t, :], x_all[:, bass.ds(b * TT + t, 1), :].rearrange("p o d -> p (o d)"),
                                                  lmv[:, t, 0:1], rstd[:, t:t + 1], ALU.subtract, ALU.mult)
                ins.then_inc(xn_ready, 1)

            def second_moments(b, n):
                dve.wait_ge(x1_ready, b + 1)
                for t in range(TT):
                    ins = nc.vector.bn_stats(bst[:, t, :], x_all[:, bass.ds(b * TT + t, 1), :].rearrange("p o d -> p (o d)"))
                link(ins)
                carry_wait()
                out = ln2[:, bass.ts(b, TT), :]
                for t in range(TT):
                    ins = nc.vector.bn_aggr(lmv[:, t, :], bst[:, t, :])
                link(ins)
                nc.vector.tensor_scalar(var[:], lmv[:, :, 1], EPS, None, ALU.add).then_inc(var_ready, 1)
                nc.vector.tensor_copy(out[:, :, 0], lmv[:, :, 0])
                dve.wait_ge(std_ready, n)
                link(nc.vector.reciprocal(out[:, :, 1], std[:]))

            def batch(b, roots, first=False, last=False):
                k = [0]
                start = b * R_ITEMS

                def item():
                    dve.wait_ge(filled, start + (k[0] + 1))
                    k[0] += 1
                    return (k[0] - 1) % R_BANKS

                for f in range(KT):
                    nc.vector.tensor_copy(xnT[:, f, :], ps[:, item(), :]).then_inc(drained, 1)
                for dst in (qT, kT):
                    for f in range(KT):
                        nc.vector.tensor_copy(dst[:, f, :], ps[:, item(), :]).then_inc(drained, 1)
                for c in range(TT):
                    nc.vector.tensor_tensor(kv[:, c, :], ps[:, item(), :], kvscale[:], ALU.mult).then_inc(drained, 1)

                def scores(c):
                    for f in range(KT):
                        for half in range(2):
                            h = f * HT + half * 4
                            nc.vector.tensor_tensor(probs[:, c % 2, h:h + 4, :],
                                                    ps[:, item(), :].rearrange("p (h t) -> p h t", h=4),
                                                    decay[:, h:h + 4, :], ALU.mult).then_inc(drained, 1)

                def states(c):
                    for f in range(KT):
                        o = item()
                        if c == 0:
                            nc.vector.tensor_tensor(state[:, 1, f, :], ps[:, o, 0:P], blockmask[:],
                                                    ALU.mult).then_inc(drained, 1)
                        else:
                            link(nc.vector.tensor_tensor(stmp[:], ps[:, o, 0:P], blockmask[:], ALU.mult))
                            nc.vector.scalar_tensor_tensor(out=state[:, c + 1, f, :], in0=state[:, c, f, :],
                                                           scalar=chunkdecay[:, f:f + 1], in1=stmp[:],
                                                           op0=ALU.mult, op1=ALU.add).then_inc(drained, 1)
                            dve.wait_ge(drained, start + k[0])

                def output(c):
                    o = item()
                    nc.vector.tensor_copy(r[:, c, :], ps[:, o, 0:D])
                    nc.vector.bn_stats(rbst[:, c, :], ps[:, o, 0:D]).then_inc(drained, 1)

                scores(0)
                if not first:
                    second_moments(b - 1, roots + 1)
                if not last:
                    normalise(b + 1, roots + (1 if first else 2))
                for c in range(1, TT):
                    scores(c)
                    states(c - 1)
                    output(c - 1)
                output(TT - 1)
                assert k[0] == R_ITEMS
                dve.wait_ge(drained, start + R_ITEMS)
                carry_wait()
                link(nc.vector.bn_aggr(rmv[:], rbst[:]))
                nc.vector.tensor_copy(rs2[:, 0:1], rmv[:, 0:1])
                nc.vector.scalar_tensor_tensor(out=rs2[:, 1:2], in0=rmv[:, 0:1], scalar=rmv[:, 0:1],
                                               in1=rmv[:, 1:2], op0=ALU.mult, op1=ALU.add).then_inc(stats_ready, 1)
                dve.wait_ge(stats_filled, b + 1)
                link(nc.vector.tensor_copy(gs2[:], ps[:, R_BANKS, 0:2]))
                link(nc.vector.tensor_scalar(rmv[:, 0:1], gs2[:, 0:1], gs2[:, 0:1], None, ALU.mult))
                link(nc.vector.tensor_scalar(rmv[:, 1:2], gs2[:, 1:2], rmv[:, 0:1], EPS, ALU.subtract, ALU.add))
                nc.vector.tensor_copy(var[:], rmv[:, 1:2].broadcast_to([P, TT])).then_inc(var_ready, 1)
                dve.wait_ge(std_ready, roots + (2 if first or last else 3))
                link(nc.vector.reciprocal(rstd[:], std[:]))
                link(nc.vector.tensor_scalar(ga[:], gw[:], rstd[:, 0:1], None, ALU.mult))
                link(nc.vector.tensor_scalar(gbm[:], ga[:], gs2[:, 0:1], None, ALU.mult))
                nc.vector.tensor_tensor(gbm[:], gb[:], gbm[:], ALU.subtract).then_inc(affine_ready, 1)

            dve.wait_ge(consts, 16 * NCONST)
            past_h = past[:].unsqueeze(2).broadcast_to([P, KT, HT, HD])
            mask_h = blockmask[:].rearrange("p (h e) -> p h e", h=HT).unsqueeze(1).broadcast_to([P, KT, HT, HD])
            for f in range(KT):
                ins = nc.vector.scalar_tensor_tensor(out=past_bd[:, f, :].rearrange("p (h e) -> p h e", h=HT),
                                                     in0=past_h[:, f], scalar=float(D), in1=mask_h[:, f],
                                                     op0=ALU.mult, op1=ALU.mult)
            ins.then_inc(past_ready, 1)
            normalise(0, 1)
            batch(0, 1, first=True)
            base[0], steps[0] = steps[0], 0
            before = base[0]
            with dve.Fori(1, B - 1) as b:
                base[0] = (b - 1) * R_LINKS + before
                batch(b, 3 * b)
            assert steps[0] == R_LINKS, steps[0]
            base[0], steps[0] = before + (B - 2) * R_LINKS, 0
            batch(B - 1, 3 * B - 3, last=True)
            second_moments(B - 1, 3 * B)



G = 4
GH = H // G
KPARTS = [0, 1, 0, 2, 0, 1]
QPARTS = [0, 0, 1, 0, 2, 1]
NB = len(KPARTS)
XR = NB * HD
MR = 3
FULL = S // 512
TAIL = S - FULL * 512
W_BANKS = 3
COLS = [(i * 512, w) for i, w in enumerate(widths(S, 512))]
V_RUNS = [(0, 2), (2, 2), (4, 2), (6, 2), (8, 2), (10, 1), (11, 1), (12, 1)]
SPLITS = KT + KT * len(COLS)


def next_group_items(g):
    out = []
    for j in range(GH):
        out += [("max", g, j, t, i) for t in range(TT) for i in range(FULL)] + [("tails", g, j)]
    return out


def projection_items():
    q = [("xnT", f) for f in range(KT)] + [("q", f) for f in range(KT)]
    k = [("k", f, i) for f in range(KT) for i in range(len(COLS))]
    v = [("v", i) for i in range(len(V_RUNS))]
    return q, k, v


def work_of(prev, following):
    plan = [[[] for _ in range(SC)] for _ in range(G)]
    q, k, v = projection_items()
    if prev:
        plan[0][1].append(("norm", G - 1))
        plan[0][3] += [("oT", 0), ("oT", 1)]
        plan[0][5].append(("wo", 0))
        plan[0][6].append(("wo", 1))
    if following:
        plan[0][7] += q[0:2]
        plan[0][9] += q[2:4]
        for n, item in enumerate(k):
            plan[1][n].append(item)
        for n, item in enumerate(v):
            plan[2][n + 1].append(item)
    for g in range(1, G):
        plan[g][1].append(("norm", g - 1))
    for g in range(G):
        if g < G - 1 or following:
            todo = next_group_items((g + 1) % G)
            for c in range(SC - 2):
                m = 5 if c < 8 else 4
                plan[g][c] += todo[:m]
                todo = todo[m:]
            assert not todo
            plan[g][SC - 2].append(("shift", (g + 1) % G))
    return plan


def order(plan):
    return [item for group in plan for chunk in group for item in chunk]


def prologue_items():
    q, k, v = projection_items()
    return q + k + v + next_group_items(0) + [("shift", 0)]


N_PRO = len(prologue_items())
N_FIRST = len(order(work_of(False, True)))
N_MID = len(order(work_of(True, True)))
PREV = N_MID - N_FIRST
X_LINKS = 22
S_ITEMS = 2 * SC * G


def cross_attention(nc, x_all, ln2, io):
    assert N_MID % W_BANKS == 0
    with ExitStack() as ctx:
        def sb(name, shape, dt=F32):
            return ctx.enter_context(nc.sbuf_tensor(name, shape, dt))

        def sem(name):
            return ctx.enter_context(nc.semaphore(name))

        ps = ctx.enter_context(nc.psum_tensor("x_ps", [P, 8, 512], F32))
        PV, WORK = 4, 5
        ident = sb("x_ident", [P, P])
        identb = sb("x_identb", [P, P], BF16)
        wq, wk, wv, wo = (sb("x_w" + n, [P, KT, D]) for n in "qkvo")
        bq, bk = sb("x_bq", [P, KT]), sb("x_bk", [P, KT])
        bv, bo = sb("x_bv", [P, D]), sb("x_bo", [P, D])
        kst = [sb(f"x_kst{g}", [XR + MR, GH, S], BF16) for g in range(G)]
        qst = [sb(f"x_qst{g}", [XR + MR, GH, T], BF16) for g in range(G)]
        vst = [sb(f"x_vst{g}", [P, SC, GH, HD + 1]) for g in range(G)]
        v_all = sb("x_v_all", [P, SC, D])
        ctxT = sb("x_ctxT", [P, KT, S])
        kp = sb("x_kp", [P, KT, 3, S], BF16)
        qp = sb("x_qp", [P, KT, 3, T], BF16)
        rest = sb("x_rest", [P, 2, 512])
        left = sb("x_left", [P, 512])
        probs = sb("x_probs", [P, 4, 2, T])
        ou = sb("x_ou", [P, T])
        o_all = sb("x_o_all", [P, TT, D])
        oT = sb("x_oT", [P, KT, T])
        otmp = ou[:].rearrange("p (n d) -> p n d", n=2)
        xn, xnT = o_all, oT
        mx = sb("x_mx", [P, GH, TT, FULL + 1])
        negm = sb("x_negm", [P, GH, TT])
        mres = sb("x_mres", [P, GH, TT])
        mparts = sb("x_mparts", [P, TT, GH, MR], BF16)
        mrows = sb("x_mrows", [GH * MR, T], BF16)
        rden = sb("x_rden", [P, TT, GH])
        k_dram = nc.dram_tensor("k_parts", [B, KT, 3, P, S], BF16, kind="Internal").ap()
        q_dram = nc.dram_tensor("q_parts", [B, KT, 3, P, T], BF16, kind="Internal").ap()

        consts, ctx_loaded, ones_set = sem("x_consts"), sem("ctx_loaded"), sem("ones_set")
        ones_loaded = sem("ones_loaded")
        filled, drained = sem("w_filled"), sem("w_drained")
        s_filled, exp_done, pv_used = sem("s_filled"), sem("exp_done"), sem("pv_used")
        pv_evac = sem("pv_evac")
        xn_ready, mparts_ready, m_loaded = sem("x_xn_ready"), sem("mparts_ready"), sem("m_loaded")
        split_step, split_done = sem("split_step"), sem("split_done")
        q_spilled, k_spilled = sem("q_spilled"), sem("k_spilled")
        v_ready = sem("v_ready")
        kq_loaded = [sem(f"kq_loaded{g}") for g in range(G)]
        link_x = sem("x_link")
        NCONST = 9
        KQ = 16 * 2 * NB

        plans = {"first": work_of(False, True), "mid": work_of(True, True), "last": work_of(True, False)}

        def start_of(b):
            return N_PRO if isinstance(b, int) and b == 0 else b * N_MID + N_PRO - PREV

        def bank_of(b, n):
            return WORK + ((N_PRO if isinstance(b, int) and b == 0 else N_PRO - PREV) + n) % W_BANKS

        def position(kind, item):
            return order(plans[kind]).index(item)

        block = ctx.enter_context(nc.Block())

        @block.sync
        def _(sp):
            for t, name in ((ident, "ident"), (bq, "bq"), (bk, "bk"), (bv, "bv"), (bo, "bo")):
                sp.dma_start(t[:], io[name]).then_inc(consts, 16)
            for t, name in ((wq, "wq"), (wk, "wk"), (wv, "wv"), (wo, "wo")):
                sp.dma_start(t[:], io[name].rearrange("(k p) n -> p k n", p=P)).then_inc(consts, 16)

            def load_ctx(b):
                sp.dma_start(ctxT[:], io["ctxT"][b].rearrange("(k p) c -> p k c", p=P)).then_inc(ctx_loaded, 16)

            def spill_q(b):
                sp.wait_ge(split_done, b * SPLITS + KT)
                sp.dma_start(q_dram[b].rearrange("k j p t -> p (k j) t"),
                             qp[:].rearrange("p k j t -> p (k j) t")).then_inc(q_spilled, 16)

            def spill_k(b):
                sp.wait_ge(split_done, b * SPLITS + SPLITS)
                sp.dma_start(k_dram[b].rearrange("k j p t -> p (k j) t"),
                             kp[:].rearrange("p k j t -> p (k j) t")).then_inc(k_spilled, 16)
                sp.wait_ge(q_spilled, b * 16 + 16)
                sp.wait_ge(k_spilled, b * 16 + 16)

            def load_group(b, g):
                f, lo = g // 2, (g % 2) * GH * HD
                for dst, src, parts in ((qst[g], q_dram, QPARTS), (kst[g], k_dram, KPARTS)):
                    for n, part in enumerate(parts):
                        sp.dma_start(dst[n * HD:(n + 1) * HD, :, :],
                                     src[b, f, part, lo:lo + GH * HD, :].rearrange("(j d) c -> d j c", d=HD)
                                     ).then_inc(kq_loaded[g], 16)

            def attended(b, g):
                sp.wait_ge(s_filled, b * S_ITEMS + (g + 1) * 2 * SC)

            def load_shift(b, g, done):
                sp.wait_ge(drained, done)
                for j in range(GH):
                    sp.dma_start(qst[g][XR:XR + MR, j, :], mrows[j * MR:(j + 1) * MR, :]).then_inc(m_loaded, 16)

            for g in range(G):
                sp.dma_start(kst[g][XR:XR + MR, :, :], io["ones_rows"]).then_inc(ones_loaded, 16)
            load_ctx(0)
            spill_q(0)
            spill_k(0)
            for g in range(G):
                load_group(0, g)
            load_shift(0, 0, N_PRO)

            def batch(b, kind):
                start = start_of(b)
                if kind != "last":
                    if kind == "first":
                        sp.wait_ge(drained, N_PRO)
                    else:
                        sp.wait_ge(drained, start - 1)
                    load_ctx(b + 1)
                if kind != "first":
                    attended(b - 1, G - 1)
                    load_group(b, G - 1)
                for g in range(G):
                    if kind != "last":
                        if g == 0:
                            spill_q(b + 1)
                        elif g == 1:
                            spill_k(b + 1)
                            load_group(b + 1, 0)
                        else:
                            attended(b, g - 1)
                            load_group(b + 1, g - 1)
                    if g < G - 1 or kind != "last":
                        load_shift(b, (g + 1) % G, start + (position(kind, ("shift", (g + 1) % G)) + 1))

            batch(0, "first")
            with sp.Fori(1, B - 1) as b:
                batch(b, "mid")
            batch(B - 1, "last")

        @block.tensor
        def _(pe):
            pe.wait_ge(consts, 16 * NCONST)
            pe.wait_ge(ones_set, 6)
            pe.wait_ge(ones_loaded, 16 * G)

            def work(item, bank, b, b1, at):
                o = ps[:, bank, :]
                kind = item[0]
                if kind == "xnT":
                    pe.wait_ge(xn_ready, b1 + 1)
                    for t in range(TT):
                        m = pe.transpose(o[:, t * P:(t + 1) * P], xn[:, t, item[1] * P:(item[1] + 1) * P], ident[:])
                elif kind == "q":
                    pe.wait_ge(drained, at(("xnT", 1)))
                    for kk in range(KT):
                        m = pe.matmul(o, wq[:, kk, item[1] * P:(item[1] + 1) * P], xnT[:, kk, :],
                                      start=kk == 0, stop=kk == KT - 1)
                elif kind == "k":
                    pe.wait_ge(ctx_loaded, b1 * 16 + 16)
                    c, w = COLS[item[2]]
                    for kk in range(KT):
                        m = pe.matmul(o[:, 0:w], wk[:, kk, item[1] * P:(item[1] + 1) * P], ctxT[:, kk, c:c + w],
                                      start=kk == 0, stop=kk == KT - 1)
                elif kind == "v":
                    c0, n = V_RUNS[item[1]]
                    for c in range(c0, c0 + n):
                        w = min(P, S - c * P)
                        for kk in range(KT):
                            m = pe.matmul(o[0:w, (c - c0) * D:(c - c0 + 1) * D], ctxT[:, kk, c * P:c * P + w],
                                          wv[:, kk, :], start=kk == 0, stop=kk == KT - 1)
                elif kind == "max":
                    _, g, j, t, i = item
                    m = pe.matmul(o, qst[g][0:XR, j, t * P:(t + 1) * P], kst[g][0:XR, j, i * 512:(i + 1) * 512],
                                  start=True, stop=True)
                elif kind == "tails":
                    _, g, j = item
                    for t in range(TT):
                        m = pe.matmul(o[:, t * TAIL:(t + 1) * TAIL], qst[g][0:XR, j, t * P:(t + 1) * P],
                                      kst[g][0:XR, j, FULL * 512:S], start=True, stop=True)
                elif kind == "shift":
                    for t in range(TT):
                        m = pe.matmul(o[0:GH * MR, t * P:(t + 1) * P], mparts[:, t, :, :], identb[:],
                                      start=True, stop=True)
                elif kind == "norm":
                    for t in range(TT):
                        m = pe.transpose(o[:, t * P:(t + 1) * P], ou[:, t * P:(t + 1) * P], ident[:])
                elif kind == "oT":
                    pe.wait_ge(drained, at(("norm", G - 1)))
                    for t in range(TT):
                        m = pe.transpose(o[:, t * P:(t + 1) * P], o_all[:, t, item[1] * P:(item[1] + 1) * P],
                                         ident[:])
                elif kind == "wo":
                    pe.wait_ge(drained, at(("oT", 1)))
                    for n in range(2):
                        t = 2 * item[1] + n
                        for kk in range(KT):
                            m = pe.matmul(o[:, n * D:(n + 1) * D], oT[:, kk, t * P:(t + 1) * P], wo[:, kk, :],
                                          start=kk == 0, stop=kk == KT - 1)
                m.then_inc(filled, 1)

            for n, item in enumerate(prologue_items()):
                if n >= W_BANKS:
                    pe.wait_ge(drained, n - W_BANKS + 1)
                if item == ("max", 0, 0, 0, 0):
                    pe.wait_ge(kq_loaded[0], KQ)
                if item == ("shift", 0):
                    pe.wait_ge(mparts_ready, 1)
                work(item, WORK + n % W_BANKS, 0, 0, lambda i: prologue_items().index(i) + 1)

            def batch(b, kind):
                start = start_of(b)
                plan = plans[kind]
                k = [0]

                def values(g, q):
                    if q == 0:
                        if not (kind == "first" and g == 0):
                            pe.wait_ge(pv_evac, b * G + g)
                        pe.wait_ge(v_ready, b * 2 * G + 2 * (g + 1))
                    pe.wait_ge(exp_done, b * S_ITEMS + (g * 2 * SC + 2 * (q + 1)))
                    w = min(P, S - q * P)
                    for j in range(GH):
                        slot = (g * 2 * SC + 2 * q + j // 2) % 4
                        m = pe.matmul(ps[32 * j:32 * j + HD + 1, PV, :], vst[g][0:w, q, j, :],
                                      probs[0:w, slot, j % 2, :], start=q == 0, stop=q == SC - 1)
                    m.then_inc(pv_used, 1)

                def fill(g, items):
                    for item in items:
                        nxt = (g + 1) % G
                        if item == ("max", nxt, 0, 0, 0):
                            pe.wait_ge(kq_loaded[nxt], (b + (g == G - 1)) * KQ + KQ)
                        if item[0] == "shift":
                            pe.wait_ge(mparts_ready, b * G + (g + 2))
                        if item[0] == "norm":
                            pe.wait_ge(pv_evac, b * G + g)
                        pe.wait_ge(drained, start + (k[0] - W_BANKS + 1))
                        work(item, bank_of(b, k[0]), b, b + 1, lambda i: start + (position(kind, i) + 1))
                        k[0] += 1

                for g in range(G):
                    pe.wait_ge(m_loaded, b * 16 * GH * G + 16 * GH * (g + 1))
                    for c in range(SC):
                        w = min(P, S - c * P)
                        for pair in range(2):
                            n = g * 2 * SC + 2 * c + pair
                            if not (kind == "first" and n < 2):
                                pe.wait_ge(exp_done, b * S_ITEMS + (n - 1))
                            for h in range(2):
                                m = pe.matmul(ps[0:w, 2 * (n % 2) + h, :], kst[g][:, 2 * pair + h, c * P:c * P + w],
                                              qst[g][:, 2 * pair + h, :], start=True, stop=True)
                            m.then_inc(s_filled, 1)
                            fill(g, plan[g][c][0:2] if pair == 0 else plan[g][c][2:3])
                        if c:
                            values(g, c - 1)
                        fill(g, plan[g][c][3:])
                    values(g, SC - 1)

            batch(0, "first")
            with pe.Fori(1, B - 1) as b:
                batch(b, "mid")
            batch(B - 1, "last")
            n = start_of(B - 1) + len(order(plans["last"]))
            end = [("norm", G - 1), ("oT", 0), ("oT", 1), ("wo", 0), ("wo", 1)]
            pe.wait_ge(pv_evac, B * G)
            for i, item in enumerate(end):
                pe.wait_ge(drained, n + i - W_BANKS + 1)
                work(item, WORK + (n + i) % W_BANKS, B - 1, B, lambda it: n + end.index(it) + 1)

        @block.scalar
        def _(act):
            def batch(b, kind):
                for g in range(G):
                    for c in range(SC):
                        w = min(P, S - c * P)
                        for pair in range(2):
                            n = g * 2 * SC + 2 * c + pair
                            act.wait_ge(s_filled, b * S_ITEMS + (n + 1))
                            if not (kind == "first" and n // 2 < 2):
                                act.wait_ge(pv_used, b * (S_ITEMS // 2) + (n // 2 - 1))
                            nc.scalar.activation(probs[0:w, n % 4, :, :], ps[0:w, 2 * (n % 2):2 * (n % 2) + 2, :],
                                                 ACT.Exp, scale=HD ** -0.5).then_inc(exp_done, 1)

            batch(0, "first")
            with act.Fori(1, B) as b:
                batch(b, "mid")

        @block.gpsimd
        def _(pool):
            for g in range(G):
                nc.gpsimd.memset(vst[g][:], 1.0).then_inc(ones_set, 1)
            pool.wait_ge(consts, 16 * NCONST)
            nc.gpsimd.tensor_copy(identb[:], ident[:]).then_inc(ones_set, 1)

            def split(dst, n, count, w):
                pool.wait_ge(drained, count)
                whole = rest[:, n[1] % 2, 0:w]
                nc.gpsimd.tensor_tensor(dst(1), whole, dst(0), ALU.subtract)
                nc.gpsimd.tensor_tensor(left[:, 0:w], whole, dst(0), ALU.subtract).then_inc(split_step, 1)
                pool.wait_ge(split_step, n[0] + (n[1] + 1))
                nc.gpsimd.tensor_tensor(dst(2), left[:, 0:w], dst(1), ALU.subtract).then_inc(split_done, 1)
                pool.wait_ge(split_done, n[0] + (n[1] + 1))

            def splits(b1, at, part):
                if part == "q":
                    for f in range(KT):
                        split(lambda j: qp[:, f, j, :], (b1 * SPLITS, f), at(("q", f)), T)
                else:
                    for f in range(KT):
                        for i, (c, w) in enumerate(COLS):
                            split(lambda j: kp[:, f, j, c:c + w], (b1 * SPLITS, KT + f * len(COLS) + i),
                                  at(("k", f, i)), w)

            def place_v(g):
                for rows, lo, hi in ((P, 0, SC - 1), (S - (SC - 1) * P, SC - 1, SC)):
                    cols = slice(g * GH * HD, (g + 1) * GH * HD)
                    nc.gpsimd.tensor_tensor(
                        vst[g][0:rows, lo:hi, :, 0:HD],
                        v_all[0:rows, lo:hi, cols].rearrange("p c (j d) -> p c j d", d=HD),
                        bv[0:rows, cols].rearrange("p (j d) -> p j d", d=HD).unsqueeze(1).broadcast_to(
                            [rows, hi - lo, GH, HD]), ALU.add).then_inc(v_ready, 1)

            pool.wait_ge(ones_set, 6)
            at0 = lambda i: prologue_items().index(i) + 1
            splits(0, at0, "q")
            splits(0, at0, "k")
            pool.wait_ge(drained, at0(("v", len(V_RUNS) - 1)))
            for g in range(G):
                place_v(g)

            def batch(b, kind):
                start = start_of(b)
                at = lambda i: start + (position(kind, i) + 1)
                if kind != "first":
                    pool.wait_ge(pv_used, b * (S_ITEMS // 2))
                    place_v(G - 1)
                if kind != "last":
                    splits(b + 1, at, "q")
                    splits(b + 1, at, "k")
                    pool.wait_ge(drained, at(("v", len(V_RUNS) - 1)))
                    for g in range(G - 1):
                        pool.wait_ge(pv_used, b * (S_ITEMS // 2) + SC * (g + 1))
                        place_v(g)

            batch(0, "first")
            with pool.Fori(1, B - 1) as b:
                batch(b, "mid")
            batch(B - 1, "last")

        @block.vector
        def _(dve):
            steps, base = [0], [0]

            def link(ins):
                steps[0] += 1
                ins.then_inc(link_x, 1)
                dve.wait_ge(link_x, base[0] + steps[0])

            def normalise(b):
                for t in range(TT):
                    row = bass.ds(b * TT + t, 1)
                    ins = nc.vector.tensor_scalar(
                        xn[:, t, :], x_all[:, row, :].rearrange("p o d -> p (o d)"),
                        ln2[:, row, 0:1].rearrange("p o d -> p (o d)"), ln2[:, row, 1:2].rearrange("p o d -> p (o d)"),
                        ALU.subtract, ALU.mult)
                ins.then_inc(xn_ready, 1)

            def first_part(o, dst, bias, n, b1, w):
                nc.vector.tensor_scalar(dst, o[:, 0:w], bias, None, ALU.add)
                if not (isinstance(b1, int) and b1 == 0 and n < 2):
                    dve.wait_ge(split_done, b1 * SPLITS + (n - 1))
                return nc.vector.tensor_scalar(rest[:, n % 2, 0:w], o[:, 0:w], bias, None, ALU.add)

            def shift_parts(count):
                dve.wait_ge(drained, count)
                link(nc.vector.tensor_reduce(out=negm[:], in_=mx[:], axis=AX.X, op=ALU.max, negate=True))
                rows, rem = (v[:].rearrange("p j t -> p t j") for v in (negm, mres))
                link(nc.vector.tensor_copy(mparts[:, :, :, 0], rows))
                link(nc.vector.tensor_tensor(rem, rows, mparts[:, :, :, 0], ALU.subtract))
                link(nc.vector.tensor_copy(mparts[:, :, :, 1], rem))
                nc.vector.tensor_tensor(mparts[:, :, :, 2], rem, mparts[:, :, :, 1],
                                        ALU.subtract).then_inc(mparts_ready, 1)

            def work(item, bank, b, b1, count, shifts):
                o = ps[:, bank, :]
                kind = item[0]
                if kind == "shift":
                    shift_parts(count - 1)
                dve.wait_ge(filled, count)
                if kind == "xnT":
                    ins = nc.vector.tensor_copy(xnT[:, item[1], :], o)
                elif kind == "q":
                    f = item[1]
                    if f == 0 and not (isinstance(b1, int) and b1 == 0):
                        dve.wait_ge(q_spilled, b1 * 16)
                    ins = first_part(o, qp[:, f, 0, :], bq[:, f:f + 1], f, b1, T)
                elif kind == "k":
                    _, f, i = item
                    c, w = COLS[i]
                    if f == 0 and i == 0 and not (isinstance(b1, int) and b1 == 0):
                        dve.wait_ge(k_spilled, b1 * 16)
                    ins = first_part(o, kp[:, f, 0, c:c + w], bk[:, f:f + 1], KT + f * len(COLS) + i, b1, w)
                elif kind == "v":
                    c0, n = V_RUNS[item[1]]
                    w = min(P, S - c0 * P)
                    if c0 == 0 and not (isinstance(b1, int) and b1 == 0):
                        dve.wait_ge(v_ready, b1 * 2 * G)
                    ins = nc.vector.tensor_copy(v_all[0:w, c0:c0 + n, :],
                                                o[0:w, 0:n * D].rearrange("p (c d) -> p c d", c=n))
                elif kind == "max":
                    _, g, j, t, i = item
                    ins = nc.vector.tensor_reduce(out=mx[:, j, t, i:i + 1], in_=o, axis=AX.X, op=ALU.max)
                elif kind == "tails":
                    _, g, j = item
                    ins = nc.vector.tensor_reduce(out=mx[:, j, :, FULL], in_=o[:, 0:TT * TAIL].rearrange("p (t c) -> p t c", t=TT),
                                                  axis=AX.X, op=ALU.max)
                elif kind == "shift":
                    if not (isinstance(shifts, int) and shifts == 0):
                        dve.wait_ge(m_loaded, shifts * 16 * GH)
                    ins = nc.vector.tensor_copy(mrows[:], o[0:GH * MR, :])
                elif kind == "norm":
                    g = item[1]
                    o4 = o.rearrange("p (t j e) -> p t j e", t=TT, j=GH)
                    link(nc.vector.reciprocal(rden[:], o4[:, :, :, HD]))
                    ins = nc.vector.tensor_tensor(
                        o_all[:, :, g * GH * HD:(g + 1) * GH * HD].rearrange("p t (j d) -> p t j d", d=HD),
                        o4[:, :, :, 0:HD], rden[:].unsqueeze(3).broadcast_to([P, TT, GH, HD]), ALU.mult)
                elif kind == "oT":
                    ins = nc.vector.tensor_copy(oT[:, item[1], :], o)
                elif kind == "wo":
                    link(nc.vector.tensor_tensor(otmp, o.rearrange("p (n d) -> p n d", n=2),
                                                 bo[:].unsqueeze(1).broadcast_to([P, 2, D]), ALU.add))
                    xb = x_all[:, bass.ds((b1 - 2) * TT + 2 * item[1], 2), :]
                    ins = nc.vector.tensor_tensor(xb, xb, otmp, ALU.add)
                ins.then_inc(drained, 1)
                if kind == "wo":
                    dve.wait_ge(drained, count)

            dve.wait_ge(consts, 16 * NCONST)
            nc.vector.memset(ps[:, PV, :], 0.0).then_inc(ones_set, 1)
            normalise(0)
            for n, item in enumerate(prologue_items()):
                work(item, WORK + n % W_BANKS, 0, 0, n + 1, 0)

            def evacuate(groups):
                dve.wait_ge(pv_used, groups)
                return nc.vector.tensor_copy(ou[:], ps[:, PV, :]).then_inc(pv_evac, 1)

            def batch(b, kind):
                start = start_of(b)
                plan = plans[kind]
                k = 0
                for g in range(G):
                    if not (kind == "first" and g == 0):
                        evacuate(b * (S_ITEMS // 2) + g * SC)
                    for c in range(SC):
                        if g == 0 and c == 5 and kind != "last":
                            normalise(b + 1)
                        for item in plan[g][c]:
                            work(item, bank_of(b, k), b, b + 1, start + (k + 1), b * G + (g + 1))
                            k += 1

            batch(0, "first")
            before = steps[0]
            steps[0] = 0
            with dve.Fori(1, B - 1) as b:
                base[0] = (b - 1) * X_LINKS + before
                batch(b, "mid")
            assert steps[0] == X_LINKS, steps[0]
            base[0], steps[0] = before + (B - 2) * X_LINKS, 0
            batch(B - 1, "last")
            evacuate(B * (S_ITEMS // 2))
            n = start_of(B - 1) + len(order(plans["last"]))
            for i, item in enumerate([("norm", G - 1), ("oT", 0), ("oT", 1), ("wo", 0), ("wo", 1)]):
                work(item, WORK + (n + i) % W_BANKS, B - 1, B + 1, n + i + 1, 0)



E = 8
TOPK = 2
HID = E + 2
NG = NT // TT
UNCHOSEN = -1e30
F_BANKS = 3


def feed_forward(nc, x_all, io, out):
    with ExitStack() as ctx:
        def sb(name, shape, dt=F32):
            return ctx.enter_context(nc.sbuf_tensor(name, shape, dt))

        def sem(name):
            return ctx.enter_context(nc.semaphore(name))

        ps = ctx.enter_context(nc.psum_tensor("f_ps", [P, 8, 512], F32))
        GATE, UP, DOWN = 0, 2, 4
        ident = sb("f_ident", [P, P])
        identb = sb("f_identb", [P, P], BF16)
        ones = sb("f_ones", [P, P])
        pick = sb("f_pick", [E, E * P])
        pickb = sb("f_pickb", [E, E * P], BF16)
        gate_w = sb("f_gate_w", [P, KT, E])
        lb = sb("f_lb", [P, E])
        wg = sb("f_wg", [P, KT, HID * P])
        wu = sb("f_wu", [P, KT, HID * P])
        wd = sb("f_wd", [P, HID, D])
        bst = sb("f_bst", [P, NT, 6])
        mv = sb("f_mv", [P, NT, 2])
        var = sb("f_var", [P, NT])
        std = sb("f_std", [P, NT])
        rstd = sb("f_rstd", [P, NT])
        xn = sb("f_xn", [P, 2, TT, D])
        xs = sb("f_xs", [P, 2, KT, T])
        xnT = sb("f_xnT", [P, KT, NT * P])
        logits = sb("f_logits", [P, NT, E])
        score = sb("f_score", [P, NT, E])
        better = sb("f_better", [P, NT, E])
        cmp = sb("f_cmp", [P, NT, E])
        chosen = sb("f_chosen", [P, NT, E])
        total = sb("f_total", [P, NT])
        sums = sb("f_sums", [P, 2 * E])
        wmean = sb("f_wmean", [P, 2 * E])
        off = sb("f_off", [P, NT, E], BF16)
        offT = sb("f_offT", [E, NT * P], BF16)
        act_g = sb("f_act_g", [P, 2, T])
        hid = sb("f_hid", [P, HID, T])

        consts = sem("f_consts")
        filled, drained = sem("f_filled"), sem("f_drained")
        var_ready, std_ready, xn_ready, xnT_kept = sem("f_var"), sem("f_std"), sem("f_xn_ready"), sem("xnT_kept")
        logits_ready, score_ready, sums_ready, off_ready = (sem("logits_ready"), sem("score_ready"),
                                                            sem("sums_ready"), sem("off_ready"))
        wd_ready, bf_ready = sem("wd_ready"), sem("f_bf_ready")
        gate_filled, up_filled, silu_done, hid_done = (sem("gate_filled"), sem("up_filled"), sem("silu_done"),
                                                       sem("hid_done"))
        down_filled, down_drained, stored = sem("down_filled"), sem("down_drained"), sem("stored")
        link_f = sem("f_link")
        NCONST = 8
        ROUTE = 6 * (NG // 2)

        block = ctx.enter_context(nc.Block())

        @block.sync
        def _(sp):
            for t, name in ((ident, "ident"), (pick, "pick"), (lb, "lb")):
                sp.dma_start(t[:], io[name]).then_inc(consts, 16)
            for t, name in ((gate_w, "gate_w"), (wg, "wg"), (wu, "wu"), (wd, "wd")):
                sp.dma_start(t[:], io[name].rearrange("(k p) n -> p k n", p=P)).then_inc(consts, 16)
            sp.dma_start(ones[:], io["ones"]).then_inc(consts, 16)
            with sp.Fori(0, NG) as n:
                sp.wait_ge(down_drained, n * 2 + 2)
                sp.dma_start(out[n].rearrange("(t p) d -> p t d", p=P), x_all[:, bass.ts(n, TT), :]).then_inc(stored, 16)
            sp.wait_ge(stored, 16 * NG)

        @block.tensor
        def _(pe):
            pe.wait_ge(consts, 16 * NCONST)
            pe.wait_ge(bf_ready, 2)

            def pair(i, first):
                k = 0

                def bank():
                    nonlocal k
                    if not (first and k < F_BANKS):
                        pe.wait_ge(drained, i * 6 + (k - F_BANKS + 1))
                    k += 1
                    return (k - 1) % F_BANKS

                for u in range(2):
                    pe.wait_ge(xn_ready, i * 2 + (u + 1))
                    for f in range(KT):
                        o = bank()
                        for t in range(TT):
                            m = pe.transpose(ps[:, o, t * P:(t + 1) * P], xn[:, u, t, f * P:(f + 1) * P], ident[:])
                        m.then_inc(filled, 1)
                for u in range(2):
                    pe.wait_ge(drained, i * 6 + 2 * (u + 1))
                    o = bank()
                    for t in range(TT):
                        for kk in range(KT):
                            m = pe.matmul(ps[:, o, t * E:(t + 1) * E], xs[:, u, kk, t * P:(t + 1) * P],
                                          gate_w[:, kk, :], start=kk == 0, stop=kk == KT - 1)
                    m.then_inc(filled, 1)

            pair(0, True)
            with pe.Fori(1, NG // 2) as i:
                pair(i, False)

            pe.wait_ge(sums_ready, 1)
            pe.wait_ge(drained, ROUTE)
            pe.matmul(ps[:, 0, 0:2 * E], ones[:], sums[:], start=True, stop=True).then_inc(filled, 1)
            pe.wait_ge(off_ready, 1)
            for n in range(NG):
                if n >= F_BANKS - 1:
                    pe.wait_ge(drained, ROUTE + 1 + n - F_BANKS + 1)
                for t in range(TT):
                    m = pe.matmul(ps[0:E, (n + 1) % F_BANKS, t * P:(t + 1) * P], off[:, n * TT + t, :], identb[:],
                                  start=True, stop=True)
                m.then_inc(filled, 1)
            pe.wait_ge(drained, ROUTE + 1 + NG)
            pe.wait_ge(xnT_kept, NG * KT)
            pe.wait_ge(wd_ready, 1)

            def tokens(n, first):
                cols = bass.ts(n, T)
                for j in range(HID):
                    if not (first and j < 2):
                        pe.wait_ge(silu_done, n * HID + (j - 1))
                    for kk in range(KT):
                        m = pe.matmul(ps[:, GATE + j % 2, :], wg[:, kk, j * P:(j + 1) * P], xnT[:, kk, cols],
                                      start=kk == 0, stop=kk == KT - 1 and j >= E)
                    if j < E:
                        m = pe.matmul(ps[:, GATE + j % 2, :], pickb[:, j * P:(j + 1) * P], offT[:, cols],
                                      start=False, stop=True)
                    m.then_inc(gate_filled, 1)
                    if not (first and j < 2):
                        pe.wait_ge(hid_done, n * HID + (j - 1))
                    for kk in range(KT):
                        m = pe.matmul(ps[:, UP + j % 2, :], wu[:, kk, j * P:(j + 1) * P], xnT[:, kk, cols],
                                      start=kk == 0, stop=kk == KT - 1)
                    m.then_inc(up_filled, 1)
                pe.wait_ge(hid_done, n * HID + HID)
                for half in range(2):
                    if not first:
                        pe.wait_ge(down_drained, n * 2 + (half - 1))
                    for t in range(2):
                        c = (2 * half + t) * P
                        for j in range(HID):
                            m = pe.matmul(ps[:, DOWN + half, t * D:(t + 1) * D], hid[:, j, c:c + P], wd[:, j, :],
                                          start=j == 0, stop=j == HID - 1)
                    m.then_inc(down_filled, 1)

            tokens(0, True)
            with pe.Fori(1, NG) as n:
                tokens(n, False)

        @block.scalar
        def _(act):
            act.wait_ge(consts, 16 * NCONST)
            nc.scalar.activation(identb[:], ident[:], ACT.Copy).then_inc(bf_ready, 1)
            nc.scalar.activation(pickb[:], pick[:], ACT.Copy).then_inc(bf_ready, 1)
            act.wait_ge(var_ready, 1)
            nc.scalar.activation(std[:], var[:], ACT.Sqrt).then_inc(std_ready, 1)
            with act.Fori(0, NG // 2) as i:
                for u in range(2):
                    act.wait_ge(drained, i * 6 + 2 * (u + 1))
                    for f in range(KT):
                        nc.scalar.activation(xnT[:, f, bass.ds(i * 2 * T + u * T, T)], xs[:, u, f, :],
                                             ACT.Copy).then_inc(xnT_kept, 1)
            act.wait_ge(logits_ready, 1)
            nc.scalar.activation(score[:], logits[:], ACT.Sigmoid).then_inc(score_ready, 1)

            def tokens(n, first):
                for j in range(HID):
                    act.wait_ge(gate_filled, n * HID + (j + 1))
                    if not (first and j < 2):
                        act.wait_ge(hid_done, n * HID + (j - 1))
                    nc.scalar.activation(act_g[:, j % 2, :], ps[:, GATE + j % 2, :], ACT.Silu).then_inc(silu_done, 1)

            tokens(0, True)
            with act.Fori(1, NG) as n:
                tokens(n, False)

        @block.vector
        def _(dve):
            steps = [0]

            def link(ins):
                steps[0] += 1
                ins.then_inc(link_f, 1)
                dve.wait_ge(link_f, steps[0])

            for t in range(NT):
                ins = nc.vector.bn_stats(bst[:, t, :], x_all[:, t, :])
            link(ins)
            for t in range(NT):
                ins = nc.vector.bn_aggr(mv[:, t, :], bst[:, t, :])
            link(ins)
            nc.vector.tensor_scalar(var[:], mv[:, :, 1], EPS, None, ALU.add).then_inc(var_ready, 1)
            dve.wait_ge(std_ready, 1)
            link(nc.vector.reciprocal(rstd[:], std[:]))
            dve.wait_ge(consts, 16 * NCONST)

            def pair(i, first):
                for u in range(2):
                    for t in range(TT):
                        row = bass.ds(i * 2 * TT + (u * TT + t), 1)
                        ins = nc.vector.tensor_scalar(
                            xn[:, u, t, :], x_all[:, row, :].rearrange("p o d -> p (o d)"),
                            mv[:, row, 0:1].rearrange("p o d -> p (o d)"), rstd[:, bass.ds(i * 2 * TT + (u * TT + t), 1)],
                            ALU.subtract, ALU.mult)
                    ins.then_inc(xn_ready, 1)
                for u in range(2):
                    for f in range(KT):
                        dve.wait_ge(filled, i * 6 + (2 * u + f + 1))
                        if not first:
                            dve.wait_ge(xnT_kept, i * 2 * KT + (u * KT + f + 1 - 2 * KT))
                        nc.vector.tensor_copy(xs[:, u, f, :], ps[:, (2 * u + f) % F_BANKS, :]).then_inc(drained, 1)
                for u in range(2):
                    dve.wait_ge(filled, i * 6 + (4 + u + 1))
                    nc.vector.tensor_tensor(
                        logits[:, bass.ds(i * 2 * TT + u * TT, TT), :],
                        ps[:, (4 + u) % F_BANKS, 0:TT * E].rearrange("p (t e) -> p t e", t=TT),
                        lb[:].unsqueeze(1).broadcast_to([P, TT, E]), ALU.add).then_inc(drained, 1)

            pair(0, True)
            with dve.Fori(1, NG // 2) as i:
                pair(i, False)
            dve.wait_ge(drained, ROUTE)
            nc.vector.memset(better[:], 0.0).then_inc(logits_ready, 1)
            dve.wait_ge(score_ready, 1)
            for j in range(E):
                sj = score[:, :, j:j + 1]
                link(nc.vector.tensor_tensor(cmp[:], sj.broadcast_to([P, NT, E]), score[:], ALU.is_gt))
                link(nc.vector.tensor_tensor(better[:], better[:], cmp[:], ALU.add))
                if j < E - 1:
                    rest = slice(j + 1, E)
                    link(nc.vector.tensor_tensor(cmp[:, :, rest], sj.broadcast_to([P, NT, E - 1 - j]),
                                                 score[:, :, rest], ALU.is_equal))
                    link(nc.vector.tensor_tensor(better[:, :, rest], better[:, :, rest], cmp[:, :, rest], ALU.add))
            link(nc.vector.tensor_scalar(chosen[:], better[:], TOPK - 0.5, None, ALU.is_lt))
            nc.vector.tensor_scalar(off[:], chosen[:], -UNCHOSEN, UNCHOSEN, ALU.mult, ALU.add).then_inc(off_ready, 1)
            link(nc.vector.tensor_tensor(cmp[:], score[:], chosen[:], ALU.mult))
            link(nc.vector.tensor_reduce(out=total[:], in_=cmp[:], axis=AX.X, op=ALU.add))
            link(nc.vector.tensor_scalar(total[:], total[:], 1e-8, None, ALU.add))
            link(nc.vector.reciprocal(total[:], total[:]))
            link(nc.vector.tensor_tensor(cmp[:], cmp[:], total[:].unsqueeze(2).broadcast_to([P, NT, E]), ALU.mult))
            nc.vector.tensor_reduce(out=sums[:, 0:E], in_=cmp[:].rearrange("p n e -> p e n"), axis=AX.X, op=ALU.add)
            nc.vector.tensor_reduce(out=sums[:, E:2 * E], in_=chosen[:].rearrange("p n e -> p e n"), axis=AX.X,
                                    op=ALU.add).then_inc(sums_ready, 1)
            dve.wait_ge(filled, ROUTE + 1)
            link(nc.vector.tensor_scalar(wmean[:, E:2 * E], ps[:, 0, E:2 * E], 1.0, None, ALU.max))
            link(nc.vector.reciprocal(wmean[:, E:2 * E], wmean[:, E:2 * E]))
            nc.vector.tensor_tensor(wmean[:, 0:E], ps[:, 0, 0:E], wmean[:, E:2 * E], ALU.mult).then_inc(drained, 1)
            dve.wait_ge(drained, ROUTE + 1)
            for j in range(E):
                ins = nc.vector.tensor_scalar(wd[:, j, :], wd[:, j, :], wmean[:, j:j + 1], None, ALU.mult)
            ins.then_inc(wd_ready, 1)
            for n in range(NG):
                dve.wait_ge(filled, ROUTE + 2 + n)
                nc.vector.tensor_copy(offT[:, n * T:(n + 1) * T], ps[0:E, (n + 1) % F_BANKS, :]).then_inc(drained, 1)

            def tokens(n, first):
                for j in range(HID):
                    dve.wait_ge(up_filled, n * HID + (j + 1))
                    dve.wait_ge(silu_done, n * HID + (j + 1))
                    nc.vector.tensor_tensor(hid[:, j, :], ps[:, UP + j % 2, :], act_g[:, j % 2, :],
                                            ALU.mult).then_inc(hid_done, 1)
                for half in range(2):
                    dve.wait_ge(down_filled, n * 2 + (half + 1))
                    xb = x_all[:, bass.ds(n * TT + 2 * half, 2), :]
                    nc.vector.tensor_tensor(xb, xb, ps[:, DOWN + half, :].rearrange("p (t d) -> p t d", t=2),
                                            ALU.add).then_inc(down_drained, 1)

            tokens(0, True)
            with dve.Fori(1, NG) as n:
                tokens(n, False)


def build(nc, io, out, stage=3):
    with ExitStack() as ctx:
        x_all = ctx.enter_context(nc.sbuf_tensor("x_all", [P, NT, D], F32))
        ln2 = ctx.enter_context(nc.sbuf_tensor("ln2", [P, NT, 2], F32))
        retention(nc, x_all, ln2, io)
        if stage > 1:
            cross_attention(nc, x_all, ln2, io)
        if stage > 2:
            feed_forward(nc, x_all, io, out)
        else:
            with nc.semaphore("dbg") as dbg, nc.Block() as block:
                @block.sync
                def _(sp):
                    sp.dma_start(out.rearrange("b (n p) d -> p (b n) d", p=P), x_all[:]).then_inc(dbg, 16)
                    sp.wait_ge(dbg, 16)


def shape_constants():
    f = np.float32
    gamma = (f(1.0) - f(2.0) ** (f(-5.0) - np.arange(H, dtype=f))).astype(f)
    i = np.arange(P)
    head = i // HD
    diff = i[None, :] - i[:, None]
    decay = np.where(diff[:, None, :] >= 0, gamma[None, :, None] ** np.maximum(diff, 0)[:, None, :].astype(f), 0)
    hs = head[:, None] + HT * np.arange(KT)[None, :]
    qdecay = gamma[hs][:, :, None] ** i[None, None, :].astype(f)
    kscale = np.repeat(gamma[None, :] ** (P - i)[:, None].astype(f), HD, axis=1)
    return {
        "ident": np.eye(P, dtype=f),
        "decay": decay.astype(f),
        "qdecay": qdecay.astype(f),
        "kvscale": np.concatenate([kscale, np.ones((P, D), f)], 1).astype(f),
        "headmask": (head[:, None] == np.arange(HT)[None, :]).astype(f),
        "blockmask": (head[:, None] == head[None, :]).astype(f),
        "chunkdecay": (gamma[hs] ** f(P)).astype(f),
        "ones": np.ones((P, P), f),
        "pick": (np.arange(E)[:, None] == np.arange(E * P)[None, :] // P).astype(f),
        "meanw": np.full((P, P), 1.0 / P, f),
    }


STAGE = 3


def kernel(**inputs):
    import ml_dtypes
    import concourse.bacc as bacc
    from concourse.bass_utils import run_bass_kernel_spmd as run

    a = {k: np.asarray(v) for k, v in inputs.items()}

    def rows(v):
        return np.broadcast_to(v[None, :], (P, v.shape[0]))

    arrays = dict(shape_constants())
    arrays.update({
        "x": a["x"],
        "wqkv": a["L0_attn_W_qkv"],
        "past": a["L0_attn_past_kv"].reshape(KT, P, HD).transpose(1, 0, 2),
        "gw": rows(np.repeat(a["L0_attn_gn_weight"], HD)),
        "gb": rows(np.repeat(a["L0_attn_gn_bias"], HD)),
        "ctxT": a["ctx_1024"].transpose(0, 2, 1),
        "wq": a["L0_xattn_Wq"].T,
        "wk": a["L0_xattn_Wk"].T,
        "wv": a["L0_xattn_Wv"].T,
        "wo": a["L0_xattn_Wo"].T,
        "bq": a["L0_xattn_bq"].reshape(KT, P).T,
        "bk": a["L0_xattn_bk"].reshape(KT, P).T,
        "bv": rows(a["L0_xattn_bv"]),
        "bo": rows(a["L0_xattn_bo"]),
        "gate_w": a["L0_ffn_gate_w"].T,
        "lb": rows(a["L0_ffn_lb_bias"]),
        "wg": np.concatenate([a["L0_ffn_expert_gate_w"].reshape(E * P, D), a["L0_ffn_shared_gate_w"]], 0).T,
        "wu": np.concatenate([a["L0_ffn_expert_up_w"].reshape(E * P, D), a["L0_ffn_shared_up_w"]], 0).T,
        "wd": np.concatenate([a["L0_ffn_expert_down_w"].transpose(0, 2, 1).reshape(E * P, D),
                              a["L0_ffn_shared_down_w"].T], 0),
    })
    arrays["ones_rows"] = np.ones((MR, GH, S), ml_dtypes.bfloat16)
    nc = bacc.Bacc("TRN2", target_bir_lowering=False, num_devices=1)
    io = {}
    for name in arrays:
        arrays[name] = np.ascontiguousarray(arrays[name])
        io[name] = nc.dram_tensor("in_" + name, arrays[name].shape,
                                  mybir.dt.from_np(arrays[name].dtype), kind="ExternalInput").ap()
    out = nc.dram_tensor("out_0", (B, T, D), F32, kind="ExternalOutput").ap()
    build(nc, io, out, STAGE)
    r = run(nc, [{"in_" + n: v for n, v in arrays.items()}], core_ids=[0])
    return r.results[0]["out_0"]
```

```python
from contextlib import ExitStack

import numpy as np

import concourse.bass as bass
from concourse import mybir

F32 = mybir.dt.float32
BF16 = mybir.dt.bfloat16
F32R = mybir.dt.float32r
ALU = mybir.AluOpType
ACT = mybir.ActivationFunctionType
AX = mybir.AxisListType

P = 128
B, T, D, H = 8, 512, 256, 16
HD = D // H
TT = T // P
KT = D // P
HT = P // HD
NT = B * TT
S = 1601
SC = -(-S // P)
EPS = 1e-5


def widths(total, step):
    return [min(step, total - i) for i in range(0, total, step)]



R_BANKS = 6
Y_BANKS = (7, 6)
R_ITEMS = 36
R_LINKS = 17


def retention(nc, x_all, ln2, io):
    with ExitStack() as ctx:
        def sb(name, shape, dt=F32):
            return ctx.enter_context(nc.sbuf_tensor(name, shape, dt))

        def sem(name):
            return ctx.enter_context(nc.semaphore(name))

        ps = ctx.enter_context(nc.psum_tensor("r_ps", [P, 8, 512], F32))
        ident = sb("r_ident", [P, P])
        decay = sb("r_decay", [P, H, P])
        qdecay = sb("r_qdecay", [P, KT, P])
        kscale = sb("r_kscale", [P, D])
        headmask = sb("r_headmask", [P, HT])
        blockmask = sb("r_blockmask", [P, P])
        chunkdecay = sb("r_chunkdecay", [P, KT])
        meanw = sb("r_meanw", [P, P])
        wqkv = sb("r_wqkv", [P, KT, 3 * D])
        past = sb("r_past", [P, KT, HD])
        gw = sb("r_gw", [P, KT])
        gb = sb("r_gb", [P, KT])

        past_bd = sb("r_past_bd", [P, KT, P])
        xn = sb("r_xn", [P, TT, D])
        xnT = sb("r_xnT", [P, KT, T])
        qT = sb("r_qT", [P, KT, T])
        qwide = sb("r_qwide", [P, KT, HT, T])
        qg = sb("r_qg", [P, KT, T])
        kT = sb("r_kT", [P, KT, T])
        kd = sb("r_kd", [P, TT, D])
        vz = sb("r_vz", [P, TT, H // 2, 4, HD])
        probs = sb("r_probs", [P, 2, H, P])
        state = sb("r_state", [P, TT, KT, P])
        stmp = sb("r_stmp", [P, P])
        rT = sb("r_rT", [P, KT, T])
        bst = sb("r_bst", [P, TT, 6])
        lmv = sb("r_lmv", [P, TT, 2])
        rbst = sb("r_rbst", [P, TT, 6])
        rmv = sb("r_rmv", [P, 2])
        rs2 = sb("r_rs2", [P, 2])
        gs2 = sb("r_gs2", [P, 2])
        var = sb("r_var", [P, TT])
        carrier = sb("r_carrier", [P, 1])
        pool_carrier = sb("r_pool_carrier", [P, KT])
        std = sb("r_std", [P, TT])
        rstd = sb("r_rstd", [P, TT])
        ga = sb("r_ga", [P, KT])
        gbm = sb("r_gbm", [P, KT])
        y = sb("r_y", [P, KT, T])

        x_loaded, consts = sem("x_loaded"), sem("r_consts")
        filled, drained = sem("r_filled"), sem("r_drained")
        var_ready, std_ready = sem("var_ready"), sem("std_ready")
        xn_ready, past_ready = sem("xn_ready"), sem("past_ready")
        q_wide, q_decayed = sem("q_wide"), sem("q_decayed")
        stats_ready, stats_filled = sem("stats_ready"), sem("stats_filled")
        affine_ready, y_ready, y_filled = sem("affine_ready"), sem("y_ready"), sem("y_filled")
        x1_ready, vz_zero = sem("x1_ready"), sem("vz_zero")
        link_r = sem("r_link")

        NCONST = 12
        block = ctx.enter_context(nc.Block())

        @block.sync
        def _(sp):
            sp.dma_start(x_all[:, 0:TT, :], io["x"][0].rearrange("(n p) d -> p n d", p=P)).then_inc(x_loaded, 16)
            sp.dma_start(wqkv[:], io["wqkv"].rearrange("(k p) n -> p k n", p=P)).then_inc(consts, 16)
            for t, name in ((ident, "ident"), (kscale, "kscale"), (qdecay, "qdecay"), (headmask, "headmask"),
                            (blockmask, "blockmask"), (chunkdecay, "chunkdecay"), (meanw, "meanw"),
                            (decay, "decay"), (past, "past"), (gw, "gw"), (gb, "gb")):
                sp.dma_start(t[:], io[name]).then_inc(consts, 16)
            for b in range(1, B):
                sp.wait_ge(x_loaded, 16 * b)
                sp.dma_start(x_all[:, b * TT:(b + 1) * TT, :],
                             io["x"][b].rearrange("(n p) d -> p n d", p=P)).then_inc(x_loaded, 16)

        @block.tensor
        def _(pe):
            pe.wait_ge(consts, 16 * NCONST)
            pe.wait_ge(past_ready, 1)

            def v_of(c, f):
                return vz[:, c, f * HT // 2:(f + 1) * HT // 2, 0:4:3, :]


            def turn_y(b):
                pe.wait_ge(y_ready, (b + 1) * KT)
                if not (isinstance(b, int) and b == 0):
                    pe.wait_ge(x1_ready, b * 2)
                for half in range(2):
                    for t in range(2):
                        for f in range(KT):
                            m = pe.transpose(ps[:, Y_BANKS[half], t * D + f * P:t * D + (f + 1) * P],
                                             y[:, f, (2 * half + t) * P:(2 * half + t + 1) * P], ident[:])
                    m.then_inc(y_filled, 1)

            def stats(b):
                pe.wait_ge(stats_ready, b + 1)
                pe.matmul(ps[:, R_BANKS, 0:2], meanw[:], rs2[:], start=True, stop=True).then_inc(stats_filled, 1)

            def batch(b):
                k = [0]
                start = b * R_ITEMS

                def bank():
                    if not (isinstance(b, int) and b == 0 and k[0] < R_BANKS):
                        pe.wait_ge(drained, start + (k[0] - R_BANKS + 1))
                    k[0] += 1
                    return (k[0] - 1) % R_BANKS

                pe.wait_ge(xn_ready, b + 1)
                for f in range(KT):
                    o = bank()
                    for t in range(TT):
                        m = pe.transpose(ps[:, o, t * P:(t + 1) * P], xn[:, t, f * P:(f + 1) * P], ident[:])
                    m.then_inc(filled, 1)
                pe.wait_ge(drained, start + KT)
                for part in range(2):
                    if part and not (isinstance(b, int) and b == 0):
                        stats(b - 1)
                    for f in range(KT):
                        o = bank()
                        for kk in range(KT):
                            m = pe.matmul(ps[:, o, :], wqkv[:, kk, part * D + f * P:part * D + (f + 1) * P],
                                          xnT[:, kk, :], start=kk == 0, stop=kk == KT - 1)
                        m.then_inc(filled, 1)
                for c in range(TT):
                    o = bank()
                    for kk in range(KT):
                        m = pe.matmul(ps[:, o, :], xnT[:, kk, c * P:(c + 1) * P], wqkv[:, kk, D:3 * D],
                                      start=kk == 0, stop=kk == KT - 1)
                    m.then_inc(filled, 1)

                def scores(c):
                    for f in range(KT):
                        if c == 0:
                            pe.wait_ge(q_wide, b * KT * HT + (f + 1) * HT)
                        for half in range(2):
                            o = bank()
                            pe.matmul(ps[:, o, :], kT[:, f, c * P:(c + 1) * P],
                                      qwide[:, f, 4 * half:4 * half + 4, c * P:(c + 1) * P],
                                      start=True, stop=True).then_inc(filled, 1)

                def states(c):
                    for f in range(KT):
                        o = bank()
                        pe.matmul(ps[:, o, 0:P], kd[:, c, f * P:(f + 1) * P],
                                  v_of(c, f), start=True, stop=True).then_inc(filled, 1)

                def output(c):
                    pe.wait_ge(drained, start + probs_item[c])
                    if c == 1:
                        pe.wait_ge(q_decayed, b + 1)
                    o = bank()
                    for f in range(KT):
                        pe.matmul(ps[:, o, f * P:(f + 1) * P], past_bd[:, f, :], qT[:, f, c * P:(c + 1) * P],
                                  start=f == 0, stop=False, skip_group_check=True)
                        if c:
                            pe.matmul(ps[:, o, f * P:(f + 1) * P], state[:, c, f, :], qg[:, f, c * P:(c + 1) * P],
                                      start=False, stop=False, skip_group_check=True)
                    for f in range(KT):
                        for odd in range(2):
                            for pair in range(HT // 2):
                                h = f * HT + 2 * pair + odd
                                m = pe.matmul(ps[32 * pair:32 * (pair + 1), o, f * P:(f + 1) * P],
                                              vz[:, c, h // 2, 2 * odd:2 * odd + 2, :].rearrange("p x d -> p (x d)"),
                                              probs[:, c % 2, h, :], start=False,
                                              stop=f == KT - 1 and odd == 1 and pair == HT // 2 - 1,
                                              tile_position=(0, 32 * pair), skip_group_check=True)
                    m.then_inc(filled, 1)

                probs_item = [14, 20, 27, 34]
                pe.wait_ge(drained, start + 10)
                scores(0)
                for c in range(1, TT):
                    scores(c)
                    if c == 1 and not (isinstance(b, int) and b == 0):
                        turn_y(b - 1)
                    states(c - 1)
                    output(c - 1)
                output(TT - 1)
                assert k[0] == R_ITEMS

            batch(0)
            with pe.Fori(1, B - 1) as b:
                batch(b)
            batch(B - 1)
            stats(B - 1)
            turn_y(B - 1)

        @block.scalar
        def _(act):
            def root(n):
                act.wait_ge(var_ready, n)
                nc.scalar.activation(std[:], var[:], ACT.Sqrt).then_inc(std_ready, 1)

            def widen(b, f):
                act.wait_ge(drained, b * R_ITEMS + (KT + f + 1))
                for h in range(HT):
                    ins = nc.scalar.activation(qwide[:, f, h, :], qT[:, f, :], ACT.Copy, scale=headmask[:, h:h + 1])
                    ins.then_inc(q_wide, 1)

            root(1)
            act.wait_ge(consts, 16 * NCONST)
            widen(0, 0)
            widen(0, 1)
            root(2)
            with act.Fori(1, B - 1) as b:
                widen(b, 0)
                root(3 * b)
                widen(b, 1)
                root(3 * b + 1)
                root(3 * b + 2)
            widen(B - 1, 0)
            root(3 * B - 3)
            widen(B - 1, 1)
            root(3 * B - 2)
            root(3 * B - 1)
            root(3 * B)

        @block.gpsimd
        def _(pool):
            nc.gpsimd.memset(vz[:], 0.0).then_inc(vz_zero, 1)
            pool.wait_ge(consts, 16 * NCONST)

            def decay_q(b):
                pool.wait_ge(drained, b * R_ITEMS + 4)
                qd = qdecay[:].unsqueeze(2).broadcast_to([P, KT, TT, P])
                nc.gpsimd.tensor_tensor(qg[:].rearrange("p k (c t) -> p k c t", c=TT),
                                        qT[:].rearrange("p k (c t) -> p k c t", c=TT), qd,
                                        ALU.mult).then_inc(q_decayed, 1)

            def group_norm(b):
                pool.wait_ge(affine_ready, b + 1)
                nc.gpsimd.tensor_tensor(pool_carrier[:], ga[:], gbm[:], ALU.add)
                for f in range(KT):
                    nc.gpsimd.tensor_scalar(y[:, f, :], rT[:, f, :], ga[:, f:f + 1], gbm[:, f:f + 1],
                                            ALU.mult, ALU.add).then_inc(y_ready, 1)

            decay_q(0)
            with pool.Fori(1, B) as b:
                decay_q(b)
                group_norm(b - 1)
            group_norm(B - 1)

        @block.vector
        def _(dve):
            steps = [0]
            base = [0]

            def link(ins):
                steps[0] += 1
                ins.then_inc(link_r, 1)
                dve.wait_ge(link_r, base[0] + steps[0])

            def carry_wait():
                nc.vector.memset(carrier[:], 0.0)

            def row_moments(b):
                for t in range(TT):
                    ins = nc.vector.bn_stats(bst[:, t, :], x_all[:, bass.ds(b * TT + t, 1), :].rearrange("p o d -> p (o d)"))
                link(ins)
                carry_wait()
                for t in range(TT):
                    ins = nc.vector.bn_aggr(lmv[:, t, :], bst[:, t, :])
                link(ins)
                nc.vector.tensor_scalar(var[:], lmv[:, :, 1], EPS, None, ALU.add).then_inc(var_ready, 1)

            def normalise_moments(b):
                dve.wait_ge(x_loaded, b * 16 + 16)
                row_moments(b)

            def normalise(b, n):
                dve.wait_ge(std_ready, n)
                link(nc.vector.reciprocal(rstd[:], std[:]))
                for t in range(TT):
                    ins = nc.vector.tensor_scalar(xn[:, t, :], x_all[:, bass.ds(b * TT + t, 1), :].rearrange("p o d -> p (o d)"),
                                                  lmv[:, t, 0:1], rstd[:, t:t + 1], ALU.subtract, ALU.mult)
                ins.then_inc(xn_ready, 1)

            def second_moments(b):
                for half in range(2):
                    dve.wait_ge(y_filled, b * 2 + (half + 1))
                    xb = x_all[:, bass.ds(b * TT + 2 * half, 2), :]
                    nc.vector.tensor_tensor(xb, xb, ps[:, Y_BANKS[half], :].rearrange("p (t d) -> p t d", t=2),
                                            ALU.add).then_inc(x1_ready, 1)
                dve.wait_ge(x1_ready, b * 2 + 2)
                carry_wait()
                row_moments(b)

            def keep_second(b, n):
                out = ln2[:, bass.ts(b, TT), :]
                nc.vector.tensor_copy(out[:, :, 0], lmv[:, :, 0])
                dve.wait_ge(std_ready, n)
                link(nc.vector.reciprocal(out[:, :, 1], std[:]))

            def batch_moments(b):
                dve.wait_ge(drained, b * R_ITEMS + R_ITEMS)
                carry_wait()
                link(nc.vector.bn_aggr(rmv[:], rbst[:]))
                nc.vector.tensor_copy(rs2[:, 0:1], rmv[:, 0:1])
                nc.vector.scalar_tensor_tensor(out=rs2[:, 1:2], in0=rmv[:, 0:1], scalar=rmv[:, 0:1],
                                               in1=rmv[:, 1:2], op0=ALU.mult, op1=ALU.add).then_inc(stats_ready, 1)

            def batch_variance(b):
                dve.wait_ge(stats_filled, b + 1)
                link(nc.vector.tensor_copy(gs2[:], ps[:, R_BANKS, 0:2]))
                link(nc.vector.tensor_scalar(rmv[:, 0:1], gs2[:, 0:1], gs2[:, 0:1], None, ALU.mult))
                link(nc.vector.tensor_scalar(rmv[:, 1:2], gs2[:, 1:2], rmv[:, 0:1], EPS, ALU.subtract, ALU.add))
                nc.vector.tensor_copy(var[:], rmv[:, 1:2].broadcast_to([P, TT])).then_inc(var_ready, 1)

            def batch_affine(n):
                dve.wait_ge(std_ready, n)
                link(nc.vector.reciprocal(rstd[:], std[:]))
                link(nc.vector.tensor_scalar(ga[:], gw[:], rstd[:, 0:1], None, ALU.mult))
                link(nc.vector.tensor_scalar(gbm[:], ga[:], gs2[:, 0:1], None, ALU.mult))
                nc.vector.tensor_tensor(gbm[:], gb[:], gbm[:], ALU.subtract).then_inc(affine_ready, 1)

            def batch(b, roots, first=False, last=False):
                k = [0]
                start = b * R_ITEMS

                def item():
                    dve.wait_ge(filled, start + (k[0] + 1))
                    k[0] += 1
                    return (k[0] - 1) % R_BANKS

                for f in range(KT):
                    nc.vector.tensor_copy(xnT[:, f, :], ps[:, item(), :]).then_inc(drained, 1)
                if not first:
                    batch_moments(b - 1)
                for dst in (qT, kT):
                    for f in range(KT):
                        nc.vector.tensor_copy(dst[:, f, :], ps[:, item(), :]).then_inc(drained, 1)
                    if dst is qT and not first:
                        batch_variance(b - 1)
                for c in range(TT):
                    o = item()
                    nc.vector.tensor_tensor(kd[:, c, :], ps[:, o, 0:D], kscale[:], ALU.mult)
                    nc.vector.tensor_copy(vz[:, c, :, 0:4:3, :], ps[:, o, D:2 * D].rearrange(
                        "p (h x d) -> p h x d", x=2, d=HD)).then_inc(drained, 1)
                    if c == 1 and not first:
                        batch_affine(roots + 1)

                def scores(c):
                    for f in range(KT):
                        for half in range(2):
                            h = f * HT + half * 4
                            nc.vector.tensor_tensor(probs[:, c % 2, h:h + 4, :],
                                                    ps[:, item(), :].rearrange("p (h t) -> p h t", h=4),
                                                    decay[:, h:h + 4, :], ALU.mult).then_inc(drained, 1)

                def states(c):
                    for f in range(KT):
                        o = item()
                        if c == 0:
                            nc.vector.tensor_tensor(state[:, 1, f, :], ps[:, o, 0:P], blockmask[:],
                                                    ALU.mult).then_inc(drained, 1)
                        else:
                            link(nc.vector.tensor_tensor(stmp[:], ps[:, o, 0:P], blockmask[:], ALU.mult))
                            nc.vector.scalar_tensor_tensor(out=state[:, c + 1, f, :], in0=state[:, c, f, :],
                                                           scalar=chunkdecay[:, f:f + 1], in1=stmp[:],
                                                           op0=ALU.mult, op1=ALU.add).then_inc(drained, 1)
                            dve.wait_ge(drained, start + k[0])

                def output(c):
                    o = item()
                    nc.vector.tensor_copy(rT[:, :, c * P:(c + 1) * P],
                                          ps[:, o, 0:D].rearrange("p (f t) -> p f t", f=KT))
                    nc.vector.bn_stats(rbst[:, c, :], ps[:, o, 0:D]).then_inc(drained, 1)

                scores(0)
                scores(1)
                if not first:
                    second_moments(b - 1)
                states(0)
                output(0)
                if not first:
                    keep_second(b - 1, roots + 2)
                scores(2)
                if not last:
                    normalise_moments(b + 1)
                states(1)
                output(1)
                if not last:
                    normalise(b + 1, roots + (1 if first else 3))
                scores(3)
                states(2)
                output(2)
                output(3)
                assert k[0] == R_ITEMS

            dve.wait_ge(consts, 16 * NCONST)
            past_h = past[:].unsqueeze(2).broadcast_to([P, KT, HT, HD])
            mask_h = blockmask[:].rearrange("p (h e) -> p h e", h=HT).unsqueeze(1).broadcast_to([P, KT, HT, HD])
            for f in range(KT):
                ins = nc.vector.scalar_tensor_tensor(out=past_bd[:, f, :].rearrange("p (h e) -> p h e", h=HT),
                                                     in0=past_h[:, f], scalar=float(D), in1=mask_h[:, f],
                                                     op0=ALU.mult, op1=ALU.mult)
            ins.then_inc(past_ready, 1)
            dve.wait_ge(vz_zero, 1)
            normalise_moments(0)
            normalise(0, 1)
            batch(0, 1, first=True)
            base[0], steps[0] = steps[0], 0
            before = base[0]
            with dve.Fori(1, B - 1) as b:
                base[0] = (b - 1) * R_LINKS + before
                batch(b, 3 * b - 1)
            assert steps[0] == R_LINKS, steps[0]
            base[0], steps[0] = before + (B - 2) * R_LINKS, 0
            batch(B - 1, 3 * B - 4, last=True)
            batch_moments(B - 1)
            batch_variance(B - 1)
            batch_affine(3 * B - 1)
            second_moments(B - 1)
            keep_second(B - 1, 3 * B)



G = 4
GH = H // G
KPARTS = [0, 1, 0, 2, 0, 1]
QPARTS = [0, 0, 1, 0, 2, 1]
NB = len(KPARTS)
XR = NB * HD
MR = 3
FULL = S // 512
TAIL = S - FULL * 512
W_BANKS = 3
COLS = [(i * 512, w) for i, w in enumerate(widths(S, 512))]
V_RUNS = [(0, 2), (2, 2), (4, 2), (6, 2), (8, 2), (10, 1), (11, 1), (12, 1)]
SPLITS = KT + KT * len(COLS)


def next_group_items(g):
    out = []
    for j in range(GH):
        out += [("max", g, j, t, i) for t in range(TT) for i in range(FULL)] + [("tails", g, j)]
    return out


def projection_items():
    q = [("xnT", f) for f in range(KT)] + [("q", f) for f in range(KT)]
    k = [("k", f, i) for f in range(KT) for i in range(len(COLS))]
    v = [("v", i) for i in range(len(V_RUNS))]
    return q, k, v


def work_of(prev, following):
    plan = [[[] for _ in range(SC)] for _ in range(G)]
    q, k, v = projection_items()
    if prev:
        plan[0][1].append(("norm", G - 1))
        plan[0][3] += [("oT", 0), ("oT", 1)]
        plan[0][5].append(("wo", 0))
        plan[0][6].append(("wo", 1))
    if following:
        plan[0][7] += q[0:2]
        plan[0][9] += q[2:4]
        for n, item in enumerate(k):
            plan[1][n].append(item)
        for n, item in enumerate(v):
            plan[2][n + 1].append(item)
    for g in range(1, G):
        plan[g][1].append(("norm", g - 1))
    for g in range(G):
        if g < G - 1 or following:
            todo = next_group_items((g + 1) % G)
            for c in range(SC - 2):
                m = 5 if c < 8 else 4
                plan[g][c] += todo[:m]
                todo = todo[m:]
            assert not todo
            plan[g][SC - 2].append(("shift", (g + 1) % G))
    return plan


def order(plan):
    return [item for group in plan for chunk in group for item in chunk]


def prologue_items():
    q, k, v = projection_items()
    return q + k + v + next_group_items(0) + [("shift", 0)]


N_PRO = len(prologue_items())
N_FIRST = len(order(work_of(False, True)))
N_MID = len(order(work_of(True, True)))
PREV = N_MID - N_FIRST
X_LINKS = 22
S_ITEMS = 2 * SC * G


def cross_attention(nc, x_all, ln2, io):
    assert N_MID % W_BANKS == 0
    with ExitStack() as ctx:
        def sb(name, shape, dt=F32):
            return ctx.enter_context(nc.sbuf_tensor(name, shape, dt))

        def sem(name):
            return ctx.enter_context(nc.semaphore(name))

        ps = ctx.enter_context(nc.psum_tensor("x_ps", [P, 8, 512], F32))
        PV, WORK = 4, 5
        ident = sb("x_ident", [P, P])
        identb = sb("x_identb", [P, P], BF16)
        wq, wk, wv, wo = (sb("x_w" + n, [P, KT, D]) for n in "qkvo")
        bq, bk = sb("x_bq", [P, KT]), sb("x_bk", [P, KT])
        bv, bo = sb("x_bv", [P, D]), sb("x_bo", [P, D])
        kst = [sb(f"x_kst{g}", [XR + MR, GH, S], BF16) for g in range(G)]
        qst = [sb(f"x_qst{g}", [XR + MR, GH, T], BF16) for g in range(G)]
        vst = [sb(f"x_vst{g}", [P, SC, GH, HD + 1]) for g in range(G)]
        v_all = sb("x_v_all", [P, SC, D])
        ctxT = sb("x_ctxT", [P, KT, S])
        kp = sb("x_kp", [P, KT, 3, S], BF16)
        qp = sb("x_qp", [P, KT, 3, T], BF16)
        rest = sb("x_rest", [P, 2, 512])
        left = sb("x_left", [P, 512])
        probs = sb("x_probs", [P, 4, 2, T])
        ou = sb("x_ou", [P, T])
        o_all = sb("x_o_all", [P, TT, D])
        oT = sb("x_oT", [P, KT, T])
        otmp = ou[:].rearrange("p (n d) -> p n d", n=2)
        xn, xnT = o_all, oT
        mx = sb("x_mx", [P, GH, TT, FULL + 1])
        negm = sb("x_negm", [P, GH, TT])
        mres = sb("x_mres", [P, GH, TT])
        mparts = sb("x_mparts", [P, TT, GH, MR], BF16)
        mrows = sb("x_mrows", [GH * MR, T], BF16)
        rden = sb("x_rden", [P, TT, GH])
        k_dram = nc.dram_tensor("k_parts", [B, KT, 3, P, S], BF16, kind="Internal").ap()
        q_dram = nc.dram_tensor("q_parts", [B, KT, 3, P, T], BF16, kind="Internal").ap()

        consts, ctx_loaded, ones_set = sem("x_consts"), sem("ctx_loaded"), sem("ones_set")
        ones_loaded = sem("ones_loaded")
        filled, drained = sem("w_filled"), sem("w_drained")
        s_filled, exp_done, pv_used = sem("s_filled"), sem("exp_done"), sem("pv_used")
        pv_evac = sem("pv_evac")
        xn_ready, mparts_ready, m_loaded = sem("x_xn_ready"), sem("mparts_ready"), sem("m_loaded")
        split_step, split_done = sem("split_step"), sem("split_done")
        q_spilled, k_spilled = sem("q_spilled"), sem("k_spilled")
        v_ready = sem("v_ready")
        kq_loaded = [sem(f"kq_loaded{g}") for g in range(G)]
        link_x = sem("x_link")
        NCONST = 9
        KQ = 16 * 2 * NB

        plans = {"first": work_of(False, True), "mid": work_of(True, True), "last": work_of(True, False)}

        def start_of(b):
            return N_PRO if isinstance(b, int) and b == 0 else b * N_MID + N_PRO - PREV

        def bank_of(b, n):
            return WORK + ((N_PRO if isinstance(b, int) and b == 0 else N_PRO - PREV) + n) % W_BANKS

        def position(kind, item):
            return order(plans[kind]).index(item)

        block = ctx.enter_context(nc.Block())

        @block.sync
        def _(sp):
            for t, name in ((ident, "ident"), (bq, "bq"), (bk, "bk"), (bv, "bv"), (bo, "bo")):
                sp.dma_start(t[:], io[name]).then_inc(consts, 16)
            for t, name in ((wq, "wq"), (wk, "wk"), (wv, "wv"), (wo, "wo")):
                sp.dma_start(t[:], io[name].rearrange("(k p) n -> p k n", p=P)).then_inc(consts, 16)

            def load_ctx(b):
                sp.dma_start(ctxT[:], io["ctxT"][b].rearrange("(k p) c -> p k c", p=P)).then_inc(ctx_loaded, 16)

            def spill_q(b):
                sp.wait_ge(split_done, b * SPLITS + KT)
                sp.dma_start(q_dram[b].rearrange("k j p t -> p (k j) t"),
                             qp[:].rearrange("p k j t -> p (k j) t")).then_inc(q_spilled, 16)

            def spill_k(b):
                sp.wait_ge(split_done, b * SPLITS + SPLITS)
                sp.dma_start(k_dram[b].rearrange("k j p t -> p (k j) t"),
                             kp[:].rearrange("p k j t -> p (k j) t")).then_inc(k_spilled, 16)
                sp.wait_ge(q_spilled, b * 16 + 16)
                sp.wait_ge(k_spilled, b * 16 + 16)

            def load_group(b, g):
                f, lo = g // 2, (g % 2) * GH * HD
                for dst, src, parts in ((qst[g], q_dram, QPARTS), (kst[g], k_dram, KPARTS)):
                    for n, part in enumerate(parts):
                        sp.dma_start(dst[n * HD:(n + 1) * HD, :, :],
                                     src[b, f, part, lo:lo + GH * HD, :].rearrange("(j d) c -> d j c", d=HD)
                                     ).then_inc(kq_loaded[g], 16)

            def attended(b, g):
                sp.wait_ge(s_filled, b * S_ITEMS + (g + 1) * 2 * SC)

            def load_shift(b, g, done):
                sp.wait_ge(drained, done)
                for j in range(GH):
                    sp.dma_start(qst[g][XR:XR + MR, j, :], mrows[j * MR:(j + 1) * MR, :]).then_inc(m_loaded, 16)

            for g in range(G):
                sp.dma_start(kst[g][XR:XR + MR, :, :], io["ones_rows"]).then_inc(ones_loaded, 16)
            load_ctx(0)
            spill_q(0)
            spill_k(0)
            for g in range(G):
                load_group(0, g)
            load_shift(0, 0, N_PRO)

            def batch(b, kind):
                start = start_of(b)
                if kind != "last":
                    if kind == "first":
                        sp.wait_ge(drained, N_PRO)
                    else:
                        sp.wait_ge(drained, start - 1)
                    load_ctx(b + 1)
                if kind != "first":
                    attended(b - 1, G - 1)
                    load_group(b, G - 1)
                for g in range(G):
                    if kind != "last":
                        if g == 0:
                            spill_q(b + 1)
                        elif g == 1:
                            spill_k(b + 1)
                            load_group(b + 1, 0)
                        else:
                            attended(b, g - 1)
                            load_group(b + 1, g - 1)
                    if g < G - 1 or kind != "last":
                        load_shift(b, (g + 1) % G, start + (position(kind, ("shift", (g + 1) % G)) + 1))

            batch(0, "first")
            with sp.Fori(1, B - 1) as b:
                batch(b, "mid")
            batch(B - 1, "last")

        @block.tensor
        def _(pe):
            pe.wait_ge(consts, 16 * NCONST)
            pe.wait_ge(ones_set, 6)
            pe.wait_ge(ones_loaded, 16 * G)

            def work(item, bank, b, b1, at):
                o = ps[:, bank, :]
                kind = item[0]
                if kind == "xnT":
                    pe.wait_ge(xn_ready, b1 + 1)
                    for t in range(TT):
                        m = pe.transpose(o[:, t * P:(t + 1) * P], xn[:, t, item[1] * P:(item[1] + 1) * P], ident[:])
                elif kind == "q":
                    pe.wait_ge(drained, at(("xnT", 1)))
                    for kk in range(KT):
                        m = pe.matmul(o, wq[:, kk, item[1] * P:(item[1] + 1) * P], xnT[:, kk, :],
                                      start=kk == 0, stop=kk == KT - 1)
                elif kind == "k":
                    pe.wait_ge(ctx_loaded, b1 * 16 + 16)
                    c, w = COLS[item[2]]
                    for kk in range(KT):
                        m = pe.matmul(o[:, 0:w], wk[:, kk, item[1] * P:(item[1] + 1) * P], ctxT[:, kk, c:c + w],
                                      start=kk == 0, stop=kk == KT - 1)
                elif kind == "v":
                    c0, n = V_RUNS[item[1]]
                    for c in range(c0, c0 + n):
                        w = min(P, S - c * P)
                        for kk in range(KT):
                            m = pe.matmul(o[0:w, (c - c0) * D:(c - c0 + 1) * D], ctxT[:, kk, c * P:c * P + w],
                                          wv[:, kk, :], start=kk == 0, stop=kk == KT - 1)
                elif kind == "max":
                    _, g, j, t, i = item
                    m = pe.matmul(o, qst[g][0:XR, j, t * P:(t + 1) * P], kst[g][0:XR, j, i * 512:(i + 1) * 512],
                                  start=True, stop=True)
                elif kind == "tails":
                    _, g, j = item
                    for t in range(TT):
                        m = pe.matmul(o[:, t * TAIL:(t + 1) * TAIL], qst[g][0:XR, j, t * P:(t + 1) * P],
                                      kst[g][0:XR, j, FULL * 512:S], start=True, stop=True)
                elif kind == "shift":
                    for t in range(TT):
                        m = pe.matmul(o[0:GH * MR, t * P:(t + 1) * P], mparts[:, t, :, :], identb[:],
                                      start=True, stop=True)
                elif kind == "norm":
                    for t in range(TT):
                        m = pe.transpose(o[:, t * P:(t + 1) * P], ou[:, t * P:(t + 1) * P], ident[:])
                elif kind == "oT":
                    pe.wait_ge(drained, at(("norm", G - 1)))
                    for t in range(TT):
                        m = pe.transpose(o[:, t * P:(t + 1) * P], o_all[:, t, item[1] * P:(item[1] + 1) * P],
                                         ident[:])
                elif kind == "wo":
                    pe.wait_ge(drained, at(("oT", 1)))
                    for n in range(2):
                        t = 2 * item[1] + n
                        for kk in range(KT):
                            m = pe.matmul(o[:, n * D:(n + 1) * D], oT[:, kk, t * P:(t + 1) * P], wo[:, kk, :],
                                          start=kk == 0, stop=kk == KT - 1)
                m.then_inc(filled, 1)

            for n, item in enumerate(prologue_items()):
                if n >= W_BANKS:
                    pe.wait_ge(drained, n - W_BANKS + 1)
                if item == ("max", 0, 0, 0, 0):
                    pe.wait_ge(kq_loaded[0], KQ)
                if item == ("shift", 0):
                    pe.wait_ge(mparts_ready, 1)
                work(item, WORK + n % W_BANKS, 0, 0, lambda i: prologue_items().index(i) + 1)

            def batch(b, kind):
                start = start_of(b)
                plan = plans[kind]
                k = [0]

                def values(g, q):
                    if q == 0:
                        if not (kind == "first" and g == 0):
                            pe.wait_ge(pv_evac, b * G + g)
                        pe.wait_ge(v_ready, b * 2 * G + 2 * (g + 1))
                    pe.wait_ge(exp_done, b * S_ITEMS + (g * 2 * SC + 2 * (q + 1)))
                    w = min(P, S - q * P)
                    for j in range(GH):
                        slot = (g * 2 * SC + 2 * q + j // 2) % 4
                        m = pe.matmul(ps[32 * j:32 * j + HD + 1, PV, :], vst[g][0:w, q, j, :],
                                      probs[0:w, slot, j % 2, :], start=q == 0, stop=q == SC - 1)
                    m.then_inc(pv_used, 1)

                def fill(g, items):
                    for item in items:
                        nxt = (g + 1) % G
                        if item == ("max", nxt, 0, 0, 0):
                            pe.wait_ge(kq_loaded[nxt], (b + (g == G - 1)) * KQ + KQ)
                        if item[0] == "shift":
                            pe.wait_ge(mparts_ready, b * G + (g + 2))
                        if item[0] == "norm":
                            pe.wait_ge(pv_evac, b * G + g)
                        pe.wait_ge(drained, start + (k[0] - W_BANKS + 1))
                        work(item, bank_of(b, k[0]), b, b + 1, lambda i: start + (position(kind, i) + 1))
                        k[0] += 1

                for g in range(G):
                    pe.wait_ge(m_loaded, b * 16 * GH * G + 16 * GH * (g + 1))
                    for c in range(SC):
                        w = min(P, S - c * P)
                        for pair in range(2):
                            n = g * 2 * SC + 2 * c + pair
                            if not (kind == "first" and n < 2):
                                pe.wait_ge(exp_done, b * S_ITEMS + (n - 1))
                            for h in range(2):
                                m = pe.matmul(ps[0:w, 2 * (n % 2) + h, :], kst[g][:, 2 * pair + h, c * P:c * P + w],
                                              qst[g][:, 2 * pair + h, :], start=True, stop=True)
                            m.then_inc(s_filled, 1)
                            fill(g, plan[g][c][0:2] if pair == 0 else plan[g][c][2:3])
                        if c:
                            values(g, c - 1)
                        fill(g, plan[g][c][3:])
                    values(g, SC - 1)

            batch(0, "first")
            with pe.Fori(1, B - 1) as b:
                batch(b, "mid")
            batch(B - 1, "last")
            n = start_of(B - 1) + len(order(plans["last"]))
            end = [("norm", G - 1), ("oT", 0), ("oT", 1), ("wo", 0), ("wo", 1)]
            pe.wait_ge(pv_evac, B * G)
            for i, item in enumerate(end):
                pe.wait_ge(drained, n + i - W_BANKS + 1)
                work(item, WORK + (n + i) % W_BANKS, B - 1, B, lambda it: n + end.index(it) + 1)

        @block.scalar
        def _(act):
            def batch(b, kind):
                for g in range(G):
                    for c in range(SC):
                        w = min(P, S - c * P)
                        for pair in range(2):
                            n = g * 2 * SC + 2 * c + pair
                            act.wait_ge(s_filled, b * S_ITEMS + (n + 1))
                            if not (kind == "first" and n // 2 < 2):
                                act.wait_ge(pv_used, b * (S_ITEMS // 2) + (n // 2 - 1))
                            nc.scalar.activation(probs[0:w, n % 4, :, :], ps[0:w, 2 * (n % 2):2 * (n % 2) + 2, :],
                                                 ACT.Exp, scale=HD ** -0.5).then_inc(exp_done, 1)

            batch(0, "first")
            with act.Fori(1, B) as b:
                batch(b, "mid")

        @block.gpsimd
        def _(pool):
            for g in range(G):
                nc.gpsimd.memset(vst[g][:], 1.0).then_inc(ones_set, 1)
            pool.wait_ge(consts, 16 * NCONST)
            nc.gpsimd.tensor_copy(identb[:], ident[:]).then_inc(ones_set, 1)

            def split(dst, n, count, w):
                pool.wait_ge(drained, count)
                whole = rest[:, n[1] % 2, 0:w]
                nc.gpsimd.tensor_tensor(dst(1), whole, dst(0), ALU.subtract)
                nc.gpsimd.tensor_tensor(left[:, 0:w], whole, dst(0), ALU.subtract).then_inc(split_step, 1)
                pool.wait_ge(split_step, n[0] + (n[1] + 1))
                nc.gpsimd.tensor_tensor(dst(2), left[:, 0:w], dst(1), ALU.subtract).then_inc(split_done, 1)
                pool.wait_ge(split_done, n[0] + (n[1] + 1))

            def splits(b1, at, part):
                if part == "q":
                    for f in range(KT):
                        split(lambda j: qp[:, f, j, :], (b1 * SPLITS, f), at(("q", f)), T)
                else:
                    for f in range(KT):
                        for i, (c, w) in enumerate(COLS):
                            split(lambda j: kp[:, f, j, c:c + w], (b1 * SPLITS, KT + f * len(COLS) + i),
                                  at(("k", f, i)), w)

            def place_v(g):
                for rows, lo, hi in ((P, 0, SC - 1), (S - (SC - 1) * P, SC - 1, SC)):
                    cols = slice(g * GH * HD, (g + 1) * GH * HD)
                    nc.gpsimd.tensor_tensor(
                        vst[g][0:rows, lo:hi, :, 0:HD],
                        v_all[0:rows, lo:hi, cols].rearrange("p c (j d) -> p c j d", d=HD),
                        bv[0:rows, cols].rearrange("p (j d) -> p j d", d=HD).unsqueeze(1).broadcast_to(
                            [rows, hi - lo, GH, HD]), ALU.add).then_inc(v_ready, 1)

            pool.wait_ge(ones_set, 6)
            at0 = lambda i: prologue_items().index(i) + 1
            splits(0, at0, "q")
            splits(0, at0, "k")
            pool.wait_ge(drained, at0(("v", len(V_RUNS) - 1)))
            for g in range(G):
                place_v(g)

            def batch(b, kind):
                start = start_of(b)
                at = lambda i: start + (position(kind, i) + 1)
                if kind != "first":
                    pool.wait_ge(pv_used, b * (S_ITEMS // 2))
                    place_v(G - 1)
                if kind != "last":
                    splits(b + 1, at, "q")
                    splits(b + 1, at, "k")
                    pool.wait_ge(drained, at(("v", len(V_RUNS) - 1)))
                    for g in range(G - 1):
                        pool.wait_ge(pv_used, b * (S_ITEMS // 2) + SC * (g + 1))
                        place_v(g)

            batch(0, "first")
            with pool.Fori(1, B - 1) as b:
                batch(b, "mid")
            batch(B - 1, "last")

        @block.vector
        def _(dve):
            steps, base = [0], [0]

            def link(ins):
                steps[0] += 1
                ins.then_inc(link_x, 1)
                dve.wait_ge(link_x, base[0] + steps[0])

            def normalise(b):
                for t in range(TT):
                    row = bass.ds(b * TT + t, 1)
                    ins = nc.vector.tensor_scalar(
                        xn[:, t, :], x_all[:, row, :].rearrange("p o d -> p (o d)"),
                        ln2[:, row, 0:1].rearrange("p o d -> p (o d)"), ln2[:, row, 1:2].rearrange("p o d -> p (o d)"),
                        ALU.subtract, ALU.mult)
                ins.then_inc(xn_ready, 1)

            def first_part(o, dst, bias, n, b1, w):
                nc.vector.tensor_scalar(dst, o[:, 0:w], bias, None, ALU.add)
                if not (isinstance(b1, int) and b1 == 0 and n < 2):
                    dve.wait_ge(split_done, b1 * SPLITS + (n - 1))
                return nc.vector.tensor_scalar(rest[:, n % 2, 0:w], o[:, 0:w], bias, None, ALU.add)

            def shift_parts(count):
                dve.wait_ge(drained, count)
                link(nc.vector.tensor_reduce(out=negm[:], in_=mx[:], axis=AX.X, op=ALU.max, negate=True))
                rows, rem = (v[:].rearrange("p j t -> p t j") for v in (negm, mres))
                link(nc.vector.tensor_copy(mparts[:, :, :, 0], rows))
                link(nc.vector.tensor_tensor(rem, rows, mparts[:, :, :, 0], ALU.subtract))
                link(nc.vector.tensor_copy(mparts[:, :, :, 1], rem))
                nc.vector.tensor_tensor(mparts[:, :, :, 2], rem, mparts[:, :, :, 1],
                                        ALU.subtract).then_inc(mparts_ready, 1)

            def work(item, bank, b, b1, count, shifts):
                o = ps[:, bank, :]
                kind = item[0]
                if kind == "shift":
                    shift_parts(count - 1)
                dve.wait_ge(filled, count)
                if kind == "xnT":
                    ins = nc.vector.tensor_copy(xnT[:, item[1], :], o)
                elif kind == "q":
                    f = item[1]
                    if f == 0 and not (isinstance(b1, int) and b1 == 0):
                        dve.wait_ge(q_spilled, b1 * 16)
                    ins = first_part(o, qp[:, f, 0, :], bq[:, f:f + 1], f, b1, T)
                elif kind == "k":
                    _, f, i = item
                    c, w = COLS[i]
                    if f == 0 and i == 0 and not (isinstance(b1, int) and b1 == 0):
                        dve.wait_ge(k_spilled, b1 * 16)
                    ins = first_part(o, kp[:, f, 0, c:c + w], bk[:, f:f + 1], KT + f * len(COLS) + i, b1, w)
                elif kind == "v":
                    c0, n = V_RUNS[item[1]]
                    w = min(P, S - c0 * P)
                    if c0 == 0 and not (isinstance(b1, int) and b1 == 0):
                        dve.wait_ge(v_ready, b1 * 2 * G)
                    ins = nc.vector.tensor_copy(v_all[0:w, c0:c0 + n, :],
                                                o[0:w, 0:n * D].rearrange("p (c d) -> p c d", c=n))
                elif kind == "max":
                    _, g, j, t, i = item
                    ins = nc.vector.tensor_reduce(out=mx[:, j, t, i:i + 1], in_=o, axis=AX.X, op=ALU.max)
                elif kind == "tails":
                    _, g, j = item
                    ins = nc.vector.tensor_reduce(out=mx[:, j, :, FULL], in_=o[:, 0:TT * TAIL].rearrange("p (t c) -> p t c", t=TT),
                                                  axis=AX.X, op=ALU.max)
                elif kind == "shift":
                    if not (isinstance(shifts, int) and shifts == 0):
                        dve.wait_ge(m_loaded, shifts * 16 * GH)
                    ins = nc.vector.tensor_copy(mrows[:], o[0:GH * MR, :])
                elif kind == "norm":
                    g = item[1]
                    o4 = o.rearrange("p (t j e) -> p t j e", t=TT, j=GH)
                    link(nc.vector.reciprocal(rden[:], o4[:, :, :, HD]))
                    ins = nc.vector.tensor_tensor(
                        o_all[:, :, g * GH * HD:(g + 1) * GH * HD].rearrange("p t (j d) -> p t j d", d=HD),
                        o4[:, :, :, 0:HD], rden[:].unsqueeze(3).broadcast_to([P, TT, GH, HD]), ALU.mult)
                elif kind == "oT":
                    ins = nc.vector.tensor_copy(oT[:, item[1], :], o)
                elif kind == "wo":
                    link(nc.vector.tensor_tensor(otmp, o.rearrange("p (n d) -> p n d", n=2),
                                                 bo[:].unsqueeze(1).broadcast_to([P, 2, D]), ALU.add))
                    xb = x_all[:, bass.ds((b1 - 2) * TT + 2 * item[1], 2), :]
                    ins = nc.vector.tensor_tensor(xb, xb, otmp, ALU.add)
                ins.then_inc(drained, 1)
                if kind == "wo":
                    dve.wait_ge(drained, count)

            dve.wait_ge(consts, 16 * NCONST)
            nc.vector.memset(ps[:, PV, :], 0.0).then_inc(ones_set, 1)
            normalise(0)
            for n, item in enumerate(prologue_items()):
                work(item, WORK + n % W_BANKS, 0, 0, n + 1, 0)

            def evacuate(groups):
                dve.wait_ge(pv_used, groups)
                return nc.vector.tensor_copy(ou[:], ps[:, PV, :]).then_inc(pv_evac, 1)

            def batch(b, kind):
                start = start_of(b)
                plan = plans[kind]
                k = 0
                for g in range(G):
                    if not (kind == "first" and g == 0):
                        evacuate(b * (S_ITEMS // 2) + g * SC)
                    for c in range(SC):
                        if g == 0 and c == 5 and kind != "last":
                            normalise(b + 1)
                        for item in plan[g][c]:
                            work(item, bank_of(b, k), b, b + 1, start + (k + 1), b * G + (g + 1))
                            k += 1

            batch(0, "first")
            before = steps[0]
            steps[0] = 0
            with dve.Fori(1, B - 1) as b:
                base[0] = (b - 1) * X_LINKS + before
                batch(b, "mid")
            assert steps[0] == X_LINKS, steps[0]
            base[0], steps[0] = before + (B - 2) * X_LINKS, 0
            batch(B - 1, "last")
            evacuate(B * (S_ITEMS // 2))
            n = start_of(B - 1) + len(order(plans["last"]))
            for i, item in enumerate([("norm", G - 1), ("oT", 0), ("oT", 1), ("wo", 0), ("wo", 1)]):
                work(item, WORK + (n + i) % W_BANKS, B - 1, B + 1, n + i + 1, 0)



E = 8
TOPK = 2
HID = E + 2
NG = NT // TT
UNCHOSEN = -1e30
F_BANKS = 3
HID_RING = 2
LEAD = 2
ORDER = [E, E + 1] + list(range(E))


def feed_forward(nc, x_all, io, out):
    with ExitStack() as ctx:
        def sb(name, shape, dt=F32):
            return ctx.enter_context(nc.sbuf_tensor(name, shape, dt))

        def sem(name):
            return ctx.enter_context(nc.semaphore(name))

        ps = ctx.enter_context(nc.psum_tensor("f_ps", [P, 8, 512], F32))
        GATE, UP, DOWN = 0, 2, 4
        ident = sb("f_ident", [P, P])
        identb = sb("f_identb", [P, P], BF16)
        ones = sb("f_ones", [P, P])
        pickb = sb("f_pickb", [E, E * P], BF16)
        gate_w = sb("f_gate_w", [P, KT, E])
        lb = sb("f_lb", [P, E])
        raw = sb("f_raw", [P, KT, HID * P])
        wg = [sb(f"f_wg{part}", [P, KT, HID * P], F32R) for part in ("_rounded", "_rest")]
        wu = [sb(f"f_wu{part}", [P, KT, HID * P], F32R) for part in ("_rounded", "_rest")]
        wd_raw = raw[:].rearrange("p k n -> p (k n)").rearrange("p (j d) -> p j d", j=HID)
        wd = [sb(f"f_wd{part}", [P, HID, D], F32R) for part in ("_rounded", "_rest")]
        bst = sb("f_bst", [P, NT, 6])
        mv = sb("f_mv", [P, NT, 2])
        var = sb("f_var", [P, NT])
        std = sb("f_std", [P, NT])
        rstd = sb("f_rstd", [P, NT])
        xn = sb("f_xn", [P, 2, TT, D])
        xs = sb("f_xs", [P, 2, KT, T])
        xnT = [sb(f"f_xnT{part}", [P, KT, NT * P], F32R) for part in ("_rounded", "_rest")]
        logits = sb("f_logits", [P, NT, E])
        score = sb("f_score", [P, NT, E])
        better = sb("f_better", [P, NT, E])
        cmp = logits
        chosen = sb("f_chosen", [P, NT, E])
        total = sb("f_total", [P, NT])
        sums = sb("f_sums", [P, 2 * E])
        wmean = sb("f_wmean", [P, 2 * E])
        off = sb("f_off", [P, NT, E], BF16)
        offT = sb("f_offT", [E, NT * P], BF16)
        hid = [sb(f"f_hid{part}", [P, HID_RING, T], F32R) for part in ("_rounded", "_rest")]

        def silu_of(j):
            return xs[:, j % 2, 0, :]

        def hid_whole(s):
            return xn[:, s // 2, (s % 2) * 2:(s % 2) * 2 + 2, :].rearrange("p t d -> p (t d)")

        consts = sem("f_consts")
        filled, drained = sem("f_filled"), sem("f_drained")
        var_ready, std_ready, xn_ready, xnT_rounded = sem("f_var"), sem("f_std"), sem("f_xn_ready"), sem("xnT_rounded")
        logits_ready, score_ready, sums_ready, off_ready = (sem("logits_ready"), sem("score_ready"),
                                                            sem("sums_ready"), sem("off_ready"))
        xnT_split = sem("xnT_split")
        w_loaded, w_rounded, w_split, wd_scaled = sem("w_loaded"), sem("w_rounded"), sem("w_split"), sem("wd_scaled")
        hid_rounded, hid_split, hid_used = sem("hid_rounded"), sem("hid_split"), sem("hid_used")
        gate_filled, up_filled, silu_done, hid_done = (sem("gate_filled"), sem("up_filled"), sem("silu_done"),
                                                       sem("hid_done"))
        down_filled, down_drained, stored = sem("down_filled"), sem("down_drained"), sem("f_stored")
        link_f = sem("f_link")
        NCONST = 6
        ROUTE = 6 * (NG // 2)

        block = ctx.enter_context(nc.Block())

        @block.sync
        def _(sp):
            for t, name in ((ident, "ident"), (lb, "lb"), (ones, "ones"), (identb, "identb"), (pickb, "pickb")):
                sp.dma_start(t[:], io[name]).then_inc(consts, 16)
            sp.dma_start(gate_w[:], io["gate_w"].rearrange("(k p) n -> p k n", p=P)).then_inc(consts, 16)
            sp.dma_start(raw[:], io["wg"].rearrange("(k p) n -> p k n", p=P)).then_inc(w_loaded, 16)
            sp.wait_ge(w_split, 1)
            sp.dma_start(raw[:], io["wu"].rearrange("(k p) n -> p k n", p=P)).then_inc(w_loaded, 16)
            sp.wait_ge(w_split, 2)
            sp.dma_start(wd_raw, io["wd"].rearrange("(k p) n -> p k n", p=P)).then_inc(w_loaded, 16)
            with sp.Fori(0, NG) as n:
                sp.wait_ge(down_drained, n * TT + TT)
                sp.dma_start(out[n].rearrange("(t p) d -> p t d", p=P), x_all[:, bass.ts(n, TT), :]).then_inc(stored, 16)
            sp.wait_ge(stored, 16 * NG)

        @block.tensor
        def _(pe):
            pe.wait_ge(consts, 16 * NCONST)

            def pair(i, first):
                k = 0

                def bank():
                    nonlocal k
                    if not (first and k < F_BANKS):
                        pe.wait_ge(drained, i * 6 + (k - F_BANKS + 1))
                    k += 1
                    return (k - 1) % F_BANKS

                for u in range(2):
                    pe.wait_ge(xn_ready, i * 2 + (u + 1))
                    for f in range(KT):
                        o = bank()
                        for t in range(TT):
                            m = pe.transpose(ps[:, o, t * P:(t + 1) * P], xn[:, u, t, f * P:(f + 1) * P], ident[:])
                        m.then_inc(filled, 1)
                for u in range(2):
                    pe.wait_ge(drained, i * 6 + 2 * (u + 1))
                    o = bank()
                    for t in range(TT):
                        for kk in range(KT):
                            m = pe.matmul(ps[:, o, t * E:(t + 1) * E], xs[:, u, kk, t * P:(t + 1) * P],
                                          gate_w[:, kk, :], start=kk == 0, stop=kk == KT - 1)
                    m.then_inc(filled, 1)

            pair(0, True)
            with pe.Fori(1, NG // 2) as i:
                pair(i, False)

            pe.wait_ge(xnT_split, NG * KT)
            pe.wait_ge(w_split, 2)
            pe.wait_ge(drained, ROUTE)

            def split_product(out_, lhs, rhs, last):
                passes = [(1, 0), (0, 1), (0, 0)]
                for n_, (l, r) in enumerate(passes):
                    for kk in range(KT):
                        m = pe.matmul(out_, lhs(l, kk), rhs(r, kk), start=n_ == 0 and kk == 0,
                                      stop=last and n_ == 2 and kk == KT - 1)
                return m

            def gate_up(n, pos, first):
                j = ORDER[pos]
                cols = bass.ts(n, T)
                if not (first and pos < 2):
                    pe.wait_ge(silu_done, n * HID + (pos - 1))
                m = split_product(ps[:, GATE + pos % 2, :], lambda part, kk: wg[part][:, kk, j * P:(j + 1) * P],
                                  lambda part, kk: xnT[part][:, kk, cols], j >= E)
                if j < E:
                    m = pe.matmul(ps[:, GATE + pos % 2, :], pickb[:, j * P:(j + 1) * P], offT[:, cols],
                                  start=False, stop=True)
                m.then_inc(gate_filled, 1)
                if not (first and pos < 2):
                    pe.wait_ge(hid_done, n * HID + (pos - 1))
                split_product(ps[:, UP + pos % 2, :], lambda part, kk: wu[part][:, kk, j * P:(j + 1) * P],
                              lambda part, kk: xnT[part][:, kk, cols], True).then_inc(up_filled, 1)

            def down(n, pos, first):
                j = ORDER[pos]
                slot = pos % HID_RING
                pe.wait_ge(hid_split, n * HID + (pos + 1))
                for t in range(TT):
                    if pos == 0 and not first:
                        pe.wait_ge(down_drained, n * TT + (t + 1 - TT))
                    for n_, (l, r) in enumerate([(1, 0), (0, 1), (0, 0)]):
                        m = pe.matmul(ps[:, DOWN + t, 0:D], hid[l][:, slot, t * P:(t + 1) * P], wd[r][:, j, :],
                                      start=pos == 0 and n_ == 0, stop=pos == HID - 1 and n_ == 2)
                    if pos == HID - 1 and t < TT - 1:
                        m.then_inc(down_filled, 1)
                m.then_inc(hid_used, 1)

            for pos in range(LEAD):
                gate_up(0, pos, True)
            pe.wait_ge(sums_ready, 1)
            pe.matmul(ps[:, DOWN, 0:2 * E], ones[:], sums[:], start=True, stop=True).then_inc(filled, 1)
            pe.wait_ge(off_ready, 1)
            for n in range(NG):
                if n >= TT - 1:
                    pe.wait_ge(drained, ROUTE + 1 + n - TT + 1)
                for t in range(TT):
                    m = pe.matmul(ps[0:E, DOWN + (n + 1) % TT, t * P:(t + 1) * P], off[:, n * TT + t, :], identb[:],
                                  start=True, stop=True)
                m.then_inc(filled, 1)
            pe.wait_ge(drained, ROUTE + 1 + NG)

            def tokens(n, first):
                for pos in range(LEAD if first else 0, HID):
                    gate_up(n, pos, first)
                    if pos == LEAD and first:
                        pe.wait_ge(w_split, 3)
                    if pos >= LEAD:
                        down(n, pos - LEAD, first)
                    elif not first:
                        down(n - 1, HID - LEAD + pos, first)

            tokens(0, True)
            with pe.Fori(1, NG) as n:
                tokens(n, False)
            for pos in range(HID - LEAD, HID):
                down(NG - 1, pos, False)

        @block.scalar
        def _(act):
            act.wait_ge(consts, 16 * NCONST)
            act.wait_ge(var_ready, 1)
            nc.scalar.activation(std[:], var[:], ACT.Sqrt).then_inc(std_ready, 1)
            for n, w in enumerate((wg, wu)):
                act.wait_ge(w_loaded, 16 * (n + 1))
                nc.scalar.activation(w[0][:], raw[:], ACT.Copy).then_inc(w_rounded, 1)
            with act.Fori(0, NG // 2) as i:
                for u in range(2):
                    act.wait_ge(drained, i * 6 + 2 * (u + 1))
                    for f in range(KT):
                        nc.scalar.activation(xnT[0][:, f, bass.ds(i * 2 * T + u * T, T)], xs[:, u, f, :],
                                             ACT.Copy).then_inc(xnT_rounded, 1)
            act.wait_ge(logits_ready, 1)
            nc.scalar.activation(score[:], logits[:], ACT.Sigmoid).then_inc(score_ready, 1)

            def silu(n, pos, first):
                act.wait_ge(gate_filled, n * HID + (pos + 1))
                if not (first and pos < 2):
                    act.wait_ge(hid_done, n * HID + (pos - 1))
                nc.scalar.activation(silu_of(pos), ps[:, GATE + pos % 2, :], ACT.Silu).then_inc(silu_done, 1)

            def round_hid(n, pos, first):
                act.wait_ge(hid_done, n * HID + (pos + 1))
                if not (first and pos < HID_RING):
                    act.wait_ge(hid_used, n * HID + (pos + 1 - HID_RING))
                nc.scalar.activation(hid[0][:, pos % HID_RING, :], hid_whole(pos % HID_RING),
                                     ACT.Copy).then_inc(hid_rounded, 1)

            silu(0, 0, True)
            for pos in range(1, HID):
                silu(0, pos, True)
                if pos == 1:
                    act.wait_ge(wd_scaled, 1)
                    nc.scalar.activation(wd[0][:], wd_raw, ACT.Copy).then_inc(w_rounded, 1)
                round_hid(0, pos - 1, True)
            with act.Fori(1, NG) as n:
                for pos in range(HID):
                    silu(n, pos, False)
                    round_hid(n, pos - 1, False)
            round_hid(NG - 1, HID - 1, False)

        @block.gpsimd
        def _(pool):
            for n, w in enumerate((wg, wu)):
                pool.wait_ge(w_rounded, n + 1)
                nc.gpsimd.tensor_tensor(w[1][:], raw[:], w[0][:], ALU.subtract).then_inc(w_split, 1)
            with pool.Fori(0, NG // 2) as i:
                for u in range(2):
                    for f in range(KT):
                        pool.wait_ge(xnT_rounded, i * 2 * KT + (u * KT + f + 1))
                        cols = bass.ds(i * 2 * T + u * T, T)
                        nc.gpsimd.tensor_tensor(xnT[1][:, f, cols], xs[:, u, f, :], xnT[0][:, f, cols],
                                                ALU.subtract).then_inc(xnT_split, 1)

            def rest(n, pos):
                slot = pos % HID_RING
                pool.wait_ge(hid_rounded, n * HID + (pos + 1))
                nc.gpsimd.tensor_tensor(hid[1][:, slot, :], hid_whole(slot), hid[0][:, slot, :],
                                        ALU.subtract).then_inc(hid_split, 1)

            pool.wait_ge(w_rounded, 3)
            nc.gpsimd.tensor_tensor(wd[1][:], wd_raw, wd[0][:], ALU.subtract).then_inc(w_split, 1)
            for pos in range(HID):
                rest(0, pos)
            with pool.Fori(1, NG) as n:
                for pos in range(HID):
                    rest(n, pos)

        @block.vector
        def _(dve):
            steps = [0]

            def link(ins):
                steps[0] += 1
                ins.then_inc(link_f, 1)
                dve.wait_ge(link_f, steps[0])

            for t in range(NT):
                ins = nc.vector.bn_stats(bst[:, t, :], x_all[:, t, :])
            link(ins)
            for t in range(NT):
                ins = nc.vector.bn_aggr(mv[:, t, :], bst[:, t, :])
            link(ins)
            nc.vector.tensor_scalar(var[:], mv[:, :, 1], EPS, None, ALU.add).then_inc(var_ready, 1)
            dve.wait_ge(std_ready, 1)
            link(nc.vector.reciprocal(rstd[:], std[:]))
            dve.wait_ge(consts, 16 * NCONST)

            def pair(i, first):
                for u in range(2):
                    for t in range(TT):
                        row = bass.ds(i * 2 * TT + (u * TT + t), 1)
                        ins = nc.vector.tensor_scalar(
                            xn[:, u, t, :], x_all[:, row, :].rearrange("p o d -> p (o d)"),
                            mv[:, row, 0:1].rearrange("p o d -> p (o d)"), rstd[:, bass.ds(i * 2 * TT + (u * TT + t), 1)],
                            ALU.subtract, ALU.mult)
                    ins.then_inc(xn_ready, 1)
                for u in range(2):
                    for f in range(KT):
                        dve.wait_ge(filled, i * 6 + (2 * u + f + 1))
                        if not first:
                            dve.wait_ge(xnT_split, i * 2 * KT + (u * KT + f + 1 - 2 * KT))
                        nc.vector.tensor_copy(xs[:, u, f, :], ps[:, (2 * u + f) % F_BANKS, :]).then_inc(drained, 1)
                for u in range(2):
                    dve.wait_ge(filled, i * 6 + (4 + u + 1))
                    nc.vector.tensor_tensor(
                        logits[:, bass.ds(i * 2 * TT + u * TT, TT), :],
                        ps[:, (4 + u) % F_BANKS, 0:TT * E].rearrange("p (t e) -> p t e", t=TT),
                        lb[:].unsqueeze(1).broadcast_to([P, TT, E]), ALU.add).then_inc(drained, 1)

            pair(0, True)
            with dve.Fori(1, NG // 2) as i:
                pair(i, False)
            dve.wait_ge(drained, ROUTE)
            nc.vector.memset(better[:], 0.0).then_inc(logits_ready, 1)
            dve.wait_ge(score_ready, 1)
            for j in range(E):
                sj = score[:, :, j:j + 1]
                link(nc.vector.tensor_tensor(cmp[:], sj.broadcast_to([P, NT, E]), score[:], ALU.is_gt))
                link(nc.vector.tensor_tensor(better[:], better[:], cmp[:], ALU.add))
                if j < E - 1:
                    rest = slice(j + 1, E)
                    link(nc.vector.tensor_tensor(cmp[:, :, rest], sj.broadcast_to([P, NT, E - 1 - j]),
                                                 score[:, :, rest], ALU.is_equal))
                    link(nc.vector.tensor_tensor(better[:, :, rest], better[:, :, rest], cmp[:, :, rest], ALU.add))
            link(nc.vector.tensor_scalar(chosen[:], better[:], TOPK - 0.5, None, ALU.is_lt))
            nc.vector.tensor_scalar(off[:], chosen[:], -UNCHOSEN, UNCHOSEN, ALU.mult, ALU.add).then_inc(off_ready, 1)
            link(nc.vector.tensor_tensor(cmp[:], score[:], chosen[:], ALU.mult))
            link(nc.vector.tensor_reduce(out=total[:], in_=cmp[:], axis=AX.X, op=ALU.add))
            link(nc.vector.tensor_scalar(total[:], total[:], 1e-8, None, ALU.add))
            link(nc.vector.reciprocal(total[:], total[:]))
            link(nc.vector.tensor_tensor(cmp[:], cmp[:], total[:].unsqueeze(2).broadcast_to([P, NT, E]), ALU.mult))
            nc.vector.tensor_reduce(out=sums[:, 0:E], in_=cmp[:].rearrange("p n e -> p e n"), axis=AX.X, op=ALU.add)
            nc.vector.tensor_reduce(out=sums[:, E:2 * E], in_=chosen[:].rearrange("p n e -> p e n"), axis=AX.X,
                                    op=ALU.add).then_inc(sums_ready, 1)
            dve.wait_ge(filled, ROUTE + 1)
            link(nc.vector.tensor_scalar(wmean[:, E:2 * E], ps[:, DOWN, E:2 * E], 1.0, None, ALU.max))
            link(nc.vector.reciprocal(wmean[:, E:2 * E], wmean[:, E:2 * E]))
            nc.vector.tensor_tensor(wmean[:, 0:E], ps[:, DOWN, 0:E], wmean[:, E:2 * E], ALU.mult).then_inc(drained, 1)
            dve.wait_ge(drained, ROUTE + 1)
            dve.wait_ge(w_loaded, 16 * 3)
            for j in range(E):
                ins = nc.vector.tensor_scalar(wd_raw[:, j, :], wd_raw[:, j, :], wmean[:, j:j + 1], None, ALU.mult)
            ins.then_inc(wd_scaled, 1)
            for n in range(NG):
                dve.wait_ge(filled, ROUTE + 2 + n)
                nc.vector.tensor_copy(offT[:, n * T:(n + 1) * T], ps[0:E, DOWN + (n + 1) % TT, :]).then_inc(drained, 1)

            def multiply(n, pos, first):
                dve.wait_ge(up_filled, n * HID + (pos + 1))
                dve.wait_ge(silu_done, n * HID + (pos + 1))
                if not (first and pos < HID_RING):
                    dve.wait_ge(hid_split, n * HID + (pos + 1 - HID_RING))
                nc.vector.tensor_tensor(hid_whole(pos % HID_RING), ps[:, UP + pos % 2, :], silu_of(pos),
                                        ALU.mult).then_inc(hid_done, 1)

            def add_down(n):
                for t in range(TT):
                    if t < TT - 1:
                        dve.wait_ge(down_filled, n * (TT - 1) + (t + 1))
                    else:
                        dve.wait_ge(hid_used, n * HID + HID)
                    xb = x_all[:, bass.ds(n * TT + t, 1), :].rearrange("p o d -> p (o d)")
                    nc.vector.tensor_tensor(xb, xb, ps[:, DOWN + t, 0:D], ALU.add).then_inc(down_drained, 1)

            for pos in range(HID):
                multiply(0, pos, True)
            with dve.Fori(1, NG) as n:
                for pos in range(HID):
                    multiply(n, pos, False)
                    if pos == LEAD - 1:
                        add_down(n - 1)
            add_down(NG - 1)


def build(nc, io, out, stage=3):
    with ExitStack() as ctx:
        x_all = ctx.enter_context(nc.sbuf_tensor("x_all", [P, NT, D], F32))
        ln2 = ctx.enter_context(nc.sbuf_tensor("ln2", [P, NT, 2], F32))
        retention(nc, x_all, ln2, io)
        if stage > 1:
            cross_attention(nc, x_all, ln2, io)
        if stage > 2:
            feed_forward(nc, x_all, io, out)
        else:
            with nc.semaphore("dbg") as dbg, nc.Block() as block:
                @block.sync
                def _(sp):
                    sp.dma_start(out.rearrange("b (n p) d -> p (b n) d", p=P), x_all[:]).then_inc(dbg, 16)
                    sp.wait_ge(dbg, 16)


def shape_constants(bf16):
    f = np.float32
    gamma = (f(1.0) - f(2.0) ** (f(-5.0) - np.arange(H, dtype=f))).astype(f)
    i = np.arange(P)
    head = i // HD
    diff = i[None, :] - i[:, None]
    decay = np.where(diff[:, None, :] >= 0, gamma[None, :, None] ** np.maximum(diff, 0)[:, None, :].astype(f), 0)
    hs = head[:, None] + HT * np.arange(KT)[None, :]
    qdecay = gamma[hs][:, :, None] ** i[None, None, :].astype(f)
    kscale = np.repeat(gamma[None, :] ** (P - i)[:, None].astype(f), HD, axis=1)
    return {
        "ident": np.eye(P, dtype=f),
        "decay": decay.astype(f),
        "qdecay": qdecay.astype(f),
        "kscale": kscale.astype(f),
        "headmask": (head[:, None] == np.arange(HT)[None, :]).astype(f),
        "blockmask": (head[:, None] == head[None, :]).astype(f),
        "chunkdecay": (gamma[hs] ** f(P)).astype(f),
        "ones": np.ones((P, P), f),
        "identb": np.eye(P, dtype=bf16),
        "pickb": (np.arange(E)[:, None] == np.arange(E * P)[None, :] // P).astype(bf16),
        "meanw": np.full((P, P), 1.0 / P, f),
    }


STAGE = 3


def kernel(**inputs):
    import ml_dtypes
    import concourse.bacc as bacc
    from concourse.bass_utils import run_bass_kernel_spmd as run

    a = {k: np.asarray(v) for k, v in inputs.items()}

    def rows(v):
        return np.broadcast_to(v[None, :], (P, v.shape[0]))

    arrays = dict(shape_constants(ml_dtypes.bfloat16))
    arrays.update({
        "x": a["x"],
        "wqkv": a["L0_attn_W_qkv"],
        "past": a["L0_attn_past_kv"].reshape(KT, P, HD).transpose(1, 0, 2),
        "gw": np.repeat(a["L0_attn_gn_weight"], HD).reshape(KT, P).T,
        "gb": np.repeat(a["L0_attn_gn_bias"], HD).reshape(KT, P).T,
        "ctxT": a["ctx_1024"].transpose(0, 2, 1),
        "wq": a["L0_xattn_Wq"].T,
        "wk": a["L0_xattn_Wk"].T,
        "wv": a["L0_xattn_Wv"].T,
        "wo": a["L0_xattn_Wo"].T,
        "bq": a["L0_xattn_bq"].reshape(KT, P).T,
        "bk": a["L0_xattn_bk"].reshape(KT, P).T,
        "bv": rows(a["L0_xattn_bv"]),
        "bo": rows(a["L0_xattn_bo"]),
        "gate_w": a["L0_ffn_gate_w"].T,
        "lb": rows(a["L0_ffn_lb_bias"]),
        "wg": np.concatenate([a["L0_ffn_expert_gate_w"].reshape(E * P, D), a["L0_ffn_shared_gate_w"]], 0).T,
        "wu": np.concatenate([a["L0_ffn_expert_up_w"].reshape(E * P, D), a["L0_ffn_shared_up_w"]], 0).T,
        "wd": np.concatenate([a["L0_ffn_expert_down_w"].transpose(0, 2, 1).reshape(E * P, D),
                              a["L0_ffn_shared_down_w"].T], 0),
    })
    arrays["ones_rows"] = np.ones((MR, GH, S), ml_dtypes.bfloat16)
    nc = bacc.Bacc("TRN2", target_bir_lowering=False, num_devices=1)
    io = {}
    for name in arrays:
        arrays[name] = np.ascontiguousarray(arrays[name])
        io[name] = nc.dram_tensor("in_" + name, arrays[name].shape,
                                  mybir.dt.from_np(arrays[name].dtype), kind="ExternalInput").ap()
    out = nc.dram_tensor("out_0", (B, T, D), F32, kind="ExternalOutput").ap()
    build(nc, io, out, STAGE)
    r = run(nc, [{"in_" + n: v for n, v in arrays.items()}], core_ids=[0])
    return r.results[0]["out_0"]
```

```python
from contextlib import ExitStack

import numpy as np

import concourse.bass as bass
from concourse import mybir

F32 = mybir.dt.float32
BF16 = mybir.dt.bfloat16
F32R = mybir.dt.float32r
ALU = mybir.AluOpType
ACT = mybir.ActivationFunctionType
AX = mybir.AxisListType

P = 128
B, T, D, H = 8, 512, 256, 16
HD = D // H
TT = T // P
KT = D // P
HT = P // HD
NT = B * TT
S = 1601
SC = -(-S // P)
EPS = 1e-5


def widths(total, step):
    return [min(step, total - i) for i in range(0, total, step)]



R_BANKS = 6
SPLIT_PASSES = ((1, 0), (0, 1), (0, 0))
Y_BANKS = (7, 6)
R_ITEMS = 36
R_LINKS = 19


def retention(nc, x_all, ln2, io):
    with ExitStack() as ctx:
        def sb(name, shape, dt=F32):
            return ctx.enter_context(nc.sbuf_tensor(name, shape, dt))

        def sem(name):
            return ctx.enter_context(nc.semaphore(name))

        ps = ctx.enter_context(nc.psum_tensor("r_ps", [P, 8, 512], F32))
        ident = sb("r_ident", [P, P])
        decay = sb("r_decay", [P, H, P])
        qdecay = sb("r_qdecay", [P, KT, P])
        kscale = sb("r_kscale", [P, D])
        headmask = sb("r_headmask", [P, HT])
        blockmask = sb("r_blockmask", [P, P])
        chunkdecay = sb("r_chunkdecay", [P, KT])
        meanw = sb("r_meanw", [P, P])
        wqkv = sb("r_wqkv", [P, KT, 3 * D])
        w_parts = [sb(f"r_w{part}", [P, KT, 3 * D], F32R) for part in ("_rounded", "_rest")]
        past = sb("r_past", [P, KT, HD])
        gw = sb("r_gw", [P, KT])
        gb = sb("r_gb", [P, KT])

        past_bd = sb("r_past_bd", [P, KT, P])
        xn = sb("r_xn", [P, TT, D])
        xnT = [sb(f"r_xnT{part}", [P, KT, T], F32R) for part in ("_rounded", "_rest")]
        qT = sb("r_qT", [P, KT, T])
        qwide = sb("r_qwide", [P, KT, HT, T])
        qg = sb("r_qg", [P, KT, T])
        kT = sb("r_kT", [P, KT, T])
        kd = sb("r_kd", [P, TT, D])
        vz = sb("r_vz", [P, TT, H // 2, 4, HD])
        probs = sb("r_probs", [P, 2, H, P])
        state = sb("r_state", [P, TT, KT, P])
        stmp = sb("r_stmp", [P, P])
        rT = sb("r_rT", [P, KT, T])
        bst = sb("r_bst", [P, TT, 6])
        lmv = sb("r_lmv", [P, TT, 2])
        rbst = sb("r_rbst", [P, TT, 6])
        rmv = sb("r_rmv", [P, 2])
        rs2 = sb("r_rs2", [P, 2])
        gs2 = sb("r_gs2", [P, 2])
        var = sb("r_var", [P, TT])
        carrier = sb("r_carrier", [P, 1])
        pool_carrier = sb("r_pool_carrier", [P, KT])
        std = sb("r_std", [P, TT])
        rstd = sb("r_rstd", [P, TT])
        ga = sb("r_ga", [P, KT])
        gbm = sb("r_gbm", [P, KT])
        y = sb("r_y", [P, KT, T])

        x_loaded, consts = sem("x_loaded"), sem("r_consts")
        filled, drained = sem("r_filled"), sem("r_drained")
        var_ready, std_ready = sem("var_ready"), sem("std_ready")
        xn_ready, past_ready = sem("xn_ready"), sem("past_ready")
        q_wide, q_decayed = sem("q_wide"), sem("q_decayed")
        stats_ready, stats_filled = sem("stats_ready"), sem("stats_filled")
        affine_ready, y_ready, y_filled = sem("affine_ready"), sem("y_ready"), sem("y_filled")
        x1_ready, vz_zero = sem("x1_ready"), sem("vz_zero")
        ident_loaded = sem("ident_loaded")
        rw_loaded, rw_rounded, rw_split = sem("rw_loaded"), sem("rw_rounded"), sem("rw_split")
        link_r = sem("r_link")

        NCONST = 10
        block = ctx.enter_context(nc.Block())

        @block.sync
        def _(sp):
            sp.dma_start(x_all[:, 0:TT, :], io["x"][0].rearrange("(n p) d -> p n d", p=P)).then_inc(x_loaded, 16)
            sp.dma_start(ident[:], io["ident"]).then_inc(ident_loaded, 16)
            sp.dma_start(wqkv[:], io["wqkv"].rearrange("(k p) n -> p k n", p=P)).then_inc(rw_loaded, 16)
            for t, name in ((kscale, "kscale"), (qdecay, "qdecay"), (headmask, "headmask"),
                            (blockmask, "blockmask"), (chunkdecay, "chunkdecay"), (meanw, "meanw"),
                            (decay, "decay"), (past, "past"), (gw, "gw"), (gb, "gb")):
                sp.dma_start(t[:], io[name]).then_inc(consts, 16)
            for b in range(1, B):
                sp.wait_ge(x_loaded, 16 * b)
                sp.dma_start(x_all[:, b * TT:(b + 1) * TT, :],
                             io["x"][b].rearrange("(n p) d -> p n d", p=P)).then_inc(x_loaded, 16)

        @block.tensor
        def _(pe):
            def v_of(c, f):
                return vz[:, c, f * HT // 2:(f + 1) * HT // 2, 0:4:3, :]


            def turn_y(b):
                pe.wait_ge(y_ready, (b + 1) * KT)
                if not (isinstance(b, int) and b == 0):
                    pe.wait_ge(x1_ready, b * 2)
                for half in range(2):
                    for t in range(2):
                        for f in range(KT):
                            m = pe.transpose(ps[:, Y_BANKS[half], t * D + f * P:t * D + (f + 1) * P],
                                             y[:, f, (2 * half + t) * P:(2 * half + t + 1) * P], ident[:])
                    m.then_inc(y_filled, 1)

            def stats(b):
                pe.wait_ge(stats_ready, b + 1)
                pe.matmul(ps[:, R_BANKS, 0:2], meanw[:], rs2[:], start=True, stop=True).then_inc(stats_filled, 1)

            def turn_rows(b, bank):
                pe.wait_ge(xn_ready, b + 1)
                for f in range(KT):
                    o = bank()
                    for t in range(TT):
                        m = pe.transpose(ps[:, o, t * P:(t + 1) * P], xn[:, t, f * P:(f + 1) * P], ident[:])
                    m.then_inc(filled, 1)

            def product(out_, lhs, rhs):
                for n, (l, r) in enumerate(SPLIT_PASSES):
                    for kk in range(KT):
                        m = pe.matmul(out_, lhs(l, kk), rhs(r, kk), start=n == 0 and kk == 0,
                                      stop=n == len(SPLIT_PASSES) - 1 and kk == KT - 1)
                return m

            def batch(b, last=False):
                k = [0]
                start = KT + b * R_ITEMS
                first = isinstance(b, int) and b == 0

                def bank():
                    if not (first and KT + k[0] < R_BANKS):
                        pe.wait_ge(drained, start + (k[0] - R_BANKS + 1))
                    k[0] += 1
                    return (KT + k[0] - 1) % R_BANKS

                pe.wait_ge(drained, start if first else start - 1)
                for part in range(2):
                    if part and not first:
                        stats(b - 1)
                    for f in range(KT):
                        product(ps[:, bank(), :],
                                lambda l, kk: w_parts[l][:, kk, part * D + f * P:part * D + (f + 1) * P],
                                lambda r, kk: xnT[r][:, kk, :]).then_inc(filled, 1)
                for c in range(TT):
                    o = bank()
                    product(ps[:, o, D:2 * D], lambda l, kk: xnT[l][:, kk, c * P:(c + 1) * P],
                            lambda r, kk: w_parts[r][:, kk, 2 * D:3 * D])
                    if c == 0:
                        pe.wait_ge(drained, start + 2 * KT)
                    for f in range(KT):
                        m = pe.transpose(ps[:, o, f * P:(f + 1) * P], kT[:, f, c * P:(c + 1) * P], ident[:])
                    m.then_inc(filled, 1)

                def scores(c):
                    for f in range(KT):
                        if c == 0:
                            pe.wait_ge(q_wide, b * KT * HT + (f + 1) * HT)
                        for half in range(2):
                            o = bank()
                            pe.matmul(ps[:, o, :], kT[:, f, c * P:(c + 1) * P],
                                      qwide[:, f, 4 * half:4 * half + 4, c * P:(c + 1) * P],
                                      start=True, stop=True).then_inc(filled, 1)

                def states(c):
                    for f in range(KT):
                        o = bank()
                        pe.matmul(ps[:, o, 0:P], kd[:, c, f * P:(f + 1) * P],
                                  v_of(c, f), start=True, stop=True).then_inc(filled, 1)

                def output(c):
                    pe.wait_ge(drained, start + probs_item[c])
                    if c == 1:
                        pe.wait_ge(q_decayed, b + 1)
                    o = bank()
                    for f in range(KT):
                        pe.matmul(ps[:, o, f * P:(f + 1) * P], past_bd[:, f, :], qT[:, f, c * P:(c + 1) * P],
                                  start=f == 0, stop=False, skip_group_check=True)
                        if c:
                            pe.matmul(ps[:, o, f * P:(f + 1) * P], state[:, c, f, :], qg[:, f, c * P:(c + 1) * P],
                                      start=False, stop=False, skip_group_check=True)
                    for f in range(KT):
                        for odd in range(2):
                            for pair in range(HT // 2):
                                h = f * HT + 2 * pair + odd
                                m = pe.matmul(ps[32 * pair:32 * (pair + 1), o, f * P:(f + 1) * P],
                                              vz[:, c, h // 2, 2 * odd:2 * odd + 2, :].rearrange("p x d -> p (x d)"),
                                              probs[:, c % 2, h, :], start=False,
                                              stop=f == KT - 1 and odd == 1 and pair == HT // 2 - 1,
                                              tile_position=(0, 32 * pair), skip_group_check=True)
                    m.then_inc(filled, 1)

                probs_item = [12, 18, 25, 32]
                pe.wait_ge(drained, start + 8)
                scores(0)
                for c in range(1, TT):
                    scores(c)
                    if c == 1 and not (isinstance(b, int) and b == 0):
                        turn_y(b - 1)
                    states(c - 1)
                    output(c - 1)
                if not last:
                    turn_rows(b + 1, bank)
                output(TT - 1)
                assert k[0] == R_ITEMS - last * KT

            order_of_banks = iter(range(KT))
            pe.wait_ge(ident_loaded, 16)
            turn_rows(0, lambda: next(order_of_banks))
            pe.wait_ge(rw_split, 1)
            pe.wait_ge(consts, 16 * NCONST)
            pe.wait_ge(past_ready, 1)
            batch(0)
            with pe.Fori(1, B - 1) as b:
                batch(b)
            batch(B - 1, last=True)
            stats(B - 1)
            turn_y(B - 1)

        @block.scalar
        def _(act):
            def root(n):
                act.wait_ge(var_ready, n)
                nc.scalar.activation(std[:], var[:], ACT.Sqrt).then_inc(std_ready, 1)

            def widen(b, f):
                act.wait_ge(drained, KT + b * R_ITEMS + (f + 1))
                for h in range(HT):
                    ins = nc.scalar.activation(qwide[:, f, h, :], qT[:, f, :], ACT.Copy, scale=headmask[:, h:h + 1])
                    ins.then_inc(q_wide, 1)

            act.wait_ge(rw_loaded, 16)
            nc.scalar.activation(w_parts[0][:], wqkv[:], ACT.Copy).then_inc(rw_rounded, 1)
            root(1)
            act.wait_ge(consts, 16 * NCONST)
            widen(0, 0)
            widen(0, 1)
            root(2)
            with act.Fori(1, B - 1) as b:
                widen(b, 0)
                root(3 * b)
                widen(b, 1)
                root(3 * b + 1)
                root(3 * b + 2)
            widen(B - 1, 0)
            root(3 * B - 3)
            widen(B - 1, 1)
            root(3 * B - 2)
            root(3 * B - 1)
            root(3 * B)

        @block.gpsimd
        def _(pool):
            nc.gpsimd.memset(vz[:], 0.0).then_inc(vz_zero, 1)
            pool.wait_ge(rw_rounded, 1)
            nc.gpsimd.tensor_tensor(w_parts[1][:], wqkv[:], w_parts[0][:], ALU.subtract).then_inc(rw_split, 1)
            pool.wait_ge(consts, 16 * NCONST)

            def decay_q(b):
                pool.wait_ge(drained, KT + b * R_ITEMS + KT)
                qd = qdecay[:].unsqueeze(2).broadcast_to([P, KT, TT, P])
                nc.gpsimd.tensor_tensor(qg[:].rearrange("p k (c t) -> p k c t", c=TT),
                                        qT[:].rearrange("p k (c t) -> p k c t", c=TT), qd,
                                        ALU.mult).then_inc(q_decayed, 1)

            def group_norm(b):
                pool.wait_ge(affine_ready, b + 1)
                nc.gpsimd.tensor_tensor(pool_carrier[:], ga[:], gbm[:], ALU.add)
                for f in range(KT):
                    nc.gpsimd.tensor_scalar(y[:, f, :], rT[:, f, :], ga[:, f:f + 1], gbm[:, f:f + 1],
                                            ALU.mult, ALU.add).then_inc(y_ready, 1)

            decay_q(0)
            with pool.Fori(1, B) as b:
                decay_q(b)
                group_norm(b - 1)
            group_norm(B - 1)

        @block.vector
        def _(dve):
            steps = [0]
            base = [0]

            def link(ins):
                steps[0] += 1
                ins.then_inc(link_r, 1)
                dve.wait_ge(link_r, base[0] + steps[0])

            def carry_wait():
                nc.vector.memset(carrier[:], 0.0)

            def row_moments(b):
                for t in range(TT):
                    ins = nc.vector.bn_stats(bst[:, t, :], x_all[:, bass.ds(b * TT + t, 1), :].rearrange("p o d -> p (o d)"))
                link(ins)
                carry_wait()
                for t in range(TT):
                    ins = nc.vector.bn_aggr(lmv[:, t, :], bst[:, t, :])
                link(ins)
                nc.vector.tensor_scalar(var[:], lmv[:, :, 1], EPS, None, ALU.add).then_inc(var_ready, 1)

            def normalise_moments(b):
                dve.wait_ge(x_loaded, b * 16 + 16)
                row_moments(b)

            def normalise(b, n):
                dve.wait_ge(std_ready, n)
                link(nc.vector.reciprocal(rstd[:], std[:]))
                for t in range(TT):
                    ins = nc.vector.tensor_scalar(xn[:, t, :], x_all[:, bass.ds(b * TT + t, 1), :].rearrange("p o d -> p (o d)"),
                                                  lmv[:, t, 0:1], rstd[:, t:t + 1], ALU.subtract, ALU.mult)
                ins.then_inc(xn_ready, 1)

            def second_moments(b):
                for half in range(2):
                    dve.wait_ge(y_filled, b * 2 + (half + 1))
                    xb = x_all[:, bass.ds(b * TT + 2 * half, 2), :]
                    nc.vector.tensor_tensor(xb, xb, ps[:, Y_BANKS[half], :].rearrange("p (t d) -> p t d", t=2),
                                            ALU.add).then_inc(x1_ready, 1)
                dve.wait_ge(x1_ready, b * 2 + 2)
                carry_wait()
                row_moments(b)

            def keep_second(b, n):
                out = ln2[:, bass.ts(b, TT), :]
                nc.vector.tensor_copy(out[:, :, 0], lmv[:, :, 0])
                dve.wait_ge(std_ready, n)
                link(nc.vector.reciprocal(out[:, :, 1], std[:]))

            def batch_moments(items):
                dve.wait_ge(drained, items)
                carry_wait()
                link(nc.vector.bn_aggr(rmv[:], rbst[:]))
                nc.vector.tensor_copy(rs2[:, 0:1], rmv[:, 0:1])
                nc.vector.scalar_tensor_tensor(out=rs2[:, 1:2], in0=rmv[:, 0:1], scalar=rmv[:, 0:1],
                                               in1=rmv[:, 1:2], op0=ALU.mult, op1=ALU.add).then_inc(stats_ready, 1)

            def batch_variance(b):
                dve.wait_ge(stats_filled, b + 1)
                link(nc.vector.tensor_copy(gs2[:], ps[:, R_BANKS, 0:2]))
                link(nc.vector.tensor_scalar(rmv[:, 0:1], gs2[:, 0:1], gs2[:, 0:1], None, ALU.mult))
                link(nc.vector.tensor_scalar(rmv[:, 1:2], gs2[:, 1:2], rmv[:, 0:1], EPS, ALU.subtract, ALU.add))
                nc.vector.tensor_copy(var[:], rmv[:, 1:2].broadcast_to([P, TT])).then_inc(var_ready, 1)

            def batch_affine(n):
                dve.wait_ge(std_ready, n)
                link(nc.vector.reciprocal(rstd[:], std[:]))
                link(nc.vector.tensor_scalar(ga[:], gw[:], rstd[:, 0:1], None, ALU.mult))
                link(nc.vector.tensor_scalar(gbm[:], ga[:], gs2[:, 0:1], None, ALU.mult))
                nc.vector.tensor_tensor(gbm[:], gb[:], gbm[:], ALU.subtract).then_inc(affine_ready, 1)

            def keep_xnT(f, o):
                link(nc.vector.tensor_copy(xnT[0][:, f, :], ps[:, o, :]))
                nc.vector.tensor_tensor(xnT[1][:, f, :], ps[:, o, :], xnT[0][:, f, :],
                                        ALU.subtract).then_inc(drained, 1)

            def batch(b, roots, first=False, last=False):
                k = [0]
                start = KT + b * R_ITEMS

                def item():
                    dve.wait_ge(filled, start + (k[0] + 1))
                    k[0] += 1
                    return (KT + k[0] - 1) % R_BANKS

                if not first:
                    batch_moments(start)
                for dst in (qT, kT):
                    for f in range(KT):
                        nc.vector.tensor_copy(dst[:, f, :], ps[:, item(), :]).then_inc(drained, 1)
                    if dst is qT and not first:
                        batch_variance(b - 1)
                for c in range(TT):
                    o = item()
                    nc.vector.tensor_tensor(kd[:, c, :], ps[:, o, 0:D], kscale[:], ALU.mult)
                    nc.vector.tensor_copy(vz[:, c, :, 0:4:3, :], ps[:, o, D:2 * D].rearrange(
                        "p (h x d) -> p h x d", x=2, d=HD)).then_inc(drained, 1)
                    if c == 1 and not first:
                        batch_affine(roots + 1)

                def scores(c):
                    for f in range(KT):
                        for half in range(2):
                            h = f * HT + half * 4
                            nc.vector.tensor_tensor(probs[:, c % 2, h:h + 4, :],
                                                    ps[:, item(), :].rearrange("p (h t) -> p h t", h=4),
                                                    decay[:, h:h + 4, :], ALU.mult).then_inc(drained, 1)

                def states(c):
                    for f in range(KT):
                        o = item()
                        if c == 0:
                            nc.vector.tensor_tensor(state[:, 1, f, :], ps[:, o, 0:P], blockmask[:],
                                                    ALU.mult).then_inc(drained, 1)
                        else:
                            link(nc.vector.tensor_tensor(stmp[:], ps[:, o, 0:P], blockmask[:], ALU.mult))
                            nc.vector.scalar_tensor_tensor(out=state[:, c + 1, f, :], in0=state[:, c, f, :],
                                                           scalar=chunkdecay[:, f:f + 1], in1=stmp[:],
                                                           op0=ALU.mult, op1=ALU.add).then_inc(drained, 1)
                            dve.wait_ge(drained, start + k[0])

                def output(c):
                    o = item()
                    nc.vector.tensor_copy(rT[:, :, c * P:(c + 1) * P],
                                          ps[:, o, 0:D].rearrange("p (f t) -> p f t", f=KT))
                    nc.vector.bn_stats(rbst[:, c, :], ps[:, o, 0:D]).then_inc(drained, 1)

                scores(0)
                scores(1)
                if not first:
                    second_moments(b - 1)
                states(0)
                output(0)
                if not first:
                    keep_second(b - 1, roots + 2)
                scores(2)
                if not last:
                    normalise_moments(b + 1)
                states(1)
                output(1)
                if not last:
                    normalise(b + 1, roots + (1 if first else 3))
                scores(3)
                states(2)
                output(2)
                if not last:
                    for f in range(KT):
                        keep_xnT(f, item())
                output(3)
                assert k[0] == R_ITEMS - last * KT

            normalise_moments(0)
            normalise(0, 1)
            for f in range(KT):
                dve.wait_ge(filled, f + 1)
                keep_xnT(f, f)
            dve.wait_ge(consts, 16 * NCONST)
            past_h = past[:].unsqueeze(2).broadcast_to([P, KT, HT, HD])
            mask_h = blockmask[:].rearrange("p (h e) -> p h e", h=HT).unsqueeze(1).broadcast_to([P, KT, HT, HD])
            for f in range(KT):
                ins = nc.vector.scalar_tensor_tensor(out=past_bd[:, f, :].rearrange("p (h e) -> p h e", h=HT),
                                                     in0=past_h[:, f], scalar=float(D), in1=mask_h[:, f],
                                                     op0=ALU.mult, op1=ALU.mult)
            ins.then_inc(past_ready, 1)
            dve.wait_ge(vz_zero, 1)
            batch(0, 1, first=True)
            base[0], steps[0] = steps[0], 0
            before = base[0]
            with dve.Fori(1, B - 1) as b:
                base[0] = (b - 1) * R_LINKS + before
                batch(b, 3 * b - 1)
            assert steps[0] == R_LINKS, steps[0]
            base[0], steps[0] = before + (B - 2) * R_LINKS, 0
            batch(B - 1, 3 * B - 4, last=True)
            batch_moments(B * R_ITEMS)
            batch_variance(B - 1)
            batch_affine(3 * B - 1)
            second_moments(B - 1)
            keep_second(B - 1, 3 * B)



G = 4
GH = H // G
KPARTS = [0, 1, 0, 2, 0, 1]
QPARTS = [0, 0, 1, 0, 2, 1]
NB = len(KPARTS)
XR = NB * HD
MR = 3
FULL = S // 512
TAIL = S - FULL * 512
W_BANKS = 3
COLS = [(i * 512, w) for i, w in enumerate(widths(S, 512))]
V_RUNS = [(0, 2), (2, 2), (4, 2), (6, 2), (8, 2), (10, 1), (11, 1), (12, 1)]
SPLITS = KT + KT * len(COLS)
K_CHUNKS = (1, 3, 6, 8)
V_CHUNKS = ((1, 11), (1, 12), (2, 11), (2, 12), (3, 1), (3, 4), (3, 7), (3, 11))


def next_group_items(g):
    out = []
    for j in range(GH):
        out += [("max", g, j, t, i) for t in range(TT) for i in range(FULL)] + [("tails", g, j)]
    return out


def projection_items():
    q = [("xnT", f) for f in range(KT)] + [("q", f) for f in range(KT)]
    k = [("k", f, i) for f in range(KT) for i in range(len(COLS))]
    v = [("v", i) for i in range(len(V_RUNS))]
    return q, k, v


def work_of(prev, following):
    plan = [[[] for _ in range(SC)] for _ in range(G)]
    q, k, v = projection_items()
    if prev:
        plan[0][1].append(("norm", G - 1))
        plan[0][3] += [("oT", 0), ("oT", 1)]
        plan[0][5].append(("wo", 0))
        plan[0][6].append(("wo", 1))
    if following:
        plan[0][7] += q[0:2]
        late_q = [(0, 11), (0, 12)]
        for n, item in enumerate(k):
            plan[1 + n // len(COLS)][K_CHUNKS[n % len(COLS)]].append(item)
        for item, (g, c) in zip(q[2:4] + v, late_q + list(V_CHUNKS)):
            if c != SC - 2:
                plan[g][c].append(item)
    for g in range(1, G):
        plan[g][1].append(("norm", g - 1))
    for g in range(G):
        if g < G - 1 or following:
            todo = next_group_items((g + 1) % G)
            for c in range(SC - 2):
                m = 5 if c < 8 else 4
                plan[g][c] += todo[:m]
                todo = todo[m:]
            assert not todo
            plan[g][SC - 2].append(("shift", (g + 1) % G))
    if following:
        for item, (g, c) in zip(q[2:4] + v, late_q + list(V_CHUNKS)):
            if c == SC - 2:
                plan[g][c].append(item)
    return plan


def order(plan):
    return [item for group in plan for chunk in group for item in chunk]


def prologue_items():
    q, k, v = projection_items()
    return q + k + v + next_group_items(0) + [("shift", 0)]


N_PRO = len(prologue_items())
N_FIRST = len(order(work_of(False, True)))
N_MID = len(order(work_of(True, True)))
PREV = N_MID - N_FIRST
X_LINKS = 22
S_ITEMS = 2 * SC * G


def cross_attention(nc, x_all, ln2, io):
    assert N_MID % W_BANKS == 0
    with ExitStack() as ctx:
        def sb(name, shape, dt=F32):
            return ctx.enter_context(nc.sbuf_tensor(name, shape, dt))

        def sem(name):
            return ctx.enter_context(nc.semaphore(name))

        ps = ctx.enter_context(nc.psum_tensor("x_ps", [P, 8, 512], F32))
        PV, WORK = 4, 5
        ident = sb("x_ident", [P, P])
        identb = sb("x_identb", [P, P], BF16)
        wq, wk, wv, wo = (sb("x_w" + n, [P, KT, D]) for n in "qkvo")
        bq, bk = sb("x_bq", [P, KT]), sb("x_bk", [P, KT])
        bv, bo = sb("x_bv", [P, D]), sb("x_bo", [P, D])
        kst = [sb(f"x_kst{g}", [XR + MR, GH, S], BF16) for g in range(G)]
        qst = [sb(f"x_qst{g}", [XR + MR, GH, T], BF16) for g in range(G)]
        vst = [sb(f"x_vst{g}", [P, SC, GH, HD + 1]) for g in range(G)]
        v_all = sb("x_v_all", [P, SC, D])
        ctxT = sb("x_ctxT", [P, KT, S])
        kp = sb("x_kp", [P, KT, 3, S], BF16)
        qp = sb("x_qp", [P, KT, 3, T], BF16)
        rest = sb("x_rest", [P, 2, 512])
        left = sb("x_left", [P, 512])
        probs = sb("x_probs", [P, 4, 2, T])
        ou = sb("x_ou", [P, T])
        o_all = sb("x_o_all", [P, TT, D])
        oT = sb("x_oT", [P, KT, T])
        otmp = ou[:].rearrange("p (n d) -> p n d", n=2)
        xn, xnT = o_all, oT
        mx = sb("x_mx", [P, GH, TT, FULL + 1])
        negm = sb("x_negm", [P, GH, TT])
        mres = sb("x_mres", [P, GH, TT])
        mparts = sb("x_mparts", [P, TT, GH, MR], BF16)
        mrows = sb("x_mrows", [GH * MR, T], BF16)
        rden = sb("x_rden", [P, TT, GH])
        k_dram = nc.dram_tensor("k_parts", [B, KT, 3, P, S], BF16, kind="Internal").ap()
        q_dram = nc.dram_tensor("q_parts", [B, KT, 3, P, T], BF16, kind="Internal").ap()

        consts, ctx_loaded, ones_set = sem("x_consts"), sem("ctx_loaded"), sem("ones_set")
        ones_loaded = sem("ones_loaded")
        filled, drained = sem("w_filled"), sem("w_drained")
        s_filled, exp_done, pv_used = sem("s_filled"), sem("exp_done"), sem("pv_used")
        pv_evac = sem("pv_evac")
        xn_ready, mparts_ready, m_loaded = sem("x_xn_ready"), sem("mparts_ready"), sem("m_loaded")
        split_step, split_done = sem("split_step"), sem("split_done")
        q_spilled, k_spilled = sem("q_spilled"), [sem(f"k_spilled{f}") for f in range(KT)]
        v_ready = sem("v_ready")
        kq_loaded = [sem(f"kq_loaded{g}") for g in range(G)]
        link_x = sem("x_link")
        NCONST = 9
        KQ = 16 * 2 * NB

        plans = {"first": work_of(False, True), "mid": work_of(True, True), "last": work_of(True, False)}

        def start_of(b):
            return N_PRO if isinstance(b, int) and b == 0 else b * N_MID + N_PRO - PREV

        def bank_of(b, n):
            return WORK + ((N_PRO if isinstance(b, int) and b == 0 else N_PRO - PREV) + n) % W_BANKS

        def position(kind, item):
            return order(plans[kind]).index(item)

        def split(engine, ops, dst, b1, n, count, w):
            engine.wait_ge(drained, count)
            whole = rest[:, n % 2, 0:w]
            ops.tensor_tensor(dst(1), whole, dst(0), ALU.subtract)
            ops.tensor_tensor(left[:, 0:w], whole, dst(0), ALU.subtract).then_inc(split_step, 1)
            engine.wait_ge(split_step, b1 * SPLITS + (n + 1))
            ops.tensor_tensor(dst(2), left[:, 0:w], dst(1), ALU.subtract).then_inc(split_done, 1)
            engine.wait_ge(split_done, b1 * SPLITS + (n + 1))

        block = ctx.enter_context(nc.Block())

        @block.sync
        def _(sp):
            for t, name in ((ident, "ident"), (bq, "bq"), (bk, "bk"), (bv, "bv"), (bo, "bo")):
                sp.dma_start(t[:], io[name]).then_inc(consts, 16)
            for t, name in ((wq, "wq"), (wk, "wk"), (wv, "wv"), (wo, "wo")):
                sp.dma_start(t[:], io[name].rearrange("(k p) n -> p k n", p=P)).then_inc(consts, 16)

            def load_ctx(b):
                sp.dma_start(ctxT[:], io["ctxT"][b].rearrange("(k p) c -> p k c", p=P)).then_inc(ctx_loaded, 16)

            def spill_q(b):
                sp.wait_ge(split_done, b * SPLITS + KT)
                sp.dma_start(q_dram[b].rearrange("k j p t -> p (k j) t"),
                             qp[:].rearrange("p k j t -> p (k j) t")).then_inc(q_spilled, 16)

            def spill_k(b, f):
                sp.wait_ge(split_done, b * SPLITS + KT + (f + 1) * len(COLS))
                sp.dma_start(k_dram[b, f].rearrange("j p t -> p j t"), kp[:, f]).then_inc(k_spilled[f], 16)

            def load_group(b, g):
                f, lo = g // 2, (g % 2) * GH * HD
                if lo == 0:
                    sp.wait_ge(k_spilled[f], b * 16 + 16)
                    if f == 0:
                        sp.wait_ge(q_spilled, b * 16 + 16)
                for dst, src, parts in ((qst[g], q_dram, QPARTS), (kst[g], k_dram, KPARTS)):
                    for n, part in enumerate(parts):
                        sp.dma_start(dst[n * HD:(n + 1) * HD, :, :],
                                     src[b, f, part, lo:lo + GH * HD, :].rearrange("(j d) c -> d j c", d=HD)
                                     ).then_inc(kq_loaded[g], 16)

            def attended(b, g):
                sp.wait_ge(s_filled, b * S_ITEMS + (g + 1) * 2 * SC)

            def load_shift(b, g, done):
                sp.wait_ge(drained, done)
                for j in range(GH):
                    sp.dma_start(qst[g][XR:XR + MR, j, :], mrows[j * MR:(j + 1) * MR, :]).then_inc(m_loaded, 16)

            for g in range(G):
                sp.dma_start(kst[g][XR:XR + MR, :, :], io["ones_rows"]).then_inc(ones_loaded, 16)
            load_ctx(0)
            spill_q(0)
            for f in range(KT):
                spill_k(0, f)
                load_group(0, 2 * f)
                load_group(0, 2 * f + 1)
            load_shift(0, 0, N_PRO)

            def batch(b, kind):
                start = start_of(b)
                if kind != "last":
                    if kind == "first":
                        sp.wait_ge(drained, N_PRO)
                    else:
                        sp.wait_ge(drained, start)
                    load_ctx(b + 1)
                if kind != "first":
                    attended(b - 1, G - 1)
                    load_group(b, G - 1)
                for g in range(G):
                    if kind != "last":
                        if g == 1:
                            spill_q(b + 1)
                            spill_k(b + 1, 0)
                        if g >= 1:
                            if g > 1:
                                attended(b, g - 1)
                            load_group(b + 1, g - 1)
                        if g == 2:
                            spill_k(b + 1, 1)
                    if g < G - 1 or kind != "last":
                        load_shift(b, (g + 1) % G, start + (position(kind, ("shift", (g + 1) % G)) + 1))

            batch(0, "first")
            with sp.Fori(1, B - 1) as b:
                batch(b, "mid")
            batch(B - 1, "last")

        @block.tensor
        def _(pe):
            pe.wait_ge(consts, 16 * NCONST)
            pe.wait_ge(ones_set, 6)
            pe.wait_ge(ones_loaded, 16 * G)

            def work(item, bank, b, b1, at):
                o = ps[:, bank, :]
                kind = item[0]
                if kind == "xnT":
                    pe.wait_ge(xn_ready, b1 + 1)
                    for t in range(TT):
                        m = pe.transpose(o[:, t * P:(t + 1) * P], xn[:, t, item[1] * P:(item[1] + 1) * P], ident[:])
                elif kind == "q":
                    pe.wait_ge(drained, at(("xnT", 1)))
                    for kk in range(KT):
                        m = pe.matmul(o, wq[:, kk, item[1] * P:(item[1] + 1) * P], xnT[:, kk, :],
                                      start=kk == 0, stop=kk == KT - 1)
                elif kind == "k":
                    pe.wait_ge(ctx_loaded, b1 * 16 + 16)
                    c, w = COLS[item[2]]
                    for kk in range(KT):
                        m = pe.matmul(o[:, 0:w], wk[:, kk, item[1] * P:(item[1] + 1) * P], ctxT[:, kk, c:c + w],
                                      start=kk == 0, stop=kk == KT - 1)
                elif kind == "v":
                    c0, n = V_RUNS[item[1]]
                    for c in range(c0, c0 + n):
                        w = min(P, S - c * P)
                        for kk in range(KT):
                            m = pe.matmul(o[0:w, (c - c0) * D:(c - c0 + 1) * D], ctxT[:, kk, c * P:c * P + w],
                                          wv[:, kk, :], start=kk == 0, stop=kk == KT - 1)
                elif kind == "max":
                    _, g, j, t, i = item
                    m = pe.matmul(o, qst[g][0:XR, j, t * P:(t + 1) * P], kst[g][0:XR, j, i * 512:(i + 1) * 512],
                                  start=True, stop=True)
                elif kind == "tails":
                    _, g, j = item
                    for t in range(TT):
                        m = pe.matmul(o[:, t * TAIL:(t + 1) * TAIL], qst[g][0:XR, j, t * P:(t + 1) * P],
                                      kst[g][0:XR, j, FULL * 512:S], start=True, stop=True)
                elif kind == "shift":
                    for t in range(TT):
                        m = pe.matmul(o[0:GH * MR, t * P:(t + 1) * P], mparts[:, t, :, :], identb[:],
                                      start=True, stop=True)
                elif kind == "norm":
                    for t in range(TT):
                        m = pe.transpose(o[:, t * P:(t + 1) * P], ou[:, t * P:(t + 1) * P], ident[:])
                elif kind == "oT":
                    pe.wait_ge(drained, at(("norm", G - 1)))
                    for t in range(TT):
                        m = pe.transpose(o[:, t * P:(t + 1) * P], o_all[:, t, item[1] * P:(item[1] + 1) * P],
                                         ident[:])
                elif kind == "wo":
                    pe.wait_ge(drained, at(("oT", 1)))
                    for n in range(2):
                        t = 2 * item[1] + n
                        for kk in range(KT):
                            m = pe.matmul(o[:, n * D:(n + 1) * D], oT[:, kk, t * P:(t + 1) * P], wo[:, kk, :],
                                          start=kk == 0, stop=kk == KT - 1)
                m.then_inc(filled, 1)

            for n, item in enumerate(prologue_items()):
                if n >= W_BANKS:
                    pe.wait_ge(drained, n - W_BANKS + 1)
                if item == ("max", 0, 0, 0, 0):
                    pe.wait_ge(kq_loaded[0], KQ)
                if item == ("shift", 0):
                    pe.wait_ge(mparts_ready, 1)
                work(item, WORK + n % W_BANKS, 0, 0, lambda i: prologue_items().index(i) + 1)

            def batch(b, kind):
                start = start_of(b)
                plan = plans[kind]
                k = [0]

                def values(g, q):
                    if q == 0:
                        if not (kind == "first" and g == 0):
                            pe.wait_ge(pv_evac, b * G + g)
                        pe.wait_ge(v_ready, b * 2 * G + 2 * (g + 1))
                    pe.wait_ge(exp_done, b * S_ITEMS + (g * 2 * SC + 2 * (q + 1)))
                    w = min(P, S - q * P)
                    for j in range(GH):
                        slot = (g * 2 * SC + 2 * q + j // 2) % 4
                        m = pe.matmul(ps[32 * j:32 * j + HD + 1, PV, :], vst[g][0:w, q, j, :],
                                      probs[0:w, slot, j % 2, :], start=q == 0, stop=q == SC - 1)
                    m.then_inc(pv_used, 1)

                def fill(g, items):
                    for item in items:
                        nxt = (g + 1) % G
                        if item == ("max", nxt, 0, 0, 0):
                            pe.wait_ge(kq_loaded[nxt], (b + (g == G - 1)) * KQ + KQ)
                        if item[0] == "shift":
                            pe.wait_ge(mparts_ready, b * G + (g + 2))
                        if item[0] == "norm":
                            pe.wait_ge(pv_evac, b * G + g)
                        pe.wait_ge(drained, start + (k[0] - W_BANKS + 1))
                        work(item, bank_of(b, k[0]), b, b + 1, lambda i: start + (position(kind, i) + 1))
                        k[0] += 1

                for g in range(G):
                    pe.wait_ge(m_loaded, b * 16 * GH * G + 16 * GH * (g + 1))
                    for c in range(SC):
                        w = min(P, S - c * P)
                        for pair in range(2):
                            n = g * 2 * SC + 2 * c + pair
                            if not (kind == "first" and n < 2):
                                pe.wait_ge(exp_done, b * S_ITEMS + (n - 1))
                            for h in range(2):
                                m = pe.matmul(ps[0:w, 2 * (n % 2) + h, :], kst[g][:, 2 * pair + h, c * P:c * P + w],
                                              qst[g][:, 2 * pair + h, :], start=True, stop=True)
                            m.then_inc(s_filled, 1)
                            if c != SC - 2:
                                fill(g, plan[g][c][0:2] if pair == 0 else plan[g][c][2:3])
                        if c:
                            values(g, c - 1)
                        fill(g, plan[g][c] if c == SC - 2 else plan[g][c][3:])
                    values(g, SC - 1)

            batch(0, "first")
            with pe.Fori(1, B - 1) as b:
                batch(b, "mid")
            batch(B - 1, "last")
            n = start_of(B - 1) + len(order(plans["last"]))
            end = [("norm", G - 1), ("oT", 0), ("oT", 1), ("wo", 0), ("wo", 1)]
            pe.wait_ge(pv_evac, B * G)
            for i, item in enumerate(end):
                pe.wait_ge(drained, n + i - W_BANKS + 1)
                work(item, WORK + (n + i) % W_BANKS, B - 1, B, lambda it: n + end.index(it) + 1)

        @block.scalar
        def _(act):
            def batch(b, kind):
                for g in range(G):
                    for c in range(SC):
                        w = min(P, S - c * P)
                        for pair in range(2):
                            n = g * 2 * SC + 2 * c + pair
                            act.wait_ge(s_filled, b * S_ITEMS + (n + 1))
                            if not (kind == "first" and n // 2 < 2):
                                act.wait_ge(pv_used, b * (S_ITEMS // 2) + (n // 2 - 1))
                            nc.scalar.activation(probs[0:w, n % 4, :, :], ps[0:w, 2 * (n % 2):2 * (n % 2) + 2, :],
                                                 ACT.Exp, scale=HD ** -0.5).then_inc(exp_done, 1)

            batch(0, "first")
            with act.Fori(1, B) as b:
                batch(b, "mid")

        @block.gpsimd
        def _(pool):
            for g in range(G):
                nc.gpsimd.memset(vst[g][:], 1.0).then_inc(ones_set, 1)
            pool.wait_ge(consts, 16 * NCONST)
            nc.gpsimd.tensor_copy(identb[:], ident[:]).then_inc(ones_set, 1)

            def splits(b1, at):
                for f in range(KT):
                    split(pool, nc.gpsimd, lambda j: qp[:, f, j, :], b1, f, at(("q", f)), T)
                for f in range(KT):
                    for i, (c, w) in enumerate(COLS):
                        split(pool, nc.gpsimd, lambda j: kp[:, f, j, c:c + w], b1, KT + f * len(COLS) + i,
                              at(("k", f, i)), w)

            def place_v(g):
                for rows, lo, hi in ((P, 0, SC - 1), (S - (SC - 1) * P, SC - 1, SC)):
                    cols = slice(g * GH * HD, (g + 1) * GH * HD)
                    nc.gpsimd.tensor_tensor(
                        vst[g][0:rows, lo:hi, :, 0:HD],
                        v_all[0:rows, lo:hi, cols].rearrange("p c (j d) -> p c j d", d=HD),
                        bv[0:rows, cols].rearrange("p (j d) -> p j d", d=HD).unsqueeze(1).broadcast_to(
                            [rows, hi - lo, GH, HD]), ALU.add).then_inc(v_ready, 1)

            pool.wait_ge(ones_set, 6)
            at0 = lambda i: prologue_items().index(i) + 1
            pool.wait_ge(drained, at0(("v", len(V_RUNS) - 1)))
            for g in range(G):
                place_v(g)

            def batch(b, kind):
                start = start_of(b)
                at = lambda i: start + (position(kind, i) + 1)
                if kind != "first":
                    pool.wait_ge(pv_used, b * (S_ITEMS // 2))
                    place_v(G - 1)
                if kind != "last":
                    splits(b + 1, at)
                    pool.wait_ge(drained, at(("v", len(V_RUNS) - 1)))
                    for g in range(G - 1):
                        pool.wait_ge(pv_used, b * (S_ITEMS // 2) + SC * (g + 1))
                        place_v(g)

            batch(0, "first")
            with pool.Fori(1, B - 1) as b:
                batch(b, "mid")
            batch(B - 1, "last")

        @block.vector
        def _(dve):
            steps, base = [0], [0]

            def link(ins):
                steps[0] += 1
                ins.then_inc(link_x, 1)
                dve.wait_ge(link_x, base[0] + steps[0])

            def normalise(b):
                for t in range(TT):
                    row = bass.ds(b * TT + t, 1)
                    ins = nc.vector.tensor_scalar(
                        xn[:, t, :], x_all[:, row, :].rearrange("p o d -> p (o d)"),
                        ln2[:, row, 0:1].rearrange("p o d -> p (o d)"), ln2[:, row, 1:2].rearrange("p o d -> p (o d)"),
                        ALU.subtract, ALU.mult)
                ins.then_inc(xn_ready, 1)

            def first_part(o, dst, bias, n, b1, w):
                nc.vector.tensor_scalar(dst, o[:, 0:w], bias, None, ALU.add)
                if not (isinstance(b1, int) and b1 == 0 and n < 2):
                    dve.wait_ge(split_done, b1 * SPLITS + (n - 1))
                return nc.vector.tensor_scalar(rest[:, n % 2, 0:w], o[:, 0:w], bias, None, ALU.add)

            def shift_parts(count):
                dve.wait_ge(drained, count)
                link(nc.vector.tensor_reduce(out=negm[:], in_=mx[:], axis=AX.X, op=ALU.max, negate=True))
                rows, rem = (v[:].rearrange("p j t -> p t j") for v in (negm, mres))
                link(nc.vector.tensor_copy(mparts[:, :, :, 0], rows))
                link(nc.vector.tensor_tensor(rem, rows, mparts[:, :, :, 0], ALU.subtract))
                link(nc.vector.tensor_copy(mparts[:, :, :, 1], rem))
                nc.vector.tensor_tensor(mparts[:, :, :, 2], rem, mparts[:, :, :, 1],
                                        ALU.subtract).then_inc(mparts_ready, 1)

            def work(item, bank, b, b1, count, shifts):
                o = ps[:, bank, :]
                kind = item[0]
                if kind == "shift":
                    shift_parts(count - 1)
                dve.wait_ge(filled, count)
                if kind == "xnT":
                    ins = nc.vector.tensor_copy(xnT[:, item[1], :], o)
                elif kind == "q":
                    f = item[1]
                    if f == 0 and not (isinstance(b1, int) and b1 == 0):
                        dve.wait_ge(q_spilled, b1 * 16)
                    ins = first_part(o, qp[:, f, 0, :], bq[:, f:f + 1], f, b1, T)
                elif kind == "k":
                    _, f, i = item
                    c, w = COLS[i]
                    if f == 0 and i == 0 and not (isinstance(b1, int) and b1 == 0):
                        for part in k_spilled:
                            dve.wait_ge(part, b1 * 16)
                    ins = first_part(o, kp[:, f, 0, c:c + w], bk[:, f:f + 1], KT + f * len(COLS) + i, b1, w)
                elif kind == "v":
                    c0, n = V_RUNS[item[1]]
                    w = min(P, S - c0 * P)
                    if c0 == 0 and not (isinstance(b1, int) and b1 == 0):
                        dve.wait_ge(v_ready, b1 * 2 * G)
                    ins = nc.vector.tensor_copy(v_all[0:w, c0:c0 + n, :],
                                                o[0:w, 0:n * D].rearrange("p (c d) -> p c d", c=n))
                elif kind == "max":
                    _, g, j, t, i = item
                    ins = nc.vector.tensor_reduce(out=mx[:, j, t, i:i + 1], in_=o, axis=AX.X, op=ALU.max)
                elif kind == "tails":
                    _, g, j = item
                    ins = nc.vector.tensor_reduce(out=mx[:, j, :, FULL], in_=o[:, 0:TT * TAIL].rearrange("p (t c) -> p t c", t=TT),
                                                  axis=AX.X, op=ALU.max)
                elif kind == "shift":
                    if not (isinstance(shifts, int) and shifts == 0):
                        dve.wait_ge(m_loaded, shifts * 16 * GH)
                    ins = nc.vector.tensor_copy(mrows[:], o[0:GH * MR, :])
                elif kind == "norm":
                    g = item[1]
                    o4 = o.rearrange("p (t j e) -> p t j e", t=TT, j=GH)
                    link(nc.vector.reciprocal(rden[:], o4[:, :, :, HD]))
                    ins = nc.vector.tensor_tensor(
                        o_all[:, :, g * GH * HD:(g + 1) * GH * HD].rearrange("p t (j d) -> p t j d", d=HD),
                        o4[:, :, :, 0:HD], rden[:].unsqueeze(3).broadcast_to([P, TT, GH, HD]), ALU.mult)
                elif kind == "oT":
                    ins = nc.vector.tensor_copy(oT[:, item[1], :], o)
                elif kind == "wo":
                    link(nc.vector.tensor_tensor(otmp, o.rearrange("p (n d) -> p n d", n=2),
                                                 bo[:].unsqueeze(1).broadcast_to([P, 2, D]), ALU.add))
                    xb = x_all[:, bass.ds((b1 - 2) * TT + 2 * item[1], 2), :]
                    ins = nc.vector.tensor_tensor(xb, xb, otmp, ALU.add)
                ins.then_inc(drained, 1)
                if kind == "wo":
                    dve.wait_ge(drained, count)
                if kind == "q" and isinstance(b1, int) and b1 == 0:
                    split(dve, nc.vector, lambda j: qp[:, f, j, :], 0, f, count, T)
                if kind == "k" and isinstance(b1, int) and b1 == 0:
                    split(dve, nc.vector, lambda j: kp[:, f, j, c:c + w], 0, KT + f * len(COLS) + i, count, w)

            dve.wait_ge(consts, 16 * NCONST)
            nc.vector.memset(ps[:, PV, :], 0.0).then_inc(ones_set, 1)
            normalise(0)
            for n, item in enumerate(prologue_items()):
                work(item, WORK + n % W_BANKS, 0, 0, n + 1, 0)

            def evacuate(groups):
                dve.wait_ge(pv_used, groups)
                return nc.vector.tensor_copy(ou[:], ps[:, PV, :]).then_inc(pv_evac, 1)

            def batch(b, kind):
                start = start_of(b)
                plan = plans[kind]
                k = 0
                for g in range(G):
                    if not (kind == "first" and g == 0):
                        evacuate(b * (S_ITEMS // 2) + g * SC)
                    for c in range(SC):
                        if g == 0 and c == 5 and kind != "last":
                            normalise(b + 1)
                        for item in plan[g][c]:
                            work(item, bank_of(b, k), b, b + 1, start + (k + 1), b * G + (g + 1))
                            k += 1

            batch(0, "first")
            before = steps[0]
            steps[0] = 0
            with dve.Fori(1, B - 1) as b:
                base[0] = (b - 1) * X_LINKS + before
                batch(b, "mid")
            assert steps[0] == X_LINKS, steps[0]
            base[0], steps[0] = before + (B - 2) * X_LINKS, 0
            batch(B - 1, "last")
            evacuate(B * (S_ITEMS // 2))
            n = start_of(B - 1) + len(order(plans["last"]))
            for i, item in enumerate([("norm", G - 1), ("oT", 0), ("oT", 1), ("wo", 0), ("wo", 1)]):
                work(item, WORK + (n + i) % W_BANKS, B - 1, B + 1, n + i + 1, 0)



E = 8
TOPK = 2
SH = 2
HID = E + SH
NG = NT // TT
UNCHOSEN = -1e30
LEAD = 2
SHARED = SH * NG


def feed_forward(nc, x_all, io, out):
    with ExitStack() as ctx:
        def sb(name, shape, dt=F32):
            return ctx.enter_context(nc.sbuf_tensor(name, shape, dt))

        def sem(name):
            return ctx.enter_context(nc.semaphore(name))

        def parts(name, shape):
            return [sb(name + part, shape, F32R) for part in ("_rounded", "_rest")]

        ps = ctx.enter_context(nc.psum_tensor("f_ps", [P, 8, 512], F32))
        GATE, UP, DOWN, MISC = 0, 2, 4, 6
        ident = sb("f_ident", [P, P])
        identb = sb("f_identb", [P, P], BF16)
        ones = sb("f_ones", [P, P])
        pickb = sb("f_pickb", [E, E * P], BF16)
        gate_w = sb("f_gate_w", [P, KT, E])
        lb = sb("f_lb", [P, E])
        raw_s = sb("f_raw_s", [P, 3, KT, SH * P])
        raw = sb("f_raw", [P, KT, E * P])
        raw_d = raw[:].rearrange("p k n -> p (k n)").rearrange("p (j d) -> p j d", j=E)
        wg = parts("f_wg", [P, KT, HID * P])
        wu = parts("f_wu", [P, KT, HID * P])
        wd = parts("f_wd", [P, HID, D])
        bst = sb("f_bst", [P, NT, 6])
        mv = sb("f_mv", [P, NT, 2])
        std = sb("f_std", [P, NT])
        rstd = sb("f_rstd", [P, NT])
        xn = sb("f_xn", [P, TT, D])
        xs = sb("f_xs", [P, KT, T])
        xnT = parts("f_xnT", [P, KT, NT * P])
        logits = sb("f_logits", [P, NT, E])
        score = sb("f_score", [P, NT, E])
        better = sb("f_better", [P, NT, E])
        cmp = logits
        chosen = sb("f_chosen", [P, NT, E])
        total = sb("f_total", [P, NT])
        sums = sb("f_sums", [P, 2 * E])
        wmean = sb("f_wmean", [P, 2 * E])
        off = sb("f_off", [P, NT, E], BF16)
        offT = sb("f_offT", [E, T], BF16)
        act_g = sb("f_act_g", [P, 2, T])
        hid_whole = sb("f_hid_whole", [P, 2, T])
        hid = parts("f_hid", [P, 2, T])

        consts, stored, link_f = sem("f_consts"), sem("f_stored"), sem("f_link")
        var_ready, std_ready, xn_ready = sem("f_var"), sem("f_std_ready"), sem("f_xn_ready")
        turned, xs_drained, xnT_rounded, xnT_split = sem("turned"), sem("xs_drained"), sem("xnT_rounded"), sem("xnT_split")
        logits_filled, logits_drained = sem("logits_filled"), sem("logits_drained")
        logits_ready, score_ready, sums_ready, off_ready = (sem("logits_ready"), sem("score_ready"),
                                                            sem("sums_ready"), sem("off_ready"))
        sums_filled, off_filled, off_turned = sem("sums_filled"), sem("off_filled"), sem("off_turned")
        ws_loaded, w_loaded, w_rounded, w_split = sem("ws_loaded"), sem("w_loaded"), sem("w_rounded"), sem("w_split")
        wd_scaled = sem("wd_scaled")
        gate_filled, up_filled, silu_done, hid_done = (sem("gate_filled"), sem("up_filled"), sem("silu_done"),
                                                       sem("hid_done"))
        hid_rounded, hid_split, hid_used = sem("hid_rounded"), sem("hid_split"), sem("hid_used")
        down_filled, down_drained = sem("down_filled"), sem("down_drained")
        NCONST = 6
        ROOTS = (slice(0, TT), slice(TT, NT))
        S_SPLITS = 3

        def shared_parts(part):
            return (wg[part][:, :, E * P:], wu[part][:, :, E * P:], wd[part][:, E:, :])

        def routed(w):
            return w[:, :, 0:E * P]

        block = ctx.enter_context(nc.Block())

        @block.sync
        def _(sp):
            sp.dma_start(ident[:], io["ident"]).then_inc(consts, 16)
            sp.dma_start(gate_w[:], io["gate_w"].rearrange("(k p) n -> p k n", p=P)).then_inc(consts, 16)
            for t, name in ((lb, "lb"), (ones, "ones"), (identb, "identb"), (pickb, "pickb")):
                sp.dma_start(t[:], io[name]).then_inc(consts, 16)
            for n, name in enumerate(("wg", "wu")):
                sp.dma_start(raw_s[:, n], io[name][:, E * P:].rearrange("(k p) n -> p k n", p=P)).then_inc(ws_loaded, 16)
            sp.dma_start(raw_s[:, 2], io["wd"][E * P:].rearrange("(k p) n -> p k n", p=P)).then_inc(ws_loaded, 16)
            sp.dma_start(raw[:], io["wg"][:, 0:E * P].rearrange("(k p) n -> p k n", p=P)).then_inc(w_loaded, 16)
            sp.wait_ge(w_split, S_SPLITS + 1)
            sp.dma_start(raw[:], io["wu"][:, 0:E * P].rearrange("(k p) n -> p k n", p=P)).then_inc(w_loaded, 16)
            sp.wait_ge(w_split, S_SPLITS + 2)
            sp.dma_start(raw_d, io["wd"][0:E * P].rearrange("(k p) n -> p k n", p=P)).then_inc(w_loaded, 16)
            with sp.Fori(0, NG) as n:
                sp.wait_ge(down_drained, (NG + n) * 2 + 2)
                sp.dma_start(out[n].rearrange("(t p) d -> p t d", p=P), x_all[:, bass.ts(n, TT), :]).then_inc(stored, 16)
            sp.wait_ge(stored, 16 * NG)

        @block.tensor
        def _(pe):
            def product(out_, lhs, rhs, last=True):
                for n, (l, r) in enumerate(SPLIT_PASSES):
                    for kk in range(KT):
                        m = pe.matmul(out_, lhs(l, kk), rhs(r, kk), start=n == 0 and kk == 0,
                                      stop=last and n == len(SPLIT_PASSES) - 1 and kk == KT - 1)
                return m

            def turn(n, first=False):
                pe.wait_ge(xn_ready, n + 1)
                if not first:
                    pe.wait_ge(logits_drained, n)
                for f in range(KT):
                    for t in range(TT):
                        m = pe.transpose(ps[:, MISC + f, t * P:(t + 1) * P], xn[:, t, f * P:(f + 1) * P], ident[:])
                    m.then_inc(turned, 1)

            def to_logits(n):
                pe.wait_ge(xs_drained, n * KT + KT)
                for t in range(TT):
                    for kk in range(KT):
                        m = pe.matmul(ps[:, MISC, t * E:(t + 1) * E], xs[:, kk, t * P:(t + 1) * P],
                                      gate_w[:, kk, :], start=kk == 0, stop=kk == KT - 1)
                m.then_inc(logits_filled, 1)

            def gate_up(n, j, number, buf, first=False):
                cols = bass.ts(n, T)
                if not first:
                    pe.wait_ge(silu_done, number - 1)
                m = product(ps[:, GATE + buf, :], lambda part, kk: wg[part][:, kk, j * P:(j + 1) * P],
                            lambda part, kk: xnT[part][:, kk, cols], j >= E)
                if j < E:
                    if j == 0:
                        pe.wait_ge(off_turned, n + 1)
                    m = pe.matmul(ps[:, GATE + buf, :], pickb[:, j * P:(j + 1) * P], offT[:], start=False, stop=True)
                m.then_inc(gate_filled, 1)
                if not first:
                    pe.wait_ge(hid_done, number - 1)
                product(ps[:, UP + buf, :], lambda part, kk: wu[part][:, kk, j * P:(j + 1) * P],
                        lambda part, kk: xnT[part][:, kk, cols]).then_inc(up_filled, 1)

            def down(j, number, buf, start, stop, group, first=False):
                pe.wait_ge(hid_split, number + 1)
                for t in range(TT):
                    if start and not first and t % 2 == 0:
                        pe.wait_ge(down_drained, group * 2 - 2 + (t // 2 + 1))
                    for n, (l, r) in enumerate(SPLIT_PASSES):
                        m = pe.matmul(ps[:, DOWN + t // 2, (t % 2) * D:(t % 2 + 1) * D],
                                      hid[l][:, buf, t * P:(t + 1) * P], wd[r][:, j, :],
                                      start=start and n == 0 and t % 2 == 0,
                                      stop=stop and n == len(SPLIT_PASSES) - 1 and t % 2 == 1, skip_group_check=True)
                    if stop and t == 1:
                        m.then_inc(down_filled, 1)
                m.then_inc(hid_used, 1)

            pe.wait_ge(consts, 16 * NCONST)
            turn(0, True)
            to_logits(0)
            pe.wait_ge(w_split, S_SPLITS)
            pe.wait_ge(xnT_split, KT)
            gate_up(0, E, 0, 0, True)
            gate_up(0, E + 1, 1, 1, True)
            turn(1)
            to_logits(1)
            down(E, 0, 0, True, False, 0, True)
            with pe.Fori(2, NG) as n:
                turn(n)
                pe.wait_ge(xnT_split, n * KT)
                gate_up(n - 1, E, n * SH - 2, 0)
                down(E + 1, n * SH - 3, 1, False, True, n - 2)
                to_logits(n)
                gate_up(n - 1, E + 1, n * SH - 1, 1)
                down(E, n * SH - 2, 0, True, False, n - 1)
            pe.wait_ge(xnT_split, NG * KT)
            gate_up(NG - 1, E, SHARED - 2, 0)
            down(E + 1, SHARED - 3, 1, False, True, NG - 2)
            gate_up(NG - 1, E + 1, SHARED - 1, 1)
            down(E, SHARED - 2, 0, True, False, NG - 1)
            down(E + 1, SHARED - 1, 1, False, True, NG - 1)
            pe.wait_ge(w_split, S_SPLITS + 2)
            pe.wait_ge(off_ready, 1)
            pe.wait_ge(logits_drained, NG)

            def experts(n, first=False):
                for t in range(TT):
                    m = pe.matmul(ps[0:E, MISC, t * P:(t + 1) * P],
                                  off[:, bass.ds(n * TT + t, 1), :].rearrange("p o e -> p (o e)"), identb[:],
                                  start=True, stop=True)
                m.then_inc(off_filled, 1)
                at = SHARED + n * E
                for e in range(E):
                    gate_up(n, e, at + e, e % 2)
                    if first and e == 0:
                        pe.wait_ge(sums_ready, 1)
                        pe.matmul(ps[:, MISC + 1, 0:2 * E], ones[:], sums[:], start=True, stop=True).then_inc(sums_filled, 1)
                    if e >= LEAD:
                        if first and e == LEAD:
                            pe.wait_ge(w_split, S_SPLITS + 3)
                        down(e - LEAD, at + e - LEAD, e % 2, e == LEAD, False, NG + n)
                    elif not first:
                        down(E + e - LEAD, at + e - LEAD, e % 2, False, e == LEAD - 1, NG + n - 1)

            experts(0, True)
            with pe.Fori(1, NG) as n:
                experts(n)
            for e in range(E - LEAD, E):
                down(e, SHARED + (NG - 1) * E + e, e % 2, False, e == E - 1, 2 * NG - 1)

        @block.scalar
        def _(act):
            def silu(number, buf, first=False):
                act.wait_ge(gate_filled, number + 1)
                if not first:
                    act.wait_ge(hid_done, number - 1)
                nc.scalar.activation(act_g[:, buf, :], ps[:, GATE + buf, :], ACT.Silu).then_inc(silu_done, 1)

            def round_hid(number, buf, first=False):
                act.wait_ge(hid_done, number + 1)
                if not first:
                    act.wait_ge(hid_used, number - 1)
                nc.scalar.activation(hid[0][:, buf, :], hid_whole[:, buf, :], ACT.Copy).then_inc(hid_rounded, 1)

            def round_xnT(n):
                for f in range(KT):
                    act.wait_ge(xs_drained, n * KT + (f + 1))
                    nc.scalar.activation(xnT[0][:, f, bass.ts(n, T)], xs[:, f, :], ACT.Copy).then_inc(xnT_rounded, 1)

            for n, tiles in enumerate(ROOTS):
                act.wait_ge(var_ready, n + 1)
                nc.scalar.activation(std[:, tiles], mv[:, tiles, 1], ACT.Sqrt).then_inc(std_ready, 1)
                if n == 0:
                    act.wait_ge(ws_loaded, 16 * S_SPLITS)
                    for m, w in enumerate(shared_parts(0)):
                        nc.scalar.activation(w, raw_s[:, m], ACT.Copy).then_inc(w_rounded, 1)
                    round_xnT(0)
            for n, w in enumerate((wg, wu)):
                act.wait_ge(w_loaded, 16 * (n + 1))
                nc.scalar.activation(routed(w[0]), raw[:], ACT.Copy).then_inc(w_rounded, 1)
                if n == 0:
                    silu(0, 0, True)
                    round_hid(0, 0, True)
                    round_xnT(1)
                    silu(1, 1, True)
                    round_hid(1, 1, True)
            with act.Fori(2, NG) as n:
                round_xnT(n)
                for s in range(SH):
                    silu(n * SH - SH + s, s)
                    round_hid(n * SH - SH + s, s)
            act.wait_ge(logits_ready, 1)
            nc.scalar.activation(score[:], logits[:], ACT.Sigmoid).then_inc(score_ready, 1)
            for s in range(SH):
                silu(SHARED - SH + s, s)
                round_hid(SHARED - SH + s, s)
            for e in range(LEAD):
                silu(SHARED + e, e % 2)
            act.wait_ge(wd_scaled, 1)
            nc.scalar.activation(wd[0][:, 0:E, :], raw_d, ACT.Copy).then_inc(w_rounded, 1)
            round_hid(SHARED, 0)
            for e in range(LEAD, E):
                silu(SHARED + e, e % 2)
                round_hid(SHARED + e - 1, (e - 1) % 2)
            with act.Fori(1, NG) as n:
                for e in range(E):
                    silu(SHARED + n * E + e, e % 2)
                    round_hid(SHARED + n * E + e - 1, (e - 1) % 2)
            round_hid(SHARED + NG * E - 1, 1)

        @block.gpsimd
        def _(pool):
            def rest_xnT(n):
                for f in range(KT):
                    pool.wait_ge(xnT_rounded, n * KT + (f + 1))
                    cols = bass.ts(n, T)
                    nc.gpsimd.tensor_tensor(xnT[1][:, f, cols], xs[:, f, :], xnT[0][:, f, cols],
                                            ALU.subtract).then_inc(xnT_split, 1)

            def rest_hid(number, buf):
                pool.wait_ge(hid_rounded, number + 1)
                nc.gpsimd.tensor_tensor(hid[1][:, buf, :], hid_whole[:, buf, :], hid[0][:, buf, :],
                                        ALU.subtract).then_inc(hid_split, 1)

            for n, (rounded, rest) in enumerate(zip(shared_parts(0), shared_parts(1))):
                pool.wait_ge(w_rounded, n + 1)
                nc.gpsimd.tensor_tensor(rest, raw_s[:, n], rounded, ALU.subtract).then_inc(w_split, 1)
            rest_xnT(0)
            for n, w in enumerate((wg, wu)):
                pool.wait_ge(w_rounded, S_SPLITS + n + 1)
                nc.gpsimd.tensor_tensor(routed(w[1]), raw[:], routed(w[0]), ALU.subtract).then_inc(w_split, 1)
                if n == 0:
                    rest_hid(0, 0)
                    rest_xnT(1)
                    rest_hid(1, 1)
            with pool.Fori(2, NG) as n:
                rest_xnT(n)
                for s in range(SH):
                    rest_hid(n * SH - SH + s, s)
            for s in range(SH):
                rest_hid(SHARED - SH + s, s)
            pool.wait_ge(w_rounded, S_SPLITS + 3)
            nc.gpsimd.tensor_tensor(wd[1][:, 0:E, :], raw_d, wd[0][:, 0:E, :], ALU.subtract).then_inc(w_split, 1)
            with pool.Fori(0, NG) as n:
                for e in range(E):
                    rest_hid(SHARED + n * E + e, e % 2)

        @block.vector
        def _(dve):
            steps = [0]

            def link(ins):
                steps[0] += 1
                ins.then_inc(link_f, 1)
                dve.wait_ge(link_f, steps[0])

            def normalise(n):
                for t in range(TT):
                    row = bass.ds(n * TT + t, 1)
                    ins = nc.vector.tensor_scalar(
                        xn[:, t, :], x_all[:, row, :].rearrange("p o d -> p (o d)"),
                        mv[:, row, 0:1].rearrange("p o d -> p (o d)"), rstd[:, row], ALU.subtract, ALU.mult)
                ins.then_inc(xn_ready, 1)

            def keep_xs(n, first=False):
                for f in range(KT):
                    dve.wait_ge(turned, n * KT + (f + 1))
                    if not first:
                        dve.wait_ge(xnT_split, n * KT + (f + 1 - KT))
                    nc.vector.tensor_copy(xs[:, f, :], ps[:, MISC + f, :]).then_inc(xs_drained, 1)

            def keep_logits(n):
                dve.wait_ge(logits_filled, n + 1)
                nc.vector.tensor_tensor(logits[:, bass.ts(n, TT), :],
                                        ps[:, MISC, 0:TT * E].rearrange("p (t e) -> p t e", t=TT),
                                        lb[:].unsqueeze(1).broadcast_to([P, TT, E]), ALU.add).then_inc(logits_drained, 1)

            def multiply(number, buf, first=False):
                dve.wait_ge(up_filled, number + 1)
                dve.wait_ge(silu_done, number + 1)
                if not first:
                    dve.wait_ge(hid_split, number - 1)
                nc.vector.tensor_tensor(hid_whole[:, buf, :], ps[:, UP + buf, :], act_g[:, buf, :],
                                        ALU.mult).then_inc(hid_done, 1)

            def add_down(n, group, last_number):
                for half in range(2):
                    if half == 0:
                        dve.wait_ge(down_filled, group + 1)
                    else:
                        dve.wait_ge(hid_used, last_number + 1)
                    xb = x_all[:, bass.ds(n * TT + 2 * half, 2), :]
                    nc.vector.tensor_tensor(xb, xb, ps[:, DOWN + half, :].rearrange("p (t d) -> p t d", t=2),
                                            ALU.add).then_inc(down_drained, 1)

            def moments(n, tiles):
                for t in range(tiles.start, tiles.stop):
                    ins = nc.vector.bn_stats(bst[:, t, :], x_all[:, t, :])
                link(ins)
                for t in range(tiles.start, tiles.stop):
                    ins = nc.vector.bn_aggr(mv[:, t, :], bst[:, t, :])
                link(ins)
                nc.vector.tensor_scalar(mv[:, tiles, 1], mv[:, tiles, 1], EPS, None, ALU.add).then_inc(var_ready, 1)
                dve.wait_ge(std_ready, n)
                link(nc.vector.reciprocal(rstd[:, tiles], std[:, tiles]))

            moments(1, ROOTS[0])
            normalise(0)
            dve.wait_ge(consts, 16 * NCONST)
            keep_xs(0, True)
            moments(2, ROOTS[1])
            normalise(1)
            keep_logits(0)
            multiply(0, 0, True)
            keep_xs(1)
            normalise(2)
            multiply(1, 1, True)
            keep_logits(1)
            with dve.Fori(2, NG - 1) as n:
                keep_xs(n)
                normalise(n + 1)
                multiply(n * SH - 2, 0)
                add_down(n - 2, n - 2, n * SH - 3)
                keep_logits(n)
                multiply(n * SH - 1, 1)
            keep_xs(NG - 1)
            multiply(SHARED - SH - 2, 0)
            add_down(NG - 3, NG - 3, SHARED - SH - 3)
            keep_logits(NG - 1)
            multiply(SHARED - SH - 1, 1)
            dve.wait_ge(logits_drained, NG)
            nc.vector.memset(better[:], 0.0).then_inc(logits_ready, 1)
            multiply(SHARED - 2, 0)
            add_down(NG - 2, NG - 2, SHARED - 3)
            multiply(SHARED - 1, 1)
            dve.wait_ge(score_ready, 1)
            for j in range(E):
                sj = score[:, :, j:j + 1]
                link(nc.vector.tensor_tensor(cmp[:], sj.broadcast_to([P, NT, E]), score[:], ALU.is_gt))
                link(nc.vector.tensor_tensor(better[:], better[:], cmp[:], ALU.add))
                if j < E - 1:
                    rest = slice(j + 1, E)
                    link(nc.vector.tensor_tensor(cmp[:, :, rest], sj.broadcast_to([P, NT, E - 1 - j]),
                                                 score[:, :, rest], ALU.is_equal))
                    link(nc.vector.tensor_tensor(better[:, :, rest], better[:, :, rest], cmp[:, :, rest], ALU.add))
            link(nc.vector.tensor_scalar(chosen[:], better[:], TOPK - 0.5, None, ALU.is_lt))
            nc.vector.tensor_scalar(off[:], chosen[:], -UNCHOSEN, UNCHOSEN, ALU.mult, ALU.add).then_inc(off_ready, 1)
            link(nc.vector.tensor_tensor(cmp[:], score[:], chosen[:], ALU.mult))
            link(nc.vector.tensor_reduce(out=total[:], in_=cmp[:], axis=AX.X, op=ALU.add))
            link(nc.vector.tensor_scalar(total[:], total[:], 1e-8, None, ALU.add))
            link(nc.vector.reciprocal(total[:], total[:]))
            link(nc.vector.tensor_tensor(cmp[:], cmp[:], total[:].unsqueeze(2).broadcast_to([P, NT, E]), ALU.mult))
            nc.vector.tensor_reduce(out=sums[:, 0:E], in_=cmp[:].rearrange("p n e -> p e n"), axis=AX.X, op=ALU.add)
            nc.vector.tensor_reduce(out=sums[:, E:2 * E], in_=chosen[:].rearrange("p n e -> p e n"), axis=AX.X,
                                    op=ALU.add).then_inc(sums_ready, 1)

            def keep_off(n):
                dve.wait_ge(off_filled, n + 1)
                nc.vector.tensor_copy(offT[:], ps[0:E, MISC, :]).then_inc(off_turned, 1)

            keep_off(0)
            add_down(NG - 1, NG - 1, SHARED - 1)
            dve.wait_ge(sums_filled, 1)
            link(nc.vector.tensor_scalar(wmean[:, E:2 * E], ps[:, MISC + 1, E:2 * E], 1.0, None, ALU.max))
            link(nc.vector.reciprocal(wmean[:, E:2 * E], wmean[:, E:2 * E]))
            link(nc.vector.tensor_tensor(wmean[:, 0:E], ps[:, MISC + 1, 0:E], wmean[:, E:2 * E], ALU.mult))
            dve.wait_ge(w_loaded, 16 * 3)
            for j in range(E):
                ins = nc.vector.tensor_scalar(raw_d[:, j, :], raw_d[:, j, :], wmean[:, j:j + 1], None, ALU.mult)
            ins.then_inc(wd_scaled, 1)
            for e in range(E):
                multiply(SHARED + e, e % 2)
            with dve.Fori(1, NG) as n:
                keep_off(n)
                for e in range(E):
                    multiply(SHARED + n * E + e, e % 2)
                    if e == LEAD - 1:
                        add_down(n - 1, NG + n - 1, SHARED + n * E - 1)
            add_down(NG - 1, 2 * NG - 1, SHARED + NG * E - 1)


def build(nc, io, out, stage=3):
    with ExitStack() as ctx:
        x_all = ctx.enter_context(nc.sbuf_tensor("x_all", [P, NT, D], F32))
        ln2 = ctx.enter_context(nc.sbuf_tensor("ln2", [P, NT, 2], F32))
        retention(nc, x_all, ln2, io)
        if stage > 1:
            cross_attention(nc, x_all, ln2, io)
        if stage > 2:
            feed_forward(nc, x_all, io, out)
        else:
            with nc.semaphore("dbg") as dbg, nc.Block() as block:
                @block.sync
                def _(sp):
                    sp.dma_start(out.rearrange("b (n p) d -> p (b n) d", p=P), x_all[:]).then_inc(dbg, 16)
                    sp.wait_ge(dbg, 16)


def shape_constants(bf16):
    f = np.float32
    gamma = (f(1.0) - f(2.0) ** (f(-5.0) - np.arange(H, dtype=f))).astype(f)
    i = np.arange(P)
    head = i // HD
    diff = i[None, :] - i[:, None]
    decay = np.where(diff[:, None, :] >= 0, gamma[None, :, None] ** np.maximum(diff, 0)[:, None, :].astype(f), 0)
    hs = head[:, None] + HT * np.arange(KT)[None, :]
    qdecay = gamma[hs][:, :, None] ** i[None, None, :].astype(f)
    kscale = np.repeat(gamma[None, :] ** (P - i)[:, None].astype(f), HD, axis=1)
    return {
        "ident": np.eye(P, dtype=f),
        "decay": decay.astype(f),
        "qdecay": qdecay.astype(f),
        "kscale": kscale.astype(f),
        "headmask": (head[:, None] == np.arange(HT)[None, :]).astype(f),
        "blockmask": (head[:, None] == head[None, :]).astype(f),
        "chunkdecay": (gamma[hs] ** f(P)).astype(f),
        "ones": np.ones((P, P), f),
        "identb": np.eye(P, dtype=bf16),
        "pickb": (np.arange(E)[:, None] == np.arange(E * P)[None, :] // P).astype(bf16),
        "meanw": np.full((P, P), 1.0 / P, f),
    }


STAGE = 3


def kernel(**inputs):
    import ml_dtypes
    import concourse.bacc as bacc
    from concourse.bass_utils import run_bass_kernel_spmd as run

    a = {k: np.asarray(v) for k, v in inputs.items()}

    def rows(v):
        return np.broadcast_to(v[None, :], (P, v.shape[0]))

    arrays = dict(shape_constants(ml_dtypes.bfloat16))
    arrays.update({
        "x": a["x"],
        "wqkv": a["L0_attn_W_qkv"],
        "past": a["L0_attn_past_kv"].reshape(KT, P, HD).transpose(1, 0, 2),
        "gw": np.repeat(a["L0_attn_gn_weight"], HD).reshape(KT, P).T,
        "gb": np.repeat(a["L0_attn_gn_bias"], HD).reshape(KT, P).T,
        "ctxT": a["ctx_1024"].transpose(0, 2, 1),
        "wq": a["L0_xattn_Wq"].T,
        "wk": a["L0_xattn_Wk"].T,
        "wv": a["L0_xattn_Wv"].T,
        "wo": a["L0_xattn_Wo"].T,
        "bq": a["L0_xattn_bq"].reshape(KT, P).T,
        "bk": a["L0_xattn_bk"].reshape(KT, P).T,
        "bv": rows(a["L0_xattn_bv"]),
        "bo": rows(a["L0_xattn_bo"]),
        "gate_w": a["L0_ffn_gate_w"].T,
        "lb": rows(a["L0_ffn_lb_bias"]),
        "wg": np.concatenate([a["L0_ffn_expert_gate_w"].reshape(E * P, D), a["L0_ffn_shared_gate_w"]], 0).T,
        "wu": np.concatenate([a["L0_ffn_expert_up_w"].reshape(E * P, D), a["L0_ffn_shared_up_w"]], 0).T,
        "wd": np.concatenate([a["L0_ffn_expert_down_w"].transpose(0, 2, 1).reshape(E * P, D),
                              a["L0_ffn_shared_down_w"].T], 0),
    })
    arrays["ones_rows"] = np.ones((MR, GH, S), ml_dtypes.bfloat16)
    nc = bacc.Bacc("TRN2", target_bir_lowering=False, num_devices=1)
    io = {}
    for name in arrays:
        arrays[name] = np.ascontiguousarray(arrays[name])
        io[name] = nc.dram_tensor("in_" + name, arrays[name].shape,
                                  mybir.dt.from_np(arrays[name].dtype), kind="ExternalInput").ap()
    out = nc.dram_tensor("out_0", (B, T, D), F32, kind="ExternalOutput").ap()
    build(nc, io, out, STAGE)
    r = run(nc, [{"in_" + n: v for n, v in arrays.items()}], core_ids=[0])
    return r.results[0]["out_0"]
```
